# Optimizing a Trainium2 kernel written in Bass

```python
import numpy as np
import jax
import jax.numpy as jnp

def _softmax(x, axis=-1):
    return jax.nn.softmax(x, axis=axis)

def _gelu(x):
    return jax.nn.gelu(x, approximate=True)

def _silu(x):
    return jax.nn.silu(x)

def _sigmoid(x):
    return jax.nn.sigmoid(x)

def _layernorm(x, axis=-1, eps=1e-05):
    m = jnp.mean(x, axis=axis, keepdims=True)
    v = jnp.var(x, axis=axis, keepdims=True)
    return (x - m) / jnp.sqrt(v + eps)

def _scatter_add(tgt, idx, src, axis=0):
    return tgt.at[idx].add(src)

def _segment_sum(src, seg, n):
    return jax.ops.segment_sum(src, seg, n)
kernel_name = 'mk_decoder_preln_d1_seqx_r4_457c2c'

def setup_inputs(seed: int=0):
    np.random.seed(seed)
    _w = jnp.asarray

    def _rec_inputs():
        import jax
        import jax.numpy as jnp
        _rk = jax.random.key(seed)
        x = -0.000125 + 0.9999 * jax.random.normal(jax.random.fold_in(_rk, 1), (4, 512, 512), jnp.float32)
        _lenS = 512 - jax.random.randint(jax.random.fold_in(_rk, 7), (4,), 0, max(1, 512 // 4) + 1, jnp.int32)
        _lenS2 = 512 - jax.random.randint(jax.random.fold_in(_rk, 8), (4,), 0, max(1, 512 // 4) + 1, jnp.int32)
        itok_BxS_13_99985 = jax.random.randint(jax.random.fold_in(_rk, 11), (4, 512), 13, 99986, jnp.int32)
        _ctx_2048P = jax.random.normal(jax.random.fold_in(_rk, 12), (4, 16, 512), jnp.float32)
        _ctx_2048c = jax.random.dirichlet(jax.random.fold_in(_rk, 512), 0.3 * jnp.ones((16,), jnp.float32), (4, 512))
        _ctx_2048t = jnp.einsum('bsk,bkd->bsd', _ctx_2048c, _ctx_2048P)
        _ctx_2048t = _ctx_2048t * jax.lax.rsqrt(jnp.mean(jnp.square(_ctx_2048t)) + 1e-12) * 0.953939
        ctx_2048 = 6.82029e-06 + 0.0200006 * (_ctx_2048t + 0.3 * jax.random.normal(jax.random.fold_in(_rk, 612), (4, 512, 512), jnp.float32))
        return (x, itok_BxS_13_99985, ctx_2048)
    x, itok_BxS_13_99985, ctx_2048 = _rec_inputs()

    def _L0_attn_setup():
        import jax, jax.numpy as jnp
        import numpy as np
        B, N, DIM = (2, 512, 512)
        H, DH = (16, 128)
        SOFTCAP = 50.0
        SCALE = DH ** (-0.5)
        key = jax.random.key(seed)
        k1, k2, k3, k4 = jax.random.split(key, 4)
        s = 1.0 / np.sqrt(DIM)
        x = jax.random.normal(k1, (B, N, DIM), dtype=jnp.float32)
        w_qkv = jax.random.normal(k2, (DIM, 3 * H * DH), dtype=jnp.float32) * s
        w_gates = jax.random.normal(k3, (DIM, H), dtype=jnp.float32) * s
        w_out = jax.random.normal(k4, (H * DH, DIM), dtype=jnp.float32) * s
        return {'x': x, 'w_qkv': w_qkv, 'w_gates': w_gates, 'w_out': w_out}
    _L0_attn_all = _L0_attn_setup()
    _L0_attn_in = {k: v for k, v in _L0_attn_all.items() if k in ('w_qkv', 'w_gates', 'w_out')}
    del _L0_attn_all

    def _L0_xattn_setup():
        import jax, jax.numpy as jnp
        import numpy as np
        B, S, D = (4, 1024, 512)
        E = 4
        F = 2048 // E
        VOCAB = 25000
        key = jax.random.key(seed)
        k1, k2, k3, k4, k5 = jax.random.split(key, 5)
        hidden_states = jax.random.normal(k1, (B, S, D), dtype=jnp.float32)
        token_ids = jax.random.randint(k2, (B, S), 0, VOCAB, dtype=jnp.int64)
        Wg = jax.random.normal(k3, (E, F, D), dtype=jnp.float32) * 0.02
        Wu = jax.random.normal(k4, (E, F, D), dtype=jnp.float32) * 0.02
        Wd = jax.random.normal(k5, (E, D, F), dtype=jnp.float32) * 0.02
        return {'hidden_states': hidden_states, 'token_ids': token_ids, 'Wg': Wg, 'Wu': Wu, 'Wd': Wd}
    _L0_xattn_all = _L0_xattn_setup()
    _L0_xattn_in = {k: v for k, v in _L0_xattn_all.items() if k in ()}
    del _L0_xattn_all

    def _L0_ffn_setup():
        import jax, jax.numpy as jnp
        import numpy as np
        H = 512
        I = 352
        E = 8
        TOP_K = 2
        N_SHARED = 2
        I_SH = I * N_SHARED
        NORM_TOPK = True

        def _moe_forward(hidden_states, gate_w, expert_gate, expert_up, expert_down, shared_gate, shared_up, shared_down):
            bsz, seq_len, hdim = hidden_states.shape
            x = hidden_states.reshape(-1, hdim)
            logits = x @ gate_w.T
            probs = jax.nn.softmax(logits, axis=-1)
            routing_weights, selected = jax.lax.top_k(probs, TOP_K)
            if NORM_TOPK:
                routing_weights = routing_weights / (routing_weights.sum(axis=-1, keepdims=True) + 1e-20)
            combine = jnp.sum(jax.nn.one_hot(selected, E, dtype=routing_weights.dtype) * routing_weights[..., None], axis=1)
            g_sh = x @ shared_gate.T
            u_sh = x @ shared_up.T
            out = jax.nn.silu(g_sh) * u_sh @ shared_down.T
            g = jnp.einsum('nh,eih->nei', x, expert_gate)
            u = jnp.einsum('nh,eih->nei', x, expert_up)
            y = jnp.einsum('nei,ehi->neh', jax.nn.silu(g) * u, expert_down)
            out = out + jnp.einsum('neh,ne->nh', y, combine)
            return out.reshape(bsz, seq_len, hdim)
        key = jax.random.key(seed)
        ks = jax.random.split(key, 8)
        s = 0.02
        return {'hidden_states': jax.random.normal(ks[0], (1, 256, H), dtype=jnp.float32), 'gate_w': jax.random.normal(ks[1], (E, H), dtype=jnp.float32) * s, 'expert_gate': jax.random.normal(ks[2], (E, I, H), dtype=jnp.float32) * s, 'expert_up': jax.random.normal(ks[3], (E, I, H), dtype=jnp.float32) * s, 'expert_down': jax.random.normal(ks[4], (E, H, I), dtype=jnp.float32) * s, 'shared_gate': jax.random.normal(ks[5], (I_SH, H), dtype=jnp.float32) * s, 'shared_up': jax.random.normal(ks[6], (I_SH, H), dtype=jnp.float32) * s, 'shared_down': jax.random.normal(ks[7], (H, I_SH), dtype=jnp.float32) * s}
    _L0_ffn_all = _L0_ffn_setup()
    _L0_ffn_in = {k: v for k, v in _L0_ffn_all.items() if k in ('gate_w', 'expert_gate', 'expert_up', 'expert_down', 'shared_gate', 'shared_up', 'shared_down')}
    del _L0_ffn_all
    return {'x': x, 'itok_BxS_13_99985': itok_BxS_13_99985, 'ctx_2048': ctx_2048, 'L0_attn_w_qkv': _L0_attn_in['w_qkv'], 'L0_attn_w_gates': _L0_attn_in['w_gates'], 'L0_attn_w_out': _L0_attn_in['w_out'], 'L0_ffn_gate_w': _L0_ffn_in['gate_w'], 'L0_ffn_expert_gate': _L0_ffn_in['expert_gate'], 'L0_ffn_expert_up': _L0_ffn_in['expert_up'], 'L0_ffn_expert_down': _L0_ffn_in['expert_down'], 'L0_ffn_shared_gate': _L0_ffn_in['shared_gate'], 'L0_ffn_shared_up': _L0_ffn_in['shared_up'], 'L0_ffn_shared_down': _L0_ffn_in['shared_down']}

def reference(x, itok_BxS_13_99985, ctx_2048, L0_attn_w_qkv, L0_attn_w_gates, L0_attn_w_out, L0_ffn_gate_w, L0_ffn_expert_gate, L0_ffn_expert_up, L0_ffn_expert_down, L0_ffn_shared_gate, L0_ffn_shared_up, L0_ffn_shared_down):
    import jax
    import jax.numpy as jnp

    def _L0_attn_ref(x, w_qkv, w_gates, w_out):
        import jax, jax.numpy as jnp
        import numpy as np
        B, N, DIM = (2, 512, 512)
        H, DH = (16, 128)
        SOFTCAP = 50.0
        SCALE = DH ** (-0.5)
        b, n, _ = x.shape
        qkv = (x @ w_qkv).reshape(b, n, 3, H, DH).transpose(2, 0, 3, 1, 4)
        q, k, v = (qkv[0], qkv[1], qkv[2])
        q = q * SCALE
        sim = jnp.einsum('bhid,bhjd->bhij', q, k)
        sim = jnp.tanh(sim / SOFTCAP) * SOFTCAP
        mask_value = -jnp.finfo(sim.dtype).max
        causal_mask = jnp.triu(jnp.ones((n, n), dtype=bool), 1)
        sim = jnp.where(causal_mask, mask_value, sim)
        attn = jax.nn.softmax(sim, axis=-1)
        out = jnp.einsum('bhij,bhjd->bhid', attn, v)
        gates = jax.nn.sigmoid(x @ w_gates)
        out = out * gates.transpose(0, 2, 1)[..., None]
        out = out.transpose(0, 2, 1, 3).reshape(b, n, H * DH) @ w_out
        return out

    def _L0_xattn_ref(hidden_states, token_ids, Wg, Wu, Wd):
        import jax, jax.numpy as jnp
        import numpy as np
        B, S, D = (4, 1024, 512)
        E = 4
        F = 2048 // E
        VOCAB = 25000
        tokens_per_expert = VOCAB // E
        tid = jnp.clip(token_ids, 0, VOCAB - 1)
        expert_ids = jnp.minimum(tid // tokens_per_expert, E - 1)
        out = jnp.zeros_like(hidden_states)
        for e in range(E):
            g = jax.nn.silu(jnp.einsum('bsd,fd->bsf', hidden_states, Wg[e]))
            u = jnp.einsum('bsd,fd->bsf', hidden_states, Wu[e])
            y = jnp.einsum('bsf,df->bsd', g * u, Wd[e])
            out = jnp.where((expert_ids == e)[..., None], y, out)
        return out

    def _L0_ffn_ref(hidden_states, gate_w, expert_gate, expert_up, expert_down, shared_gate, shared_up, shared_down):
        import jax, jax.numpy as jnp
        import numpy as np
        H = 512
        I = 352
        E = 8
        TOP_K = 2
        N_SHARED = 2
        I_SH = I * N_SHARED
        NORM_TOPK = True

        def _moe_forward(hidden_states, gate_w, expert_gate, expert_up, expert_down, shared_gate, shared_up, shared_down):
            bsz, seq_len, hdim = hidden_states.shape
            x = hidden_states.reshape(-1, hdim)
            logits = x @ gate_w.T
            probs = jax.nn.softmax(logits, axis=-1)
            routing_weights, selected = jax.lax.top_k(probs, TOP_K)
            if NORM_TOPK:
                routing_weights = routing_weights / (routing_weights.sum(axis=-1, keepdims=True) + 1e-20)
            combine = jnp.sum(jax.nn.one_hot(selected, E, dtype=routing_weights.dtype) * routing_weights[..., None], axis=1)
            g_sh = x @ shared_gate.T
            u_sh = x @ shared_up.T
            out = jax.nn.silu(g_sh) * u_sh @ shared_down.T
            g = jnp.einsum('nh,eih->nei', x, expert_gate)
            u = jnp.einsum('nh,eih->nei', x, expert_up)
            y = jnp.einsum('nei,ehi->neh', jax.nn.silu(g) * u, expert_down)
            out = out + jnp.einsum('neh,ne->nh', y, combine)
            return out.reshape(bsz, seq_len, hdim)
        return _moe_forward(hidden_states, gate_w, expert_gate, expert_up, expert_down, shared_gate, shared_up, shared_down)
    x = x + _L0_attn_ref(_layernorm(x, axis=-1), L0_attn_w_qkv, L0_attn_w_gates, L0_attn_w_out)
    x = x + _L0_xattn_ref(_layernorm(x, axis=-1), itok_BxS_13_99985, ctx_2048, ctx_2048, ctx_2048)
    x = x + _L0_ffn_ref(_layernorm(x, axis=-1), L0_ffn_gate_w, L0_ffn_expert_gate, L0_ffn_expert_up, L0_ffn_expert_down, L0_ffn_shared_gate, L0_ffn_shared_up, L0_ffn_shared_down)
    return x

_drawn_inputs = setup_inputs


def setup_inputs(seed=0):
    import zlib

    import numpy as np

    out = dict(_drawn_inputs(seed))
    spreads = {}
    factors = {}
    for name, (base, spread) in spreads.items():
        noise = np.random.default_rng([zlib.crc32(name.encode()), seed]).standard_normal(out[name].shape)
        drawn = base * np.exp(spread * noise) if base else spread * noise
        out[name] = jnp.asarray(drawn.astype(out[name].dtype))
    for name, factor in factors.items():
        out[name] = (out[name] * factor).astype(out[name].dtype)
    return out
```

```python
from contextlib import ExitStack

import concourse.bass as bass
from concourse import mybir

F32 = mybir.dt.float32
F32R = mybir.dt.float32r
ALU = mybir.AluOpType
ACT = mybir.ActivationFunctionType

P = 128
BATCH, SEQ, D = 4, 512, 512
T = BATCH * SEQ
KC = D // P
TILES = T // P
TB = SEQ // P
HEADS, DH = 16, 128
SOFTCAP = 50.0
SCALE = DH ** -0.5
EPS = 1e-5
PCOLS = sum(SEQ - P * j for j in range(TB))
POFF = {0: 0, 1: SEQ, 3: 2 * SEQ - P, 2: 2 * SEQ}

VOCAB, TOKEN_EXPERTS = 25000, 4
IDS_PER_EXPERT = VOCAB // TOKEN_EXPERTS
XTILES = T // P + TOKEN_EXPERTS - 1
EXPERTS, TOPK, INNER = 8, 2, 352
SHARED = 2 * INNER
ROWS = 2 * P
ETILES = (TOPK * T + EXPERTS * (ROWS - 1)) // ROWS
ETILES += ETILES % 2
IC = -(-INNER // P)
SC = -(-SHARED // P)


def build(nc, x, token_ids, wqkv, wgates, wo, ctxT, router, exp_up, exp_down, sh_up, sh_down, out):
    with ExitStack() as ctx:
        I32, U32 = mybir.dt.int32, mybir.dt.uint32
        SBUF0, ALIGN = 16512, 32

        class Region:

            def __init__(self, start):
                self.at = start

            def __call__(self, name, shape, dt=F32):
                size = 4
                for n in shape[1:]:
                    size *= n
                t = nc.alloc_sbuf_tensor_at(name, shape, dt, offset=self.at)
                self.at += -(-size // ALIGN) * ALIGN
                return t

        def sem(name):
            return ctx.enter_context(nc.semaphore(name))

        bank = [ctx.enter_context(nc.psum_tensor(f"bank{i}", [P, 512], F32)) for i in range(8)]

        sb = Region(SBUF0)
        resid = sb("resid", [P, TILES, D])
        ident = sb("ident", [P, P])
        earlier = sb("earlier", [P, P])
        ones = sb("ones", [P, P])
        neghalf = sb("neghalf", [P, TB])
        iota = sb("iota", [P, ETILES])
        stats = sb("stats", [P, TB, 6])
        meanvar = sb("meanvar", [P, TB, 2])
        vareps = sb("vareps", [P, TB])
        rstd = sb("rstd", [P, TB])
        ids = sb("ids", [P, TILES], I32)
        slot_x = sb("slot_x", [P, TILES], U32)
        slot_e = [sb(f"slot_e{c}", [P, TILES], U32) for c in range(TOPK)]
        weight_e = [sb(f"weight_e{c}", [P, TILES]) for c in range(TOPK)]
        expert_x = sb("expert_x", [P, XTILES], I32)
        expert_e = sb("expert_e", [P, ETILES], I32)
        router_w = sb("router_w", [P, KC, EXPERTS])

        first_region = sb.at
        sb = Region(first_region)
        xnT_hi = sb("xnT_hi", [P, KC, T], F32R)
        xnT_lo = sb("xnT_lo", [P, KC, T], F32R)
        second_region = sb.at
        ct_hi = xnT_hi[:, :, :].rearrange("p e (k f) -> p e k f", k=KC)
        ct_lo = xnT_lo[:, :, :].rearrange("p e (k f) -> p e k f", k=KC)
        sb = Region(first_region)
        x3 = sb("x3", [P, TILES, D])

        def expert_weights(region, n):
            return [[region(f"e{n}_{what}_{part}", shape, F32R) for part in ("hi", "lo")]
                    for what, shape in (("up", [P, KC, 2 * INNER]), ("down", [P, IC, D]))]

        even_weights = expert_weights(Region(first_region), 0)

        sb = Region(second_region)
        rows = sb("rows", [P, TB, D])
        xT_hi = sb("xT_hi", [P, KC, P], F32R)
        xT_lo = sb("xT_lo", [P, KC, P], F32R)
        act_sb = sb("act_sb", [P, SHARED])
        aT_hi = sb("aT_hi", [P, SC, P], F32R)
        aT_lo = sb("aT_lo", [P, SC, P], F32R)
        shared_region = sb.at
        sh_up_hi = sb("sh_up_hi", [P, KC, 2 * SHARED], F32R)
        sh_up_lo = sb("sh_up_lo", [P, KC, 2 * SHARED], F32R)
        sh_down_hi = sb("sh_down_hi", [P, SC, D], F32R)
        sh_down_lo = sb("sh_down_lo", [P, SC, D], F32R)
        raw = sb("raw", [P, KC * 2 * INNER + IC * D])
        assert sb.at <= nc.sbuf_usable_end
        odd_weights = expert_weights(Region(shared_region), 1)
        weights = [even_weights, odd_weights]
        raw_up = raw[:, 0:KC * 2 * INNER].rearrange("p (k n) -> p k n", k=KC)
        raw_down = raw[:, KC * 2 * INNER:].rearrange("p (k n) -> p k n", k=IC)
        sb = Region(SBUF0 + (sb.at - SBUF0) - 4 * raw.shape[1])
        zeros = sb("zeros", [P, D])
        x3T = sb("x3T", [P, 2, D])
        NE = EXPERTS * TILES
        logits, chosen, running, ahead, places, above = (sb(n, [P, NE]) for n in ("logits", "chosen", "running", "ahead", "places", "above"))
        choice = [sb(f"choice{c}", [P, NE]) for c in range(TOPK)]
        restart = sb("restart", [P, NE])
        best = sb("best", [P, TILES, 8])
        best_at = sb("best_at", [P, TILES, 8], U32)
        best_f = sb("best_f", [P, TILES, TOPK])
        ids_ge = sb("ids_ge", [P, TOKEN_EXPERTS + 1, TILES])
        tile_of = sb("tile_of", [P, ETILES, EXPERTS - 1])
        tile_f = sb("tile_f", [P, ETILES])
        slot_f = sb("slot_f", [P, TILES])
        row_max = sb("row_max", [P, TILES])
        row_sum = sb("row_sum", [P, TILES])
        full, upto, base = (sb(n, [P, EXPERTS]) for n in ("full", "upto", "base"))
        assert sb.at <= nc.sbuf_usable_end

        sb = Region(second_region + 4 * TB * D)
        xn = rows
        causal = sb("causal", [P, 2, P])
        wqkv_raw = sb("wqkv_raw", [P, 3, KC, DH])
        wqkv_hi = sb("wqkv_hi", [P, 3, KC, DH], F32R)
        wqkv_lo = sb("wqkv_lo", [P, 3, KC, DH], F32R)
        wo_raw = sb("wo_raw", [P, D])
        wo_hi = sb("wo_hi", [P, D], F32R)
        wo_lo = sb("wo_lo", [P, D], F32R)
        wg_raw = sb("wg_raw", [P, KC, P])
        wg_hi = sb("wg_hi", [P, KC, P], F32R)
        wg_lo = sb("wg_lo", [P, KC, P], F32R)
        gateT = sb("gateT", [P, SEQ])
        gate_den = sb("gate_den", [P, TILES, HEADS])
        q_hi, q_lo, k_hi, k_lo, v_hi, v_lo = (sb(n, [P, SEQ], F32R) for n in ("q_hi", "q_lo", "k_hi", "k_lo", "v_hi", "v_lo"))
        vT = sb("vT", [P, SEQ])
        probs = sb("probs", [P, PCOLS])
        p_hi = sb("p_hi", [P, PCOLS], F32R)
        p_lo = sb("p_lo", [P, PCOLS], F32R)
        psum_keys = sb("psum_keys", [P, SEQ])
        o_hi = sb("o_hi", [P, 2, SEQ], F32R)
        o_lo = sb("o_lo", [P, 2, SEQ], F32R)
        denom = sb("denom", [P, TB])
        factor = sb("factor", [P, 2, TB])
        assert sb.at <= SBUF0 + nc.sbuf_usable_end - SBUF0 - 4 * raw.shape[1]

        xs = nc.dram_tensor("xs", (XTILES * P, D), F32, kind="Internal").ap()
        xs_out = nc.dram_tensor("xs_out", (XTILES * P, D), F32, kind="Internal").ap()
        es = nc.dram_tensor("es", (ETILES * ROWS, D), F32, kind="Internal").ap()
        es_out = nc.dram_tensor("es_out", (ETILES * ROWS, D), F32, kind="Internal").ap()

        names = """x_loaded0 x_loaded1 x_loaded2 x_loaded3 const_ready ln_stats ln_aggr ln_eps ln_rstd xn_ready xnT_ready xnT_hi_done xnT_lo_done
        wg_loaded wg_hi_done wg_split gateT_ready gateT_copied gate_ready gate_exp gate_done
        wqkv_loaded wo_loaded w_hi wq_split wk_split wv_split wo_split
        q_ready k_ready vT_ready v_ready s_ready pv_ready sum_ready y_ready
        q_hi_done k_hi_done vT_done v_hi_done o_hi_done tanh_done exp_done
        q_lo_done k_lo_done v_lo_done p_hi_done p_lo_done o_lo_done den_done factor_done y_added masked ssum_step ssum_done stored
        ids_loaded router_loaded zeros_ready zero_filled0 zero_filled1 step prefix_ready prefix_read prefix_e_read chosen_ready route_x_done route_e_done
        ct_loaded0 ct_loaded1 ct_hi_done ct_lo_pool ct_lo_dve sh_loaded sh_hi sh_split
        scat0 scat1 scat2 scat3 gath0 gath1 gath2 gath3 x_added scat_e
        x3_T x3_copied logits_ready logits_read minus_max exp_router
        up_loaded down_loaded up_hi up_lo down_hi down_lo combined
        """ + " ".join(f"{ph}_{n}" for ph in "xse" for n in ("row", "xT_ready", "xT_hi", "xT_lo", "up", "silu", "act", "aT_ready", "aT_hi", "aT_lo", "y", "y_out", "y_stored"))
        S = {n: sem(n) for n in names.split()}
        x_loaded = [S[f"x_loaded{b}"] for b in range(BATCH)]

        scat, gath = ([S[f"{n}{i}"] for i in range(TB)] for n in ("scat", "gath"))
        U = HEADS * BATCH
        XT, AT, YB = 4, 5, 7
        ROUTE_STEP = 4
        NCH = {"x": KC, "s": SC, "e": IC}
        HALVES = {"x": 1, "s": 2, "e": 1}
        WIDTH = {"x": D, "s": INNER, "e": INNER}
        NSTEPS = {"x": XTILES, "s": TILES, "e": 2 * ETILES}

        def chunk(ph, c):
            total = HALVES[ph] * WIDTH[ph]
            return c * P, min(P, total - c * P)

        block = ctx.enter_context(nc.Block())
        xv = x.rearrange("(t p) d -> p t d", p=P)
        ov = out.rearrange("(t p) d -> p t d", p=P)

        def triple(out_ap, a_hi, a_lo, b_hi, b_lo, first, last):
            nc.tensor.matmul(out_ap, a_hi, b_hi, start=first, stop=False)
            nc.tensor.matmul(out_ap, a_hi, b_lo, start=False, stop=False)
            return nc.tensor.matmul(out_ap, a_lo, b_hi, start=False, stop=last)

        def aT_parts(ph):
            return {"x": [(0, KC)], "s": [(0, KC), (KC, SC - 1), (SC - 1, SC)], "e": [(0, IC - 1), (IC - 1, IC)]}[ph]

        def aT_bank(ph, c0, c1, w):
            return bank[AT + c0 // KC][0:w, c0 % KC * P:(c0 % KC + c1 - c0) * P].rearrange("p (c n) -> p c n", n=P)

        @block.sync
        def _(sp):
            sp.dma_start(ids[:, :], token_ids).then_inc(S["ids_loaded"], 16)
            for b in range(BATCH):
                sp.dma_start(resid[:, TB * b:TB * b + TB, :], xv[:, TB * b:TB * b + TB, :]).then_inc(x_loaded[b], 16)
                if b == 0:
                    sp.dma_start(wg_raw[:, :, :], wgates).then_inc(S["wg_loaded"], 16)
                    sp.dma_start(wqkv_raw[:, :, :, :], wqkv[0]).then_inc(S["wqkv_loaded"], 16)
                    sp.dma_start(wo_raw[:, :], wo[0]).then_inc(S["wo_loaded"], 16)
            sp.dma_start(router_w[:, :, :], router).then_inc(S["router_loaded"], 16)
            sp.wait_ge(S["zeros_ready"], 1)
            for n, (rows_of, tiles) in enumerate(((xs, XTILES), (es, 2 * ETILES))):
                sp.dma_start(rows_of.rearrange("(t p) d -> p t d", p=P), zeros[:, :].unsqueeze(1).to_broadcast([P, tiles, D])).then_inc(S[f"zero_filled{n}"], 16)
            with sp.Fori(1, HEADS) as h:
                sp.wait_ge(S["wv_split"], h)
                sp.dma_start(wqkv_raw[:, :, :, :], wqkv[bass.ds(h, 1)].rearrange("a p c k d -> p (a c) k d")).then_inc(S["wqkv_loaded"], 16)
                sp.wait_ge(S["wo_split"], h)
                sp.dma_start(wo_raw[:, :], wo[bass.ds(h, 1)].rearrange("a p d -> p (a d)")).then_inc(S["wo_loaded"], 16)
            sp.wait_ge(S["zero_filled0"], 16)
            sp.wait_ge(S["zero_filled1"], 16)
            sp.wait_ge(S["route_x_done"], 1)
            for e in range(TOKEN_EXPERTS):
                if e == 2:
                    sp.wait_ge(S["ct_lo_pool"], 1)
                if e == 3:
                    sp.wait_ge(S["ct_lo_dve"], 1)
                sp.dma_start(raw[:, (e % 2) * KC * D:(e % 2 + 1) * KC * D].rearrange("p (k n) -> p k n", k=KC), ctxT[e]).then_inc(S[f"ct_loaded{e % 2}"], 16)

            def load_row(ph, source, g):
                sp.dma_start(rows[:, 0, :], source[bass.ds(g * P, P)]).then_inc(S[f"{ph}_row"], 16)

            def store_y(ph, target, g):
                sp.wait_ge(S[f"{ph}_y_out"], g + 1)
                sp.dma_start(target[bass.ds(g * P, P)], rows[:, 1, :]).then_inc(S[f"{ph}_y_stored"], 16)

            for i in range(TB):
                sp.wait_ge(scat[i], 16 * BATCH)
            load_row("x", xs, 0)

            def x_step(g, first, last):
                if not last:
                    sp.wait_ge(S["x_xT_ready"], g + 1)
                    load_row("x", xs, g + 1)
                if not first:
                    store_y("x", xs_out, g - 1)

            def load_shared(c):
                src = sh_sources[c]
                sp.dma_start(raw[:, 0:src.shape[1] * src.shape[2]].rearrange("p (k n) -> p k n", k=src.shape[1]), src).then_inc(S["sh_loaded"], 16)

            sh_sources = [sh_up[:, 0:2, :], sh_up[:, 2:4, :], sh_down]
            x_step(0, True, False)
            x_step(1, False, False)
            sp.wait_ge(S["ct_lo_pool"], 1)
            sp.wait_ge(S["ct_lo_dve"], 3)
            load_shared(0)
            with sp.Fori(2, XTILES // 3) as g:
                x_step(g, False, False)
            sp.wait_ge(S["sh_split"], 1)
            load_shared(1)
            with sp.Fori(XTILES // 3, 2 * XTILES // 3) as g:
                x_step(g, False, False)
            sp.wait_ge(S["sh_split"], 2)
            load_shared(2)
            with sp.Fori(2 * XTILES // 3, XTILES - 1) as g:
                x_step(g, False, False)
            x_step(XTILES - 1, False, True)
            store_y("x", xs_out, XTILES - 1)

            def load_weights(part, n, wait=True):
                e = sp.value_load(expert_e[0:1, bass.ds(n, 1)], min_val=0, max_val=EXPERTS - 1)
                if wait:
                    sp.wait_ge(S[f"{part}_lo"], n)
                to, of = (raw_up, exp_up) if part == "up" else (raw_down, exp_down)
                sp.dma_start(to, of[bass.ds(e, 1)].rearrange("e p k n -> p (e k) n")).then_inc(S[f"{part}_loaded"], 16)

            sp.wait_ge(S["route_e_done"], 1)
            load_weights("up", 0, False)
            load_weights("down", 0, False)
            sp.wait_ge(S["scat_e"], 16 * TOPK * TILES)
            sp.wait_ge(S["s_xT_ready"], TILES)
            load_row("e", es, 0)
            load_weights("up", 1)
            load_weights("down", 1)

            def e_steps(it, first, last):
                for j in range(4):
                    s, n = 4 * it + j, 2 * it + j // 2 + 1
                    if not (last and j == 3):
                        sp.wait_ge(S["e_xT_ready"], s + 1)
                        load_row("e", es, s + 1)
                    if not (first and j == 0):
                        store_y("e", es_out, s - 1)
                    if not (last and j >= 0):
                        load_weights(("up", "down")[j % 2], n + 1)

            e_steps(0, True, False)
            with sp.Fori(1, ETILES // 2 - 1) as it:
                e_steps(it, False, False)
            e_steps(ETILES // 2 - 1, False, True)
            store_y("e", es_out, 2 * ETILES - 1)
            for t in range(TILES):
                sp.wait_ge(S["combined"], TOPK * (t + 1))
                sp.dma_start(ov[:, t, :], resid[:, t, :]).then_inc(S["stored"], 16)
            sp.wait_ge(S["stored"], 16 * TILES)

        @block.gpsimd
        def _(pool):
            nc.gpsimd.memset(zeros[:, :], 0.0).then_inc(S["zeros_ready"], 1)
            nc.gpsimd.memset(ones[:, :], 1.0)
            nc.gpsimd.memset(neghalf[:, :], -0.5)
            nc.gpsimd.memset(ident[:, :], 0.0).then_inc(S["const_ready"], 1)
            pool.wait_ge(S["const_ready"], 1)
            nc.gpsimd.affine_select(out=ident[:, :], in_=ident[:, :], compare_op=ALU.not_equal, fill=1.0, base=0,
                                    pattern=[[-1, P]], channel_multiplier=1).then_inc(S["const_ready"], 1)
            nc.gpsimd.memset(causal[:, :, :], 1.0).then_inc(S["const_ready"], 1)
            pool.wait_ge(S["const_ready"], 3)
            nc.gpsimd.affine_select(out=causal[:, :, :], in_=causal[:, :, :], compare_op=ALU.is_ge, fill=0.0, base=0,
                                    pattern=[[0, 2], [1, P]], channel_multiplier=-1).then_inc(S["const_ready"], 1)

            nc.gpsimd.memset(earlier[:, :], 1.0).then_inc(S["const_ready"], 1)
            pool.wait_ge(S["const_ready"], 5)
            nc.gpsimd.affine_select(out=earlier[:, :], in_=earlier[:, :], compare_op=ALU.is_gt, fill=0.0, base=0,
                                    pattern=[[1, P]], channel_multiplier=-1).then_inc(S["const_ready"], 1)
            nc.gpsimd.iota(iota[:, :], [[1, ETILES]], base=0, channel_multiplier=0, allow_small_or_imprecise_dtypes=True).then_inc(S["const_ready"], 1)

            def low(raw, hi, lo, done, n):
                pool.wait_ge(S["w_hi"], n)
                nc.gpsimd.tensor_tensor(lo, raw, hi.bitcast(F32), ALU.subtract).then_inc(done, 1)

            def low_qkv(h, c, done):
                low(wqkv_raw[:, c, :, :], wqkv_hi[:, c, :, :], wqkv_lo[:, c, :, :], done, 4 * h + c + 2)

            def low_wo(h):
                low(wo_raw[:, :], wo_hi[:, :], wo_lo[:, :], S["wo_split"], 4 * h + 5)

            low(wg_raw[:, :, :], wg_hi[:, :, :], wg_lo[:, :, :], S["wg_split"], 1)
            for b in range(BATCH):
                pool.wait_ge(S["ln_eps"], b + 1)
                nc.gpsimd.tensor_tensor(rstd[:, :], vareps[:, :], neghalf[:, :], ALU.pow).then_inc(S["ln_rstd"], 1)
                if b == 0:
                    low_qkv(0, 0, S["wq_split"])
                    low_qkv(0, 1, S["wk_split"])
                    low_qkv(0, 2, S["wv_split"])
                    low_wo(0)

            def softmax_part(u):
                pool.wait_ge(S["exp_done"], u + 1)
                for diagonal in (probs[:, 0:2 * SEQ].rearrange("p (a c) -> p a c", a=2)[:, :, 0:P],
                                 probs[:, POFF[3]:POFF[3] + 2 * P].rearrange("p (a c) -> p a c", a=2)):
                    nc.gpsimd.tensor_tensor(diagonal, diagonal, causal[:, :, :], ALU.mult).then_inc(S["masked"], 1)
                pool.wait_ge(S["masked"], 2 * u + 2)
                nc.gpsimd.tensor_tensor(psum_keys[:, P:], probs[:, P:SEQ], probs[:, POFF[1]:POFF[1] + SEQ - P], ALU.add).then_inc(S["ssum_step"], 1)
                pool.wait_ge(S["ssum_step"], 2 * u + 1)
                nc.gpsimd.tensor_tensor(psum_keys[:, 2 * P:], psum_keys[:, 2 * P:], probs[:, POFF[2]:POFF[2] + 2 * P], ALU.add).then_inc(S["ssum_step"], 1)
                pool.wait_ge(S["ssum_step"], 2 * u + 2)
                nc.gpsimd.tensor_tensor(psum_keys[:, 3 * P:], psum_keys[:, 3 * P:], probs[:, POFF[3]:POFF[3] + P], ALU.add).then_inc(S["ssum_done"], 1)

            def head(h, first, last):
                for b in range(BATCH):
                    u = BATCH * h + b
                    if not (first and b == 0):
                        if not (first and b == 1):
                            pool.wait_ge(S["sum_ready"], u - 1)
                        softmax_part(u - 1)
                    if b == 1 and not first:
                        low_wo(h)
                    if b == BATCH - 1 and not last:
                        for c, done in enumerate(("wq_split", "wk_split", "wv_split")):
                            low_qkv(h + 1, c, S[done])

            pool.wait_ge(S["const_ready"], 4)
            head(0, True, False)
            with pool.Fori(1, HEADS - 1) as h:
                head(h, False, False)
            head(HEADS - 1, False, True)

            def rsqrt(n):
                pool.wait_ge(S["ln_eps"], n + 1)
                nc.gpsimd.tensor_tensor(rstd[:, :], vareps[:, :], neghalf[:, :], ALU.pow).then_inc(S["ln_rstd"], 1)

            def scatter_x(b):
                for i in range(TB):
                    pool.wait_ge(S["xn_ready"], TILES + TB * b + i + 1)
                    nc.gpsimd.indirect_dma_start(xs, bass.IndirectOffsetOnAxis(slot_x[:, TB * b + i:TB * b + i + 1], 0), rows[:, i, :], None).then_inc(scat[i], 16)

            pool.wait_ge(S["zero_filled0"], 16)
            pool.wait_ge(S["route_x_done"], 1)
            rsqrt(BATCH)
            scatter_x(0)
            pool.wait_ge(S["sum_ready"], U - 1)
            softmax_part(U - 1)
            pool.wait_ge(S["ct_hi_done"], 1)
            nc.gpsimd.tensor_tensor(ct_lo[:, 0], raw[:, 0:KC * D].rearrange("p (k n) -> p k n", k=KC), ct_hi[:, 0].bitcast(F32), ALU.subtract).then_inc(S["ct_lo_pool"], 1)
            for b in range(1, BATCH):
                rsqrt(BATCH + b)
                scatter_x(b)

            pool.wait_ge(S["y_added"], U * TB)
            for c, (hi, lo) in enumerate(((sh_up_hi[:, 0:2], sh_up_lo[:, 0:2]), (sh_up_hi[:, 2:4], sh_up_lo[:, 2:4]), (sh_down_hi[:, :], sh_down_lo[:, :]))):
                piece = raw[:, 0:hi.shape[1] * hi.shape[2]].rearrange("p (k n) -> p k n", k=hi.shape[1])
                pool.wait_ge(S["sh_loaded"], 16 * c + 16)
                nc.gpsimd.tensor_copy(hi, piece).then_inc(S["sh_hi"], 1)
                pool.wait_ge(S["sh_hi"], c + 1)
                nc.gpsimd.tensor_tensor(lo, piece, hi.bitcast(F32), ALU.subtract).then_inc(S["sh_split"], 1)

            pool.wait_ge(S["x_y_stored"], 16 * XTILES)

            def gather_x(b):
                for i in range(TB):
                    if b:
                        pool.wait_ge(S["x_added"], TB * (b - 1) + i + 1)
                    nc.gpsimd.indirect_dma_start(rows[:, i, :], None, xs_out, bass.IndirectOffsetOnAxis(slot_x[:, TB * b + i:TB * b + i + 1], 0)).then_inc(gath[i], 16)

            gather_x(0)
            for b in range(BATCH):
                if b + 1 < BATCH:
                    gather_x(b + 1)
                rsqrt(2 * BATCH + b)

            pool.wait_ge(S["zero_filled1"], 16)
            pool.wait_ge(S["route_e_done"], 1)
            for t in range(TILES):
                for c in range(TOPK):
                    nc.gpsimd.indirect_dma_start(es, bass.IndirectOffsetOnAxis(slot_e[c][:, t:t + 1], 0), x3[:, t, :], None).then_inc(S["scat_e"], 16)

            def down_low(n, p):
                pool.wait_ge(S["down_hi"], n + 1)
                nc.gpsimd.tensor_tensor(weights[p][1][1][:, :, :], raw_down, weights[p][1][0][:, :, :].bitcast(F32), ALU.subtract).then_inc(S["down_lo"], 1)

            down_low(0, 0)
            with pool.Fori(0, ETILES // 2 - 1) as it:
                down_low(2 * it + 1, 1)
                down_low(2 * it + 2, 0)
            down_low(ETILES - 1, 1)

            pool.wait_ge(S["e_y_stored"], 16 * 2 * ETILES)
            for t in range(TILES):
                for c in range(TOPK):
                    n = TOPK * t + c
                    if n >= TB:
                        pool.wait_ge(S["combined"], n - TB + 1)
                    nc.gpsimd.indirect_dma_start(rows[:, n % TB, :], None, es_out, bass.IndirectOffsetOnAxis(slot_e[c][:, t:t + 1], 0)).then_inc(gath[n % TB], 16)

        @block.scalar
        def _(act):
            def high(hi, raw):
                nc.scalar.activation(hi, raw, ACT.Copy).then_inc(S["w_hi"], 1)

            act.wait_ge(S["wg_loaded"], 16)
            high(wg_hi[:, :, :], wg_raw[:, :, :])
            act.wait_ge(S["wqkv_loaded"], 16)
            for c in range(3):
                high(wqkv_hi[:, c, :, :], wqkv_raw[:, c, :, :])
            act.wait_ge(S["wo_loaded"], 16)
            high(wo_hi[:, :], wo_raw[:, :])
            for t in range(TILES):
                act.wait_ge(S["xnT_ready"], t + 1)
                nc.scalar.activation(xnT_hi[:, :, t * P:t * P + P], bank[t % 2][:, :].rearrange("p (k n) -> p k n", k=KC), ACT.Copy).then_inc(S["xnT_hi_done"], 1)
            for b in range(BATCH):
                act.wait_ge(S["gateT_ready"], b + 1)
                nc.scalar.activation(gateT[:, :], bank[2][:, :], ACT.Copy).then_inc(S["gateT_copied"], 1)
                act.wait_ge(S["gate_ready"], b + 1)
                nc.scalar.activation(gate_den[:, TB * b:TB * b + TB, :],
                                     bank[3][:, :].rearrange("p (t h) -> p t h", t=TB)[:, :, 0:HEADS], ACT.Exp, scale=-1.0).then_inc(S["gate_exp"], 1)

            def softmax_part(u, first):
                if not first:
                    act.wait_ge(S["p_lo_done"], u)
                    act.wait_ge(S["sum_ready"], u)
                act.wait_ge(S["s_ready"], u + 1)
                for i, (lo, n) in enumerate(((0, SEQ), (SEQ, SEQ), (2 * SEQ, 2 * P))):
                    nc.scalar.activation(probs[:, lo:lo + n], bank[2 + i][:, 0:n], ACT.Tanh, scale=SCALE / SOFTCAP).then_inc(S["tanh_done"], 1)
                act.wait_ge(S["tanh_done"], 3 * u + 3)
                nc.scalar.activation(probs[:, :], probs[:, :], ACT.Exp, scale=SOFTCAP).then_inc(S["exp_done"], 1)

            def o_part(u, b, early):
                act.wait_ge(S["pv_ready"], u + 1)
                if not early:
                    act.wait_ge(S["y_ready"], TB * (u - 1))
                nc.scalar.activation(o_hi[:, b % 2, :], bank[5][:, :], ACT.Copy).then_inc(S["o_hi_done"], 1)

            def high_qkv(h, c, u, ready):
                act.wait_ge(S["wqkv_loaded"], 16 * h + 32)
                act.wait_ge(S[ready], u + 1)
                high(wqkv_hi[:, c, :, :], wqkv_raw[:, c, :, :])

            def head(h, first, last):
                for b in range(BATCH):
                    u = BATCH * h + b
                    start = first and b == 0
                    refresh = b == BATCH - 1 and not last
                    if not start:
                        softmax_part(u - 1, first and b == 1)
                    act.wait_ge(S["q_ready"], u + 1)
                    if not start:
                        act.wait_ge(S["s_ready"], u)
                    nc.scalar.activation(q_hi[:, :], bank[0][:, :], ACT.Copy).then_inc(S["q_hi_done"], 1)
                    act.wait_ge(S["k_ready"], u + 1)
                    nc.scalar.activation(k_hi[:, :], bank[1][:, :], ACT.Copy).then_inc(S["k_hi_done"], 1)
                    if refresh:
                        high_qkv(h, 0, u, "q_ready")
                    act.wait_ge(S["vT_ready"], u + 1)
                    if not start:
                        act.wait_ge(S["v_ready"], u)
                    nc.scalar.activation(vT[:, :], bank[0][:, :], ACT.Copy).then_inc(S["vT_done"], 1)
                    if refresh:
                        high_qkv(h, 1, u, "k_ready")
                    if not start:
                        o_part(u - 1, b + 1, first and b < 3)
                    if refresh:
                        high_qkv(h, 2, u, "vT_ready")
                    act.wait_ge(S["v_ready"], u + 1)
                    if not start:
                        act.wait_ge(S["pv_ready"], u)
                    nc.scalar.activation(v_hi[:, :], bank[1][:, :], ACT.Copy).then_inc(S["v_hi_done"], 1)
                    if b == 1 and not first:
                        act.wait_ge(S["wo_loaded"], 16 * h + 16)
                        act.wait_ge(S["y_ready"], TB * BATCH * h)
                        high(wo_hi[:, :], wo_raw[:, :])

            head(0, True, False)
            with act.Fori(1, HEADS - 1) as h:
                head(h, False, False)
            head(HEADS - 1, False, True)
            softmax_part(U - 1, False)

            def ct_high(e):
                act.wait_ge(S[f"ct_loaded{e % 2}"], 16 * (e // 2) + 16)
                if e == 0:
                    act.wait_ge(S["vT_ready"], U)
                nc.scalar.activation(ct_hi[:, e], raw[:, (e % 2) * KC * D:(e % 2 + 1) * KC * D].rearrange("p (k n) -> p k n", k=KC), ACT.Copy).then_inc(S["ct_hi_done"], 1)

            ct_high(0)
            o_part(U - 1, 1, False)
            for e in range(1, TOKEN_EXPERTS):
                ct_high(e)

            def xT_high(ph, g):
                act.wait_ge(S[f"{ph}_xT_ready"], g + 1)
                nc.scalar.activation(xT_hi[:, :, :], bank[XT][:, :].rearrange("p (k n) -> p k n", k=KC), ACT.Copy).then_inc(S[f"{ph}_xT_hi"], 1)

            def y_copy(ph, g, second):
                act.wait_ge(S[f"{ph}_y"], g + 1)
                if second:
                    act.wait_ge(S[f"{ph}_y_stored"], 16 * g)
                nc.scalar.activation(rows[:, 1, :], bank[YB][:, :], ACT.Copy).then_inc(S[f"{ph}_y_out"], 1)

            def aT_high(ph, g):
                act.wait_ge(S[f"{ph}_aT_ready"], g + 1)
                for c0, c1 in aT_parts(ph):
                    w = chunk(ph, c0)[1]
                    nc.scalar.activation(aT_hi[0:w, c0:c1, :], aT_bank(ph, c0, c1, w), ACT.Copy).then_inc(S[f"{ph}_aT_hi"], 1)

            def step(ph, g, first, last, second=True):
                W, H = WIDTH[ph], HALVES[ph]
                act.wait_ge(S[f"{ph}_up"], g + 1)
                if not first:
                    act.wait_ge(S[f"{ph}_aT_ready"], g)
                for j in range(H):
                    nc.scalar.activation(act_sb[:, j * W:j * W + W], bank[2 * j][:, 0:W], ACT.Silu).then_inc(S[f"{ph}_silu"], 1)
                if not last:
                    xT_high(ph, g + 1)
                if not first and ph != "s":
                    y_copy(ph, g - 1, second)
                if ph == "s" and not first:
                    act.wait_ge(S["s_y"], g)
                aT_high(ph, g)

            xT_high("x", 0)
            step("x", 0, True, False)
            step("x", 1, False, False, False)
            with act.Fori(2, XTILES - 1) as g:
                step("x", g, False, False)
            step("x", XTILES - 1, False, True)
            y_copy("x", XTILES - 1, True)

            for t in range(TILES):
                act.wait_ge(S["x3_T"], t + 1)
                if t >= 2:
                    act.wait_ge(S["logits_ready"], t - 1)
                nc.scalar.activation(x3T[:, t % 2, :], bank[XT + t % 2][:, :], ACT.Copy).then_inc(S["x3_copied"], 1)

            xT_high("s", 0)
            step("s", 0, True, False)
            act.wait_ge(S["minus_max"], 1)
            nc.scalar.activation(logits[:, :], logits[:, :], ACT.Exp).then_inc(S["exp_router"], 1)
            step("s", 1, False, False)
            with act.Fori(2, TILES - 1) as g:
                step("s", g, False, False)
            step("s", TILES - 1, False, True)

            def up_high(n, p, wait):
                act.wait_ge(S["up_loaded"], 16 * n + 16)
                if wait:
                    act.wait_ge(S["e_up"], 2 * n - 2)
                nc.scalar.activation(weights[p][0][0][:, :, :], raw_up, ACT.Copy).then_inc(S["up_hi"], 1)

            act.wait_ge(S["scat_e"], 16 * TOPK * TILES)
            act.wait_ge(S["s_row"], TILES)
            up_high(0, 0, False)
            act.wait_ge(S["s_y"], TILES)
            xT_high("e", 0)

            def e_steps(it, first, last):
                for j in range(4):
                    s = 4 * it + j
                    step("e", s, first and j == 0, last and j == 3, not (first and j == 1))
                    if j % 2 == 0 and not (last and j == 2):
                        up_high(2 * it + j // 2 + 1, (j // 2 + 1) % 2, not (first and j == 0))

            e_steps(0, True, False)
            with act.Fori(1, ETILES // 2 - 1) as it:
                e_steps(it, False, False)
            e_steps(ETILES // 2 - 1, False, True)
            y_copy("e", 2 * ETILES - 1, True)

        @block.vector
        def _(dve):
            def layernorm(n, b, target, free):
                for i in range(TB):
                    nc.vector.bn_stats(stats[:, i, :], resid[:, TB * b + i, :]).then_inc(S["ln_stats"], 1)
                for i in range(TB):
                    dve.wait_ge(S["ln_stats"], TB * n + i + 1)
                    nc.vector.bn_aggr(meanvar[:, i, :], stats[:, i, :]).then_inc(S["ln_aggr"], 1)
                dve.wait_ge(S["ln_aggr"], TB * n + TB)
                nc.vector.tensor_scalar(vareps[:, :], meanvar[:, :, 1], EPS, None, ALU.add).then_inc(S["ln_eps"], 1)
                dve.wait_ge(S["ln_rstd"], n + 1)
                for i in range(TB):
                    free(i)
                    nc.vector.tensor_scalar(target(i), resid[:, TB * b + i, :], meanvar[:, i, 0:1], rstd[:, i:i + 1],
                                            ALU.subtract, ALU.mult).then_inc(S["xn_ready"], 1)

            steps = [0]

            def link(instruction):
                steps[0] += 1
                instruction.then_inc(S["step"], 1)
                dve.wait_ge(S["step"], steps[0])

            def route(experts, unit, tiles, mask, choices, prefix, prefix_done, tile_expert):
                n = experts * TILES
                by = lambda a: a[:, 0:n].rearrange("p (e t) -> p e t", e=experts)
                link(nc.vector.memset(restart[:, 0:n], 1.0))
                link(nc.vector.memset(by(restart)[:, :, 0], 0.0))
                link(nc.vector.tensor_tensor_scan(running[:, 0:n], restart[:, 0:n], prefix[:, n:2 * n], 0.0, ALU.mult, ALU.add))
                link(nc.vector.tensor_tensor(ahead[:, 0:n], running[:, 0:n], prefix[:, n:2 * n], ALU.subtract))
                nc.vector.tensor_tensor(ahead[:, 0:n], ahead[:, 0:n], prefix[:, 0:n], ALU.add).then_inc(prefix_done, 1)
                link(nc.vector.tensor_scalar(places[:, 0:TILES], iota[:, 0:TILES], float(unit), None, ALU.mult))
                link(nc.vector.tensor_tensor(by(above), by(running)[:, :, TILES - 1].unsqueeze(2).to_broadcast([P, experts, TILES]),
                                             places[:, 0:TILES].unsqueeze(1).to_broadcast([P, experts, TILES]), ALU.is_gt))
                link(nc.vector.tensor_reduce(full[:, 0:experts], by(above), mybir.AxisListType.X, ALU.add))
                link(nc.vector.tensor_tensor_scan(upto[:, 0:experts], ones[:, 0:experts], full[:, 0:experts], 0.0, ALU.mult, ALU.add))
                link(nc.vector.tensor_tensor(base[:, 0:experts], upto[:, 0:experts], full[:, 0:experts], ALU.subtract))
                link(nc.vector.tensor_scalar(base[:, 0:experts], base[:, 0:experts], float(unit), None, ALU.mult))
                dve.wait_ge(prefix_done, 1)
                link(nc.vector.tensor_tensor(by(places), by(ahead), base[:, 0:experts].unsqueeze(2).to_broadcast([P, experts, TILES]), ALU.add))
                for one, slot in choices:
                    link(nc.vector.tensor_tensor(above[:, 0:n], places[:, 0:n], one[:, 0:n], ALU.mult))
                    link(nc.vector.tensor_reduce(slot_f[:, :], above[:, 0:n].rearrange("p (e t) -> p t e", e=experts), mybir.AxisListType.X, ALU.add))
                    link(nc.vector.tensor_copy(slot[:, :], slot_f[:, :]))
                owners = tile_of[:, 0:tiles, 0:experts - 1]
                link(nc.vector.tensor_tensor(owners, iota[:, 0:tiles].unsqueeze(2).to_broadcast([P, tiles, experts - 1]),
                                             upto[:, 0:experts - 1].unsqueeze(1).to_broadcast([P, tiles, experts - 1]), ALU.is_ge))
                link(nc.vector.tensor_reduce(tile_f[:, 0:tiles], owners, mybir.AxisListType.X, ALU.add))
                return nc.vector.tensor_copy(tile_expert[:, :], tile_f[:, 0:tiles])

            def free_xn(b):
                return lambda i: dve.wait_ge(S["xnT_ready"], TB * (b - 1) + i + 1) if b else None

            for b in range(BATCH):
                dve.wait_ge(x_loaded[b], 16)
                layernorm(b, b, lambda i: xn[:, i, :], free_xn(b))
                for i in range(TB):
                    t = TB * b + i
                    cols = slice(t * P, t * P + P)
                    dve.wait_ge(S["xnT_hi_done"], t + 1)
                    nc.vector.tensor_tensor(xnT_lo[:, :, cols], bank[t % 2][:, :].rearrange("p (k n) -> p k n", k=KC),
                                            xnT_hi[:, :, cols].bitcast(F32), ALU.subtract).then_inc(S["xnT_lo_done"], 1)
            dve.wait_ge(S["gate_exp"], BATCH)
            nc.vector.tensor_scalar(gate_den[:, :, :], gate_den[:, :, :], 1.0, None, ALU.add).then_inc(S["gate_done"], 1)
            dve.wait_ge(S["gate_done"], 1)

            dve.wait_ge(S["ids_loaded"], 16)
            dve.wait_ge(S["const_ready"], 7)
            link(nc.vector.memset(ids_ge[:, 0, :], 1.0))
            link(nc.vector.memset(ids_ge[:, TOKEN_EXPERTS, :], 0.0))
            for e in range(1, TOKEN_EXPERTS):
                link(nc.vector.tensor_scalar(ids_ge[:, e, :], ids[:, :], float(e * IDS_PER_EXPERT), None, ALU.is_ge))
            nx = TOKEN_EXPERTS * TILES
            nc.vector.tensor_tensor(chosen[:, 0:nx].rearrange("p (e t) -> p e t", t=TILES), ids_ge[:, 0:TOKEN_EXPERTS, :], ids_ge[:, 1:, :], ALU.subtract).then_inc(S["chosen_ready"], 1)
            dve.wait_ge(S["prefix_ready"], 1)
            route(TOKEN_EXPERTS, P, XTILES, chosen, [(chosen, slot_x)], bank[4], S["prefix_read"], expert_x).then_inc(S["route_x_done"], 1)

            def lo_part(lo, ps, hi, hi_done, done, u):
                dve.wait_ge(S[hi_done], u + 1)
                nc.vector.tensor_tensor(lo, ps, hi.bitcast(F32), ALU.subtract).then_inc(S[done], 1)

            def y_add(u, b, i):
                dve.wait_ge(S["y_ready"], TB * u + i + 1)
                row = resid[:, TB * b + i, :]
                nc.vector.scalar_tensor_tensor(out=row, in0=bank[7][:, :], scalar=factor[:, b % 2, i:i + 1], in1=row,
                                               op0=ALU.mult, op1=ALU.add).then_inc(S["y_added"], 1)

            def p_part(u, first):
                if not first:
                    dve.wait_ge(S["pv_ready"], u)
                dve.wait_ge(S["masked"], 2 * u + 2)
                nc.vector.tensor_copy(p_hi[:, :], probs[:, :]).then_inc(S["p_hi_done"], 1)
                dve.wait_ge(S["p_hi_done"], u + 1)
                nc.vector.tensor_tensor(p_lo[:, :], probs[:, :], p_hi[:, :].bitcast(F32), ALU.subtract).then_inc(S["p_lo_done"], 1)

            def o_part(u, h, b):
                lo_part(o_lo[:, b % 2, :], bank[5][:, :], o_hi[:, b % 2, :], "o_hi_done", "o_lo_done", u)
                dve.wait_ge(S["sum_ready"], u + 1)
                nc.vector.tensor_tensor(denom[:, :], bank[6][:, 0:2 * TB].rearrange("p (t c) -> p t c", c=2)[:, :, 0],
                                        gate_den[:, TB * b:TB * b + TB, bass.ds(h, 1)].rearrange("p t a -> p (t a)"), ALU.mult).then_inc(S["den_done"], 1)
                dve.wait_ge(S["den_done"], u + 1)
                nc.vector.reciprocal(factor[:, b % 2, :], denom[:, :]).then_inc(S["factor_done"], 1)

            def head(h, first):
                for b in range(BATCH):
                    u = BATCH * h + b
                    start = first and b == 0
                    adds = not (first and b < 2)
                    b2 = (b + 2) % BATCH
                    if adds:
                        dve.wait_ge(S["factor_done"], u - 1)
                        y_add(u - 2, b2, 0)
                    lo_part(q_lo[:, :], bank[0][:, :], q_hi[:, :], "q_hi_done", "q_lo_done", u)
                    if not start:
                        p_part(u - 1, first and b == 1)
                    if adds:
                        y_add(u - 2, b2, 1)
                    lo_part(k_lo[:, :], bank[1][:, :], k_hi[:, :], "k_hi_done", "k_lo_done", u)
                    if adds:
                        y_add(u - 2, b2, 2)
                    if not start:
                        o_part(u - 1, h if b else h - 1, (b - 1) % BATCH)
                    if adds:
                        y_add(u - 2, b2, 3)
                    lo_part(v_lo[:, :], bank[1][:, :], v_hi[:, :], "v_hi_done", "v_lo_done", u)

            head(0, True)
            with dve.Fori(1, HEADS) as h:
                head(h, False)

            def layernorm_x(b):
                def free(i):
                    if b:
                        dve.wait_ge(scat[i], 16 * b)
                    else:
                        dve.wait_ge(S["xnT_ready"], TILES)
                dve.wait_ge(S["y_added"], TB * (U - BATCH + b + 1))
                layernorm(BATCH + b, b, lambda i: rows[:, i, :], free)

            layernorm_x(0)
            dve.wait_ge(S["factor_done"], U - 1)
            for i in range(TB):
                y_add(U - 2, BATCH - 2, i)
            p_part(U - 1, False)
            layernorm_x(1)
            o_part(U - 1, HEADS - 1, BATCH - 1)
            dve.wait_ge(S["factor_done"], U)
            for i in range(TB):
                y_add(U - 1, BATCH - 1, i)
            layernorm_x(2)
            layernorm_x(3)
            for e in range(1, TOKEN_EXPERTS):
                dve.wait_ge(S["ct_hi_done"], e + 1)
                nc.vector.tensor_tensor(ct_lo[:, e], raw[:, (e % 2) * KC * D:(e % 2 + 1) * KC * D].rearrange("p (k n) -> p k n", k=KC),
                                        ct_hi[:, e].bitcast(F32), ALU.subtract).then_inc(S["ct_lo_dve"], 1)

            def xT_low(ph, g):
                dve.wait_ge(S[f"{ph}_xT_hi"], g + 1)
                nc.vector.tensor_tensor(xT_lo[:, :, :], bank[XT][:, :].rearrange("p (k n) -> p k n", k=KC), xT_hi[:, :, :].bitcast(F32), ALU.subtract).then_inc(S[f"{ph}_xT_lo"], 1)

            def copy_row(t):
                nc.vector.tensor_copy(rows[:, 0, :], x3[:, bass.ds(t, 1), :].rearrange("p a d -> p (a d)")).then_inc(S["s_row"], 1)

            def shared_add(t):
                dve.wait_ge(S["s_y"], t + 1)
                row = resid[:, bass.ds(t, 1), :].rearrange("p a d -> p (a d)")
                nc.vector.tensor_tensor(row, bank[YB][:, :], row, ALU.add).then_inc(S["s_y_out"], 1)

            def step(ph, g, first, last, rows_left=True):
                W, H = WIDTH[ph], HALVES[ph]
                for j in range(H):
                    dve.wait_ge(S[f"{ph}_silu"], H * g + j + 1)
                    part = act_sb[:, j * W:j * W + W]
                    nc.vector.tensor_tensor(part, part, bank[2 * j + (ph != "x")][:, 0:W], ALU.mult).then_inc(S[f"{ph}_act"], 1)
                if not last:
                    xT_low(ph, g + 1)
                    if ph == "s" and rows_left:
                        copy_row(g + 2)
                if ph == "s" and not first:
                    shared_add(g - 1)
                parts = aT_parts(ph)
                for c0, c1 in parts:
                    w = chunk(ph, c0)[1]
                    read = sum(p[0] // KC <= c0 // KC for p in parts)
                    dve.wait_ge(S[f"{ph}_aT_hi"], len(parts) * g + read)
                    nc.vector.tensor_tensor(aT_lo[0:w, c0:c1, :], aT_bank(ph, c0, c1, w), aT_hi[0:w, c0:c1, :].bitcast(F32), ALU.subtract).then_inc(S[f"{ph}_aT_lo"], 1)

            xT_low("x", 0)
            step("x", 0, True, False)
            with dve.Fori(1, XTILES - 1) as g:
                step("x", g, False, False)
            step("x", XTILES - 1, False, True)

            for b in range(BATCH):
                for i in range(TB):
                    dve.wait_ge(gath[i], 16 * b + 16)
                    row = resid[:, TB * b + i, :]
                    nc.vector.tensor_tensor(row, row, rows[:, i, :], ALU.add).then_inc(S["x_added"], 1)
                dve.wait_ge(S["x_added"], TB * b + TB)
                layernorm(2 * BATCH + b, b, lambda i: x3[:, TB * b + i, :], lambda i: None)
            dve.wait_ge(S["xn_ready"], 3 * TILES)
            copy_row(0)
            dve.wait_ge(S["logits_ready"], TILES)
            nc.vector.tensor_copy(logits[:, :], bank[YB][:, 0:NE]).then_inc(S["logits_read"], 1)
            xT_low("s", 0)
            copy_row(1)

            dve.wait_ge(S["logits_read"], 1)
            by_expert = logits[:, :].rearrange("p (t e) -> p t e", e=EXPERTS)
            over = lambda a: a.unsqueeze(2).to_broadcast([P, TILES, EXPERTS])
            link(nc.vector.tensor_reduce(row_max[:, :], by_expert, mybir.AxisListType.X, ALU.max))
            nc.vector.tensor_tensor(by_expert, by_expert, over(row_max[:, :]), ALU.subtract).then_inc(S["minus_max"], 1)
            step("s", 0, True, False)
            dve.wait_ge(S["exp_router"], 1)
            link(nc.vector.tensor_reduce(row_sum[:, :], by_expert, mybir.AxisListType.X, ALU.add))
            link(nc.vector.reciprocal(row_sum[:, :], row_sum[:, :]))
            link(nc.vector.tensor_tensor(by_expert, by_expert, over(row_sum[:, :]), ALU.mult))
            for t in range(TILES):
                top = nc.vector.max(best[:, t, :], by_expert[:, t, :])
            link(top)
            for t in range(TILES):
                top = nc.vector.max_index(best_at[:, t, :], best[:, t, :], by_expert[:, t, :])
            link(top)
            link(nc.vector.tensor_copy(best_f[:, :, :], best_at[:, :, 0:TOPK]))
            link(nc.vector.tensor_tensor(row_sum[:, :], best[:, :, 0], best[:, :, 1], ALU.add))
            link(nc.vector.tensor_scalar(row_sum[:, :], row_sum[:, :], 1e-20, None, ALU.add))
            link(nc.vector.reciprocal(row_sum[:, :], row_sum[:, :]))
            for c in range(TOPK):
                link(nc.vector.tensor_tensor(weight_e[c][:, :], best[:, :, c], row_sum[:, :], ALU.mult))
                link(nc.vector.tensor_tensor(choice[c][:, :].rearrange("p (e t) -> p e t", e=EXPERTS),
                                             iota[:, 0:EXPERTS].unsqueeze(2).to_broadcast([P, EXPERTS, TILES]),
                                             best_f[:, :, c].unsqueeze(1).to_broadcast([P, EXPERTS, TILES]), ALU.is_equal))
            nc.vector.tensor_tensor(chosen[:, :], choice[0][:, :], choice[1][:, :], ALU.add).then_inc(S["chosen_ready"], 1)
            for g in range(1, ROUTE_STEP):
                step("s", g, False, False)
            dve.wait_ge(S["prefix_ready"], 2)
            dve.wait_ge(S["prefix_read"], 1)
            route(EXPERTS, ROWS, ETILES, chosen, list(zip(choice, slot_e)), bank[YB], S["prefix_e_read"], expert_e).then_inc(S["route_e_done"], 1)
            with dve.Fori(ROUTE_STEP, TILES - 2) as g:
                step("s", g, False, False)
            step("s", TILES - 2, False, False, False)
            step("s", TILES - 1, False, True)
            shared_add(TILES - 1)

            def up_low(n, p):
                dve.wait_ge(S["up_hi"], n + 1)
                nc.vector.tensor_tensor(weights[p][0][1][:, :, :], raw_up, weights[p][0][0][:, :, :].bitcast(F32), ALU.subtract).then_inc(S["up_lo"], 1)

            def down_high(n, p, wait):
                dve.wait_ge(S["down_loaded"], 16 * n + 16)
                if wait:
                    dve.wait_ge(S["e_y"], 2 * n - 2)
                nc.vector.tensor_copy(weights[p][1][0][:, :, :], raw_down).then_inc(S["down_hi"], 1)

            up_low(0, 0)
            down_high(0, 0, False)
            xT_low("e", 0)

            def e_steps(it, first, last):
                for j in range(4):
                    s, n, p = 4 * it + j, 2 * it + j // 2 + 1, (j // 2 + 1) % 2
                    step("e", s, first and j == 0, last and j == 3)
                    if not (last and j >= 2):
                        if j % 2 == 0:
                            up_low(n, p)
                        else:
                            down_high(n, p, not (first and j == 1))

            e_steps(0, True, False)
            with dve.Fori(1, ETILES // 2 - 1) as it:
                e_steps(it, False, False)
            e_steps(ETILES // 2 - 1, False, True)

            for t in range(TILES):
                row = resid[:, t, :]
                for c in range(TOPK):
                    n = TOPK * t + c
                    dve.wait_ge(gath[n % TB], 16 * BATCH + 16 * (n // TB) + 16)
                    if c:
                        dve.wait_ge(S["combined"], n)
                    nc.vector.scalar_tensor_tensor(out=row, in0=rows[:, n % TB, :], scalar=weight_e[c][:, t:t + 1], in1=row,
                                                   op0=ALU.mult, op1=ALU.add).then_inc(S["combined"], 1)

        @block.tensor
        def _(pe):
            pe.wait_ge(S["const_ready"], 6)
            for t in range(TILES):
                if t >= 2:
                    pe.wait_ge(S["xnT_lo_done"], t - 1)
                pe.wait_ge(S["xn_ready"], t + 1)
                for k in range(KC):
                    last = nc.tensor.transpose(bank[t % 2][:, k * P:k * P + P], xn[:, t % TB, k * P:k * P + P], ident[:, :])
                last.then_inc(S["xnT_ready"], 1)
            pe.wait_ge(S["wg_split"], 1)
            pe.wait_ge(S["xnT_lo_done"], TILES)
            for b in range(BATCH):
                cols = slice(b * SEQ, b * SEQ + SEQ)
                for k in range(KC):
                    last = triple(bank[2][:, :], wg_hi[:, k, :], wg_lo[:, k, :], xnT_hi[:, k, cols], xnT_lo[:, k, cols], k == 0, k == KC - 1)
                last.then_inc(S["gateT_ready"], 1)
                pe.wait_ge(S["gateT_copied"], b + 1)
                if b:
                    pe.wait_ge(S["gate_exp"], b)
                for i in range(TB):
                    last = nc.tensor.transpose(bank[3][:, i * P:i * P + P], gateT[:, i * P:i * P + P], ident[:, :])
                last.then_inc(S["gate_ready"], 1)

            def count_ahead(experts, to, n):
                pe.wait_ge(S["chosen_ready"], n)
                n = experts * TILES
                nc.tensor.matmul(to[:, 0:n], earlier[:, :], chosen[:, 0:n], start=True, stop=True)
                nc.tensor.matmul(to[:, n:2 * n], ones[:, :], chosen[:, 0:n], start=True, stop=True).then_inc(S["prefix_ready"], 1)

            count_ahead(TOKEN_EXPERTS, bank[4], 1)

            def project(c, b, to, ready):
                cols = slice(b * SEQ, b * SEQ + SEQ)
                for k in range(KC):
                    last = triple(to[:, :], wqkv_hi[:, c, k, :], wqkv_lo[:, c, k, :], xnT_hi[:, k, cols], xnT_lo[:, k, cols], k == 0, k == KC - 1)
                last.then_inc(S[ready], 1)

            def scores(u, first):
                pe.wait_ge(S["q_lo_done"], u + 1)
                pe.wait_ge(S["k_lo_done"], u + 1)
                if first:
                    pe.wait_ge(S["gate_exp"], BATCH)
                    pe.wait_ge(S["prefix_read"], 1)
                else:
                    pe.wait_ge(S["exp_done"], u)
                for j in (0, 1, 3, 2):
                    to = bank[2 + POFF[j] // SEQ][:, POFF[j] % SEQ:POFF[j] % SEQ + SEQ - P * j]
                    last = triple(to, k_hi[:, j * P:j * P + P], k_lo[:, j * P:j * P + P], q_hi[:, j * P:], q_lo[:, j * P:], True, True)
                last.then_inc(S["s_ready"], 1)

            def values(u, first):
                pe.wait_ge(S["p_lo_done"], u + 1)
                if not first:
                    pe.wait_ge(S["o_lo_done"], u)
                for j in range(TB):
                    n = SEQ - P * j
                    last = triple(bank[5][:, P * j:], v_hi[:, j * P:j * P + P], v_lo[:, j * P:j * P + P],
                                  p_hi[:, POFF[j]:POFF[j] + n], p_lo[:, POFF[j]:POFF[j] + n], j == 0, j == TB - 1)
                last.then_inc(S["pv_ready"], 1)
                pe.wait_ge(S["ssum_done"], u + 1)
                if not first:
                    pe.wait_ge(S["factor_done"], u)
                for i in range(TB):
                    src = probs if i == 0 else psum_keys
                    last = nc.tensor.matmul(bank[6][:, 2 * i:2 * i + 2], src[:, i * P:i * P + P], ones[:, 0:2], start=True, stop=True)
                last.then_inc(S["sum_ready"], 1)

            def output(u, b, i, h, very_first):
                pe.wait_ge(S["o_lo_done"], u + 1)
                if i == 0 and b == 0:
                    pe.wait_ge(S["wo_split"], h + 1)
                if not very_first:
                    pe.wait_ge(S["y_added"], TB * u + i)
                triple(bank[7][:, :], o_hi[:, b % 2, i * P:i * P + P], o_lo[:, b % 2, i * P:i * P + P], wo_hi[:, :], wo_lo[:, :], True, True).then_inc(S["y_ready"], 1)

            def head(h, first):
                for b in range(BATCH):
                    u = BATCH * h + b
                    start = first and b == 0
                    outputs = not (first and b < 2)
                    b2, h2 = (b + 2) % BATCH, h if b >= 2 else h - 1
                    if b == 0:
                        for n in ("wq_split", "wk_split", "wv_split"):
                            pe.wait_ge(S[n], h + 1)
                    if not start:
                        pe.wait_ge(S["vT_done"], u)
                    project(0, b, bank[0], "q_ready")
                    if outputs:
                        output(u - 2, b2, 0, h2, first and b == 2)
                    if not start:
                        pe.wait_ge(S["v_lo_done"], u)
                    project(1, b, bank[1], "k_ready")
                    if outputs:
                        output(u - 2, b2, 1, h2, False)
                    pe.wait_ge(S["q_lo_done"], u + 1)
                    project(2, b, bank[0], "vT_ready")
                    if outputs:
                        output(u - 2, b2, 2, h2, False)
                    if not start:
                        values(u - 1, first and b == 1)
                    if outputs:
                        output(u - 2, b2, 3, h2, False)
                    scores(u, start)
                    pe.wait_ge(S["vT_done"], u + 1)
                    for i in range(TB):
                        last = nc.tensor.transpose(bank[1][:, i * P:i * P + P], vT[:, i * P:i * P + P], ident[:, :])
                    last.then_inc(S["v_ready"], 1)

            head(0, True)
            with pe.Fori(1, HEADS) as h:
                head(h, False)
            for i in range(TB):
                output(U - 2, BATCH - 2, i, HEADS - 1, False)
            pe.wait_ge(S["v_lo_done"], U)
            values(U - 1, False)
            for i in range(TB):
                output(U - 1, BATCH - 1, i, HEADS - 1, False)

            def transpose_rows(ph, g):
                pe.wait_ge(S[f"{ph}_row"], (1 if ph == "s" else 16) * (g + 1))
                for k in range(KC):
                    last = nc.tensor.transpose(bank[XT][:, k * P:k * P + P], rows[:, 0, k * P:k * P + P], ident[:, :])
                last.then_inc(S[f"{ph}_xT_ready"], 1)

            def up(ph, g, products, first):
                pe.wait_ge(S[f"{ph}_xT_lo"], g + 1)
                if not first:
                    pe.wait_ge(S[f"{ph}_act"], HALVES[ph] * g)
                for j, (hi, lo) in enumerate(products):
                    for k in range(KC):
                        last = triple(bank[j][:, 0:WIDTH[ph]], xT_hi[:, k, :], xT_lo[:, k, :], hi(k), lo(k), k == 0, k == KC - 1)
                last.then_inc(S[f"{ph}_up"], 1)

            def down(ph, g, hi, lo, second):
                pe.wait_ge(S[f"{ph}_aT_lo"], len(aT_parts(ph)) * (g + 1))
                if second:
                    pe.wait_ge(S[f"{ph}_y_out"], g)
                for c in range(NCH[ph]):
                    w = chunk(ph, c)[1]
                    last = triple(bank[YB][:, :], aT_hi[0:w, c, :], aT_lo[0:w, c, :], hi(c, w), lo(c, w), c == 0, c == NCH[ph] - 1)
                last.then_inc(S[f"{ph}_y"], 1)

            def transpose_act(ph, g):
                pe.wait_ge(S[f"{ph}_act"], HALVES[ph] * (g + 1))
                for c in range(NCH[ph]):
                    c0, w = chunk(ph, c)
                    last = nc.tensor.transpose(bank[AT + c // KC][0:w, c % KC * P:c % KC * P + P], act_sb[:, c0:c0 + w], ident[:, :])
                last.then_inc(S[f"{ph}_aT_ready"], 1)

            def matrix(g):
                e = pe.value_load(expert_x[0:1, bass.ds(g, 1)], min_val=0, max_val=TOKEN_EXPERTS - 1)
                return [lambda k, w=P, m=m: m[0:w, bass.ds(e, 1), k, :].rearrange("p a n -> p (a n)") for m in (ct_hi, ct_lo)]

            def x_step(g, first, last, second=True):
                up("x", g, [matrix(g)], first)
                if not last:
                    transpose_rows("x", g + 1)
                if not first:
                    down("x", g - 1, *matrix(g - 1), second)
                transpose_act("x", g)

            transpose_rows("x", 0)
            pe.wait_ge(S["ct_lo_pool"], 1)
            pe.wait_ge(S["ct_lo_dve"], TOKEN_EXPERTS - 1)
            x_step(0, True, False)
            x_step(1, False, False, False)
            with pe.Fori(2, XTILES - 1) as g:
                x_step(g, False, False)
            x_step(XTILES - 1, False, True)
            down("x", XTILES - 1, *matrix(XTILES - 1), True)

            def transpose_x3(t):
                pe.wait_ge(S["xn_ready"], 2 * TILES + t + 1)
                if t >= 2:
                    pe.wait_ge(S["x3_copied"], t - 1)
                for k in range(KC):
                    last = nc.tensor.transpose(bank[XT + t % 2][:, k * P:k * P + P], x3[:, t, k * P:k * P + P], ident[:, :])
                last.then_inc(S["x3_T"], 1)

            pe.wait_ge(S["router_loaded"], 16)
            pe.wait_ge(S["x_y_out"], XTILES)
            transpose_x3(0)
            for t in range(TILES):
                if t + 1 < TILES:
                    transpose_x3(t + 1)
                pe.wait_ge(S["x3_copied"], t + 1)
                for k in range(KC):
                    last = nc.tensor.matmul(bank[YB][:, t * EXPERTS:(t + 1) * EXPERTS], x3T[:, t % 2, k * P:k * P + P], router_w[:, k, :], start=(k == 0), stop=(k == KC - 1))
                last.then_inc(S["logits_ready"], 1)

            pe.wait_ge(S["sh_split"], 3)
            shared = [[lambda k, m=m, j=j: m[:, k, j * INNER:(j + 1) * INNER] for m in (sh_up_hi, sh_up_lo)] for j in range(4)]
            shared_down = [lambda c, w, m=m: m[0:w, c, :] for m in (sh_down_hi, sh_down_lo)]

            def s_step(g, first, last, second=True):
                up("s", g, shared, first)
                if not last:
                    transpose_rows("s", g + 1)
                if not first:
                    down("s", g - 1, *shared_down, second)
                transpose_act("s", g)

            transpose_rows("s", 0)
            s_step(0, True, False)
            pe.wait_ge(S["logits_read"], 1)
            for g in range(1, ROUTE_STEP):
                s_step(g, False, False, g > 1)
            pe.wait_ge(S["s_y_out"], ROUTE_STEP - 1)
            count_ahead(EXPERTS, bank[YB], 2)
            pe.wait_ge(S["prefix_e_read"], 1)
            with pe.Fori(ROUTE_STEP, TILES - 1) as g:
                s_step(g, False, False)
            s_step(TILES - 1, False, True)
            down("s", TILES - 1, *shared_down, True)

            def e_steps(it, first, last):
                for j in range(4):
                    s, n, p = 4 * it + j, 2 * it + j // 2, j // 2
                    if j % 2 == 0:
                        pe.wait_ge(S["up_lo"], n + 1)
                    products = [[lambda k, m=m, c=c: m[:, k, c * INNER:(c + 1) * INNER] for m in weights[p][0]] for c in range(2)]
                    up("e", s, products, first and j == 0)
                    if not (last and j == 3):
                        transpose_rows("e", s + 1)
                    if not (first and j == 0):
                        e_down(s - 1, n if j % 2 else n - 1, (j + 3) % 4, not (first and j == 1))
                    transpose_act("e", s)

            def e_down(s, n, j, second):
                if j % 2 == 0:
                    pe.wait_ge(S["down_lo"], n + 1)
                down("e", s, *[lambda c, w, m=m: m[0:w, c, :] for m in weights[j // 2][1]], second)

            pe.wait_ge(S["s_y_out"], TILES)
            transpose_rows("e", 0)
            e_steps(0, True, False)
            with pe.Fori(1, ETILES // 2 - 1) as it:
                e_steps(it, False, False)
            e_steps(ETILES // 2 - 1, False, True)
            e_down(2 * ETILES - 1, ETILES - 1, 3, True)


def kernel(x, itok_BxS_13_99985, ctx_2048, L0_attn_w_qkv, L0_attn_w_gates, L0_attn_w_out, L0_ffn_gate_w, L0_ffn_expert_gate, L0_ffn_expert_up, L0_ffn_expert_down, L0_ffn_shared_gate, L0_ffn_shared_up, L0_ffn_shared_down):
    import numpy as np
    import concourse.bacc as bacc
    from concourse.bass_utils import run_bass_kernel_spmd

    c = np.ascontiguousarray
    f = lambda a: np.asarray(a)
    wg = np.zeros((D, P), np.float32)
    wg[:, :HEADS] = f(L0_attn_w_gates)
    chunks = lambda a: a.reshape(-1, P, a.shape[-1]).transpose(1, 0, 2)
    up = np.concatenate([f(L0_ffn_expert_gate), f(L0_ffn_expert_up)], 1).transpose(0, 2, 1)
    down = np.zeros((EXPERTS, IC * P, D), np.float32)
    down[:, :INNER] = f(L0_ffn_expert_down).transpose(0, 2, 1)
    halves = [m[j * INNER:(j + 1) * INNER] for j in range(2) for m in (f(L0_ffn_shared_gate), f(L0_ffn_shared_up))]
    sh_down = np.zeros((SC * P, D), np.float32)
    sh_down[:SHARED] = f(L0_ffn_shared_down).T
    arrays = {
        "x": c(f(x).reshape(T, D)),
        "token_ids": c(f(itok_BxS_13_99985).reshape(TILES, P).T),
        "wqkv": c(f(L0_attn_w_qkv).reshape(KC, P, 3, HEADS, DH).transpose(3, 1, 2, 0, 4)),
        "wgates": c(wg.reshape(KC, P, P).transpose(1, 0, 2)),
        "wo": c(f(L0_attn_w_out).reshape(HEADS, DH, D)),
        "ctxT": c(np.stack([chunks(m.T) for m in f(ctx_2048)])),
        "router": c(chunks(f(L0_ffn_gate_w).T)),
        "exp_up": c(np.stack([chunks(m) for m in up])),
        "exp_down": c(np.stack([chunks(m) for m in down])),
        "sh_up": c(chunks(np.concatenate(halves, 0).T)),
        "sh_down": c(chunks(sh_down)),
    }
    nc = bacc.Bacc("TRN2", target_bir_lowering=False, num_devices=1)
    args = [nc.dram_tensor(n, a.shape, mybir.dt.from_np(a.dtype), kind="ExternalInput").ap() for n, a in arrays.items()]
    args.append(nc.dram_tensor("out", (T, D), F32, kind="ExternalOutput").ap())
    build(nc, *args)
    r = run_bass_kernel_spmd(nc, [arrays], core_ids=[0])
    return r.results[0]["out"].reshape(BATCH, SEQ, D)
```

```python
from contextlib import ExitStack

import concourse.bass as bass
from concourse import mybir

F32 = mybir.dt.float32
F32R = mybir.dt.float32r
ALU = mybir.AluOpType
ACT = mybir.ActivationFunctionType

P = 128
BATCH, SEQ, D = 4, 512, 512
T = BATCH * SEQ
KC = D // P
TILES = T // P
TB = SEQ // P
HEADS, DH = 16, 128
SOFTCAP = 50.0
SCALE = DH ** -0.5
EPS = 1e-5
PCOLS = sum(SEQ - P * j for j in range(TB))
POFF = {0: 0, 1: SEQ, 3: 2 * SEQ - P, 2: 2 * SEQ}

VOCAB, TOKEN_EXPERTS = 25000, 4
IDS_PER_EXPERT = VOCAB // TOKEN_EXPERTS
XTILES = T // P + TOKEN_EXPERTS - 1
EXPERTS, TOPK, INNER = 8, 2, 352
SHARED = 2 * INNER
ETILES = TOPK * T // P + EXPERTS - 1
IC = -(-INNER // P)
SC = -(-SHARED // P)


def build(nc, x, token_ids, wqkv, wgates, wo, ctxT, router, exp_up, exp_down, sh_up, sh_down, out):
    with ExitStack() as ctx:
        I32, U32 = mybir.dt.int32, mybir.dt.uint32
        SBUF0, ALIGN = 16512, 32

        class Region:

            def __init__(self, start):
                self.at = start

            def __call__(self, name, shape, dt=F32):
                size = 4
                for n in shape[1:]:
                    size *= n
                t = nc.alloc_sbuf_tensor_at(name, shape, dt, offset=self.at)
                self.at += -(-size // ALIGN) * ALIGN
                return t

        def sem(name):
            return ctx.enter_context(nc.semaphore(name))

        bank = [ctx.enter_context(nc.psum_tensor(f"bank{i}", [P, 512], F32)) for i in range(8)]

        sb = Region(SBUF0)
        resid = sb("resid", [P, TILES, D])
        ident = sb("ident", [P, P])
        earlier = sb("earlier", [P, P])
        ones = sb("ones", [P, P])
        neghalf = sb("neghalf", [P, TB])
        iota = sb("iota", [P, ETILES])
        stats = sb("stats", [P, TB, 6])
        meanvar = sb("meanvar", [P, TB, 2])
        vareps = sb("vareps", [P, TB])
        rstd = sb("rstd", [P, TB])
        ids = sb("ids", [P, TILES], I32)
        slot_x = sb("slot_x", [P, TILES], U32)
        slot_e = [sb(f"slot_e{c}", [P, TILES], U32) for c in range(TOPK)]
        weight_e = [sb(f"weight_e{c}", [P, TILES]) for c in range(TOPK)]
        expert_x = sb("expert_x", [P, XTILES], I32)
        expert_e = sb("expert_e", [P, ETILES], I32)
        place_e = sb("place_e", [P, ETILES], I32)
        expert_end = sb("expert_end", [P, EXPERTS], I32)
        router_w = sb("router_w", [P, KC, EXPERTS])

        rows = sb("rows", [P, TB, D])

        first_region = sb.at
        xnT_hi = sb("xnT_hi", [P, KC, T], F32R)
        xnT_lo = sb("xnT_lo", [P, KC, T], F32R)
        ct_hi = xnT_hi[:, :, :].rearrange("p e (k f) -> p e k f", k=KC)
        ct_lo = xnT_lo[:, :, :].rearrange("p e (k f) -> p e k f", k=KC)
        UP, DOWN = KC * 2 * INNER, IC * D
        sb = Region(first_region)
        x3 = sb("x3", [P, TILES, D])
        weights_at = sb.at
        expert_w = sb("expert_w", [P, 2, 2 * (UP + DOWN)], F32R)
        over_shared = Region(sb.at)
        second_region = weights_at + 4 * 2 * (UP + DOWN)

        sb = Region(second_region)
        sh_up_hi = sb("sh_up_hi", [P, KC, 2 * SHARED], F32R)
        sh_up_lo = sb("sh_up_lo", [P, KC, 2 * SHARED], F32R)
        sh_down_hi = sb("sh_down_hi", [P, SC, D], F32R)
        sh_down_lo = sb("sh_down_lo", [P, SC, D], F32R)
        raw_odd = over_shared("raw_odd", [P, UP + DOWN])
        assert over_shared.at <= sb.at
        xT_hi = sb("xT_hi", [P, KC, P], F32R)
        xT_lo = sb("xT_lo", [P, KC, P], F32R)
        act_sb = sb("act_sb", [P, SHARED])
        aT_hi = sb("aT_hi", [P, SC, P], F32R)
        aT_lo = sb("aT_lo", [P, SC, P], F32R)
        raw_at = sb.at
        raw = sb("raw", [P, UP + DOWN])
        assert sb.at <= nc.sbuf_usable_end

        def up_of(weights):
            return weights.rearrange("p (k n) -> p k n", k=KC)

        def down_of(weights):
            return weights.rearrange("p (c n) -> p c n", c=IC)

        sb = Region(raw_at)
        zeros = sb("zeros", [P, D])
        x3T = sb("x3T", [P, 2, D])
        NE = EXPERTS * TILES
        logits, chosen, running, ahead, places, above = (sb(n, [P, NE]) for n in ("logits", "chosen", "running", "ahead", "places", "above"))
        choice = [sb(f"choice{c}", [P, NE]) for c in range(TOPK)]
        restart = sb("restart", [P, NE])
        best = sb("best", [P, TILES, 8])
        best_at = sb("best_at", [P, TILES, 8], U32)
        best_f = sb("best_f", [P, TILES, TOPK])
        ids_ge = sb("ids_ge", [P, TOKEN_EXPERTS + 1, TILES])
        tile_of = sb("tile_of", [P, ETILES, EXPERTS - 1])
        tile_f = sb("tile_f", [P, ETILES])
        odd_f = sb("odd_f", [P, ETILES])
        slot_f = sb("slot_f", [P, TILES])
        row_max = sb("row_max", [P, TILES])
        row_sum = sb("row_sum", [P, TILES])
        full, upto, base = (sb(n, [P, EXPERTS]) for n in ("full", "upto", "base"))
        assert sb.at <= nc.sbuf_usable_end

        sb = Region(second_region)
        xn = rows
        causal = sb("causal", [P, 2, P])
        wqkv_raw = sb("wqkv_raw", [P, 3, KC, DH])
        wqkv_hi = sb("wqkv_hi", [P, 3, KC, DH], F32R)
        wqkv_lo = sb("wqkv_lo", [P, 3, KC, DH], F32R)
        wo_raw = sb("wo_raw", [P, D])
        wo_hi = sb("wo_hi", [P, D], F32R)
        wo_lo = sb("wo_lo", [P, D], F32R)
        wg_raw = sb("wg_raw", [P, KC, P])
        wg_hi = sb("wg_hi", [P, KC, P], F32R)
        wg_lo = sb("wg_lo", [P, KC, P], F32R)
        gateT = sb("gateT", [P, SEQ])
        gate_den = sb("gate_den", [P, TILES, HEADS])
        q_hi, q_lo, k_hi, k_lo, v_hi, v_lo = (sb(n, [P, SEQ], F32R) for n in ("q_hi", "q_lo", "k_hi", "k_lo", "v_hi", "v_lo"))
        vT = sb("vT", [P, SEQ])
        probs = sb("probs", [P, PCOLS])
        p_hi = sb("p_hi", [P, PCOLS], F32R)
        p_lo = sb("p_lo", [P, PCOLS], F32R)
        psum_keys = sb("psum_keys", [P, SEQ])
        o_hi = sb("o_hi", [P, 2, SEQ], F32R)
        o_lo = sb("o_lo", [P, 2, SEQ], F32R)
        denom = sb("denom", [P, TB])
        factor = sb("factor", [P, 2, TB])
        assert sb.at <= raw_at

        xs = nc.dram_tensor("xs", (XTILES * P, D), F32, kind="Internal").ap()
        xs_out = nc.dram_tensor("xs_out", (XTILES * P, D), F32, kind="Internal").ap()
        es = nc.dram_tensor("es", (ETILES * P, D), F32, kind="Internal").ap()
        es_out = nc.dram_tensor("es_out", (ETILES * P, D), F32, kind="Internal").ap()

        names = """x_loaded0 x_loaded1 x_loaded2 x_loaded3 const_ready ln_stats ln_aggr ln_eps ln_rstd xn_ready xnT_ready xnT_hi_done xnT_lo_done
        wg_loaded wg_hi_done wg_split gateT_ready gateT_copied gate_ready gate_exp gate_done
        wqkv_loaded wo_loaded w_hi wq_split wk_split wv_split wo_split
        q_ready k_ready vT_ready v_ready s_ready pv_ready sum_ready y_ready
        q_hi_done k_hi_done vT_done v_hi_done o_hi_done tanh_done exp_done
        q_lo_done k_lo_done v_lo_done p_hi_done p_lo_done o_lo_done den_done factor_done y_added masked ssum_step ssum_done stored
        ids_loaded router_loaded zeros_ready zero_filled0 zero_filled1 step prefix_ready prefix_read prefix_e_read chosen_ready route_x_done route_e_done
        ct_loaded0 ct_loaded1 ct_hi_done ct_lo_pool ct_lo_dve sh_loaded sh_hi sh_split
        scat0 scat1 scat2 scat3 gath0 gath1 gath2 gath3 x_added scat_e
        x3_T x3_copied logits_ready logits_read minus_max exp_router
        up_loaded0 up_loaded1 down_loaded0 down_loaded1 up_hi up_lo down_hi down_lo combined
        """ + " ".join(f"{ph}_{n}" for ph in "xse" for n in ("row", "row0", "row1", "y_stored0", "y_stored1", "xT_ready", "xT_hi", "xT_lo", "up", "silu", "act", "aT_ready", "aT_hi", "aT_lo", "y", "y_out"))
        S = {n: sem(n) for n in names.split()}
        x_loaded = [S[f"x_loaded{b}"] for b in range(BATCH)]

        scat, gath = ([S[f"{n}{i}"] for i in range(TB)] for n in ("scat", "gath"))
        U = HEADS * BATCH
        XT, AT, YB = 4, 5, 7
        ROUTE_STEP = 4
        NCH = {"x": KC, "s": SC, "e": IC}
        HALVES = {"x": 1, "s": 2, "e": 1}
        WIDTH = {"x": D, "s": INNER, "e": INNER}
        NSTEPS = {"x": XTILES, "s": TILES, "e": ETILES}

        def chunk(ph, c):
            total = HALVES[ph] * WIDTH[ph]
            return c * P, min(P, total - c * P)

        block = ctx.enter_context(nc.Block())
        xv = x.rearrange("(t p) d -> p t d", p=P)
        ov = out.rearrange("(t p) d -> p t d", p=P)

        def triple(out_ap, a_hi, a_lo, b_hi, b_lo, first, last):
            nc.tensor.matmul(out_ap, a_hi, b_hi, start=first, stop=False)
            nc.tensor.matmul(out_ap, a_hi, b_lo, start=False, stop=False)
            return nc.tensor.matmul(out_ap, a_lo, b_hi, start=False, stop=last)

        def aT_parts(ph):
            return {"x": [(0, KC)], "s": [(0, KC), (KC, SC - 1), (SC - 1, SC)], "e": [(0, IC - 1), (IC - 1, IC)]}[ph]

        def aT_bank(ph, c0, c1, w):
            return bank[AT + c0 // KC][0:w, c0 % KC * P:(c0 % KC + c1 - c0) * P].rearrange("p (c n) -> p c n", n=P)

        @block.sync
        def _(sp):
            sp.dma_start(ids[:, :], token_ids).then_inc(S["ids_loaded"], 16)
            for b in range(BATCH):
                sp.dma_start(resid[:, TB * b:TB * b + TB, :], xv[:, TB * b:TB * b + TB, :]).then_inc(x_loaded[b], 16)
                if b == 0:
                    sp.dma_start(wg_raw[:, :, :], wgates).then_inc(S["wg_loaded"], 16)
                    sp.dma_start(wqkv_raw[:, :, :, :], wqkv[0]).then_inc(S["wqkv_loaded"], 16)
                    sp.dma_start(wo_raw[:, :], wo[0]).then_inc(S["wo_loaded"], 16)
            sp.dma_start(router_w[:, :, :], router).then_inc(S["router_loaded"], 16)
            sp.wait_ge(S["zeros_ready"], 1)
            for n, (rows_of, tiles) in enumerate(((xs, XTILES), (es, ETILES))):
                sp.dma_start(rows_of.rearrange("(t p) d -> p t d", p=P), zeros[:, :].unsqueeze(1).to_broadcast([P, tiles, D])).then_inc(S[f"zero_filled{n}"], 16)
            with sp.Fori(1, HEADS) as h:
                sp.wait_ge(S["wv_split"], h)
                sp.dma_start(wqkv_raw[:, :, :, :], wqkv[bass.ds(h, 1)].rearrange("a p c k d -> p (a c) k d")).then_inc(S["wqkv_loaded"], 16)
                sp.wait_ge(S["wo_split"], h)
                sp.dma_start(wo_raw[:, :], wo[bass.ds(h, 1)].rearrange("a p d -> p (a d)")).then_inc(S["wo_loaded"], 16)
            sp.wait_ge(S["zero_filled0"], 16)
            sp.wait_ge(S["zero_filled1"], 16)
            sp.wait_ge(S["route_x_done"], 1)
            for e in range(TOKEN_EXPERTS):
                if e == 2:
                    sp.wait_ge(S["ct_lo_pool"], 1)
                if e == 3:
                    sp.wait_ge(S["ct_lo_dve"], 1)
                sp.dma_start(raw[:, (e % 2) * KC * D:(e % 2 + 1) * KC * D].rearrange("p (k n) -> p k n", k=KC), ctxT[e]).then_inc(S[f"ct_loaded{e % 2}"], 16)

            def load_row(ph, source, g, j):
                sp.dma_start(rows[:, j, :], source[bass.ds(g * P, P)]).then_inc(S[f"{ph}_row{j}"], 16)

            def store_y(ph, target, g, j):
                sp.wait_ge(S[f"{ph}_y_out"], g + 1)
                sp.dma_start(target[bass.ds(g * P, P)], rows[:, 2 + j, :]).then_inc(S[f"{ph}_y_stored{j}"], 16)

            def feed_forward(ph, source, target):
                tiles = NSTEPS[ph]

                def step(g, j, first=False, load=True):
                    if load:
                        sp.wait_ge(S[f"{ph}_xT_ready"], g + 1)
                        load_row(ph, source, g + 2, j)
                    if not first:
                        store_y(ph, target, g - 1, 1 - j)

                load_row(ph, source, 0, 0)
                load_row(ph, source, 1, 1)
                step(0, 0, True)
                with sp.Fori(0, (tiles - 3) // 2) as it:
                    step(2 * it + 1, 1)
                    step(2 * it + 2, 0)
                step(tiles - 2, 1, load=False)
                step(tiles - 1, 0, load=False)
                store_y(ph, target, tiles - 1, 0)

            for i in range(TB):
                sp.wait_ge(scat[i], 16 * BATCH)
            feed_forward("x", xs, xs_out)

            sp.wait_ge(S["scat_e"], 16 * TOPK * TILES)
            sp.wait_ge(S["s_xT_ready"], TILES)
            feed_forward("e", es, es_out)
            for t in range(TILES):
                sp.wait_ge(S["combined"], TOPK * (t + 1))
                sp.dma_start(ov[:, t, :], resid[:, t, :]).then_inc(S["stored"], 16)
            sp.wait_ge(S["stored"], 16 * TILES)

        @block.gpsimd
        def _(pool):
            nc.gpsimd.memset(zeros[:, :], 0.0).then_inc(S["zeros_ready"], 1)
            nc.gpsimd.memset(ones[:, :], 1.0)
            nc.gpsimd.memset(neghalf[:, :], -0.5)
            nc.gpsimd.memset(ident[:, :], 0.0).then_inc(S["const_ready"], 1)
            pool.wait_ge(S["const_ready"], 1)
            nc.gpsimd.affine_select(out=ident[:, :], in_=ident[:, :], compare_op=ALU.not_equal, fill=1.0, base=0,
                                    pattern=[[-1, P]], channel_multiplier=1).then_inc(S["const_ready"], 1)
            nc.gpsimd.memset(causal[:, :, :], 1.0).then_inc(S["const_ready"], 1)
            pool.wait_ge(S["const_ready"], 3)
            nc.gpsimd.affine_select(out=causal[:, :, :], in_=causal[:, :, :], compare_op=ALU.is_ge, fill=0.0, base=0,
                                    pattern=[[0, 2], [1, P]], channel_multiplier=-1).then_inc(S["const_ready"], 1)

            nc.gpsimd.memset(earlier[:, :], 1.0).then_inc(S["const_ready"], 1)
            pool.wait_ge(S["const_ready"], 5)
            nc.gpsimd.affine_select(out=earlier[:, :], in_=earlier[:, :], compare_op=ALU.is_gt, fill=0.0, base=0,
                                    pattern=[[1, P]], channel_multiplier=-1).then_inc(S["const_ready"], 1)
            nc.gpsimd.iota(iota[:, :], [[1, ETILES]], base=0, channel_multiplier=0, allow_small_or_imprecise_dtypes=True).then_inc(S["const_ready"], 1)

            def low(raw, hi, lo, done, n):
                pool.wait_ge(S["w_hi"], n)
                nc.gpsimd.tensor_tensor(lo, raw, hi.bitcast(F32), ALU.subtract).then_inc(done, 1)

            def low_qkv(h, c, done):
                low(wqkv_raw[:, c, :, :], wqkv_hi[:, c, :, :], wqkv_lo[:, c, :, :], done, 4 * h + c + 2)

            def low_wo(h):
                low(wo_raw[:, :], wo_hi[:, :], wo_lo[:, :], S["wo_split"], 4 * h + 5)

            low(wg_raw[:, :, :], wg_hi[:, :, :], wg_lo[:, :, :], S["wg_split"], 1)
            for b in range(BATCH):
                pool.wait_ge(S["ln_eps"], b + 1)
                nc.gpsimd.tensor_tensor(rstd[:, :], vareps[:, :], neghalf[:, :], ALU.pow).then_inc(S["ln_rstd"], 1)
                if b == 0:
                    low_qkv(0, 0, S["wq_split"])
                    low_qkv(0, 1, S["wk_split"])
                    low_qkv(0, 2, S["wv_split"])
                    low_wo(0)

            def softmax_part(u):
                pool.wait_ge(S["exp_done"], u + 1)
                for diagonal in (probs[:, 0:2 * SEQ].rearrange("p (a c) -> p a c", a=2)[:, :, 0:P],
                                 probs[:, POFF[3]:POFF[3] + 2 * P].rearrange("p (a c) -> p a c", a=2)):
                    nc.gpsimd.tensor_tensor(diagonal, diagonal, causal[:, :, :], ALU.mult).then_inc(S["masked"], 1)
                pool.wait_ge(S["masked"], 2 * u + 2)
                nc.gpsimd.tensor_tensor(psum_keys[:, P:], probs[:, P:SEQ], probs[:, POFF[1]:POFF[1] + SEQ - P], ALU.add).then_inc(S["ssum_step"], 1)
                pool.wait_ge(S["ssum_step"], 2 * u + 1)
                nc.gpsimd.tensor_tensor(psum_keys[:, 2 * P:], psum_keys[:, 2 * P:], probs[:, POFF[2]:POFF[2] + 2 * P], ALU.add).then_inc(S["ssum_step"], 1)
                pool.wait_ge(S["ssum_step"], 2 * u + 2)
                nc.gpsimd.tensor_tensor(psum_keys[:, 3 * P:], psum_keys[:, 3 * P:], probs[:, POFF[3]:POFF[3] + P], ALU.add).then_inc(S["ssum_done"], 1)

            def head(h, first, last):
                for b in range(BATCH):
                    u = BATCH * h + b
                    if not (first and b == 0):
                        if not (first and b == 1):
                            pool.wait_ge(S["sum_ready"], u - 1)
                        softmax_part(u - 1)
                    if b == 1 and not first:
                        low_wo(h)
                    if b == BATCH - 1 and not last:
                        for c, done in enumerate(("wq_split", "wk_split", "wv_split")):
                            low_qkv(h + 1, c, S[done])

            pool.wait_ge(S["const_ready"], 4)
            head(0, True, False)
            with pool.Fori(1, HEADS - 1) as h:
                head(h, False, False)
            head(HEADS - 1, False, True)

            def rsqrt(n):
                pool.wait_ge(S["ln_eps"], n + 1)
                nc.gpsimd.tensor_tensor(rstd[:, :], vareps[:, :], neghalf[:, :], ALU.pow).then_inc(S["ln_rstd"], 1)

            def scatter_x(b):
                for i in range(TB):
                    pool.wait_ge(S["xn_ready"], TILES + TB * b + i + 1)
                    nc.gpsimd.indirect_dma_start(xs, bass.IndirectOffsetOnAxis(slot_x[:, TB * b + i:TB * b + i + 1], 0), rows[:, i, :], None).then_inc(scat[i], 16)

            pool.wait_ge(S["zero_filled0"], 16)
            pool.wait_ge(S["route_x_done"], 1)
            rsqrt(BATCH)
            scatter_x(0)
            pool.wait_ge(S["sum_ready"], U - 1)
            softmax_part(U - 1)
            pool.wait_ge(S["ct_hi_done"], 1)
            nc.gpsimd.tensor_tensor(ct_lo[:, 0], raw[:, 0:KC * D].rearrange("p (k n) -> p k n", k=KC), ct_hi[:, 0].bitcast(F32), ALU.subtract).then_inc(S["ct_lo_pool"], 1)
            for b in range(1, BATCH):
                rsqrt(BATCH + b)
                scatter_x(b)

            def split(raw, hi, lo, hi_done, n, done):
                nc.gpsimd.tensor_tensor(hi, raw, ones[:, 0:1].to_broadcast([P, raw.shape[1]]), ALU.mult).then_inc(hi_done, 1)
                pool.wait_ge(hi_done, n)
                nc.gpsimd.tensor_tensor(lo, raw, hi.bitcast(F32), ALU.subtract).then_inc(done, 1)

            pool.wait_ge(S["ct_lo_pool"], 1)
            pool.wait_ge(S["ct_lo_dve"], TOKEN_EXPERTS - 1)
            pool.wait_ge(S["y_added"], U * TB)
            for c, (source, hi, lo) in enumerate(((sh_up[:, 0:2, :], sh_up_hi[:, 0:2], sh_up_lo[:, 0:2]), (sh_up[:, 2:4, :], sh_up_hi[:, 2:4], sh_up_lo[:, 2:4]), (sh_down, sh_down_hi[:, :], sh_down_lo[:, :]))):
                piece = raw[:, 0:hi.shape[1] * hi.shape[2]]
                if c:
                    pool.wait_ge(S["sh_split"], c)
                nc.gpsimd.dma_start(piece.rearrange("p (k n) -> p k n", k=hi.shape[1]), source).then_inc(S["sh_loaded"], 16)
                pool.wait_ge(S["sh_loaded"], 16 * c + 16)
                hi, lo = (a.rearrange("p k n -> p (k n)") for a in (hi, lo))
                split(piece, hi, lo, S["sh_hi"], c + 1, S["sh_split"])

            for j in range(2):
                pool.wait_ge(S[f"x_y_stored{j}"], 16 * ((XTILES + 1 - j) // 2))

            def gather_x(b):
                for i in range(TB):
                    if b:
                        pool.wait_ge(S["x_added"], TB * (b - 1) + i + 1)
                    nc.gpsimd.indirect_dma_start(rows[:, i, :], None, xs_out, bass.IndirectOffsetOnAxis(slot_x[:, TB * b + i:TB * b + i + 1], 0)).then_inc(gath[i], 16)

            gather_x(0)
            for b in range(BATCH):
                if b + 1 < BATCH:
                    gather_x(b + 1)
                rsqrt(2 * BATCH + b)

            def load_weights(e, p):
                to = (raw, raw_odd)[p]
                nc.gpsimd.dma_start(up_of(to[:, 0:UP]), exp_up[bass.ds(e, 1)].rearrange("e p k n -> p (e k) n")).then_inc(S[f"up_loaded{p}"], 16)
                nc.gpsimd.dma_start(down_of(to[:, UP:]), exp_down[bass.ds(e, 1)].rearrange("e p k n -> p (e k) n")).then_inc(S[f"down_loaded{p}"], 16)

            def split_weights(i, p, wait=True):
                e = 2 * i + p
                if wait:
                    tiles_before = pool.value_load(expert_end[0:1, bass.ds(e - 2, 1)], min_val=0, max_val=ETILES)
                source = (raw, raw_odd)[p]
                for part, used, lo, hi in (("up", "e_xT_ready", 0, UP), ("down", "e_aT_ready", UP, UP + DOWN)):
                    pool.wait_ge(S[f"{part}_loaded{p}"], 16 * i + 16)
                    if wait:
                        pool.wait_ge(S[used], tiles_before + 1)
                    split(source[:, lo:hi], expert_w[:, p, 2 * lo:lo + hi], expert_w[:, p, lo + hi:2 * hi], S[f"{part}_hi"], e + 1, S[f"{part}_lo"])

            def next_weights(e, p):
                pool.wait_ge(S["down_lo"], e + 1)
                load_weights(e + 2, p)

            pool.wait_ge(S["zero_filled1"], 16)
            pool.wait_ge(S["route_e_done"], 1)
            load_weights(0, 0)
            for t in range(TILES):
                for c in range(TOPK):
                    nc.gpsimd.indirect_dma_start(es, bass.IndirectOffsetOnAxis(slot_e[c][:, t:t + 1], 0), x3[:, t, :], None).then_inc(S["scat_e"], 16)
            split_weights(0, 0, False)
            pool.wait_ge(S["s_y"], TILES)
            load_weights(1, 1)
            next_weights(0, 0)
            split_weights(0, 1, False)
            next_weights(1, 1)
            with pool.Fori(1, EXPERTS // 2 - 1) as i:
                for p in range(2):
                    split_weights(i, p)
                    next_weights(2 * i + p, p)
            for p in range(2):
                split_weights(EXPERTS // 2 - 1, p)

            for j in range(2):
                pool.wait_ge(S[f"e_y_stored{j}"], 16 * ((ETILES + 1 - j) // 2))
            for t in range(TILES):
                for c in range(TOPK):
                    n = TOPK * t + c
                    if n >= TB:
                        pool.wait_ge(S["combined"], n - TB + 1)
                    nc.gpsimd.indirect_dma_start(rows[:, n % TB, :], None, es_out, bass.IndirectOffsetOnAxis(slot_e[c][:, t:t + 1], 0)).then_inc(gath[n % TB], 16)

        @block.scalar
        def _(act):
            def high(hi, raw):
                nc.scalar.activation(hi, raw, ACT.Copy).then_inc(S["w_hi"], 1)

            act.wait_ge(S["wg_loaded"], 16)
            high(wg_hi[:, :, :], wg_raw[:, :, :])
            act.wait_ge(S["wqkv_loaded"], 16)
            for c in range(3):
                high(wqkv_hi[:, c, :, :], wqkv_raw[:, c, :, :])
            act.wait_ge(S["wo_loaded"], 16)
            high(wo_hi[:, :], wo_raw[:, :])
            for t in range(TILES):
                act.wait_ge(S["xnT_ready"], t + 1)
                nc.scalar.activation(xnT_hi[:, :, t * P:t * P + P], bank[t % 2][:, :].rearrange("p (k n) -> p k n", k=KC), ACT.Copy).then_inc(S["xnT_hi_done"], 1)
            for b in range(BATCH):
                act.wait_ge(S["gateT_ready"], b + 1)
                nc.scalar.activation(gateT[:, :], bank[2][:, :], ACT.Copy).then_inc(S["gateT_copied"], 1)
                act.wait_ge(S["gate_ready"], b + 1)
                nc.scalar.activation(gate_den[:, TB * b:TB * b + TB, :],
                                     bank[3][:, :].rearrange("p (t h) -> p t h", t=TB)[:, :, 0:HEADS], ACT.Exp, scale=-1.0).then_inc(S["gate_exp"], 1)

            def softmax_part(u, first):
                if not first:
                    act.wait_ge(S["p_lo_done"], u)
                    act.wait_ge(S["sum_ready"], u)
                act.wait_ge(S["s_ready"], u + 1)
                for i, (lo, n) in enumerate(((0, SEQ), (SEQ, SEQ), (2 * SEQ, 2 * P))):
                    nc.scalar.activation(probs[:, lo:lo + n], bank[2 + i][:, 0:n], ACT.Tanh, scale=SCALE / SOFTCAP).then_inc(S["tanh_done"], 1)
                act.wait_ge(S["tanh_done"], 3 * u + 3)
                nc.scalar.activation(probs[:, :], probs[:, :], ACT.Exp, scale=SOFTCAP).then_inc(S["exp_done"], 1)

            def o_part(u, b, early):
                act.wait_ge(S["pv_ready"], u + 1)
                if not early:
                    act.wait_ge(S["y_ready"], TB * (u - 1))
                nc.scalar.activation(o_hi[:, b % 2, :], bank[5][:, :], ACT.Copy).then_inc(S["o_hi_done"], 1)

            def high_qkv(h, c, u, ready):
                act.wait_ge(S["wqkv_loaded"], 16 * h + 32)
                act.wait_ge(S[ready], u + 1)
                high(wqkv_hi[:, c, :, :], wqkv_raw[:, c, :, :])

            def head(h, first, last):
                for b in range(BATCH):
                    u = BATCH * h + b
                    start = first and b == 0
                    refresh = b == BATCH - 1 and not last
                    if not start:
                        softmax_part(u - 1, first and b == 1)
                    act.wait_ge(S["q_ready"], u + 1)
                    if not start:
                        act.wait_ge(S["s_ready"], u)
                    nc.scalar.activation(q_hi[:, :], bank[0][:, :], ACT.Copy).then_inc(S["q_hi_done"], 1)
                    act.wait_ge(S["k_ready"], u + 1)
                    nc.scalar.activation(k_hi[:, :], bank[1][:, :], ACT.Copy).then_inc(S["k_hi_done"], 1)
                    if refresh:
                        high_qkv(h, 0, u, "q_ready")
                    act.wait_ge(S["vT_ready"], u + 1)
                    if not start:
                        act.wait_ge(S["v_ready"], u)
                    nc.scalar.activation(vT[:, :], bank[0][:, :], ACT.Copy).then_inc(S["vT_done"], 1)
                    if refresh:
                        high_qkv(h, 1, u, "k_ready")
                    if not start:
                        o_part(u - 1, b + 1, first and b < 3)
                    if refresh:
                        high_qkv(h, 2, u, "vT_ready")
                    act.wait_ge(S["v_ready"], u + 1)
                    if not start:
                        act.wait_ge(S["pv_ready"], u)
                    nc.scalar.activation(v_hi[:, :], bank[1][:, :], ACT.Copy).then_inc(S["v_hi_done"], 1)
                    if b == 1 and not first:
                        act.wait_ge(S["wo_loaded"], 16 * h + 16)
                        act.wait_ge(S["y_ready"], TB * BATCH * h)
                        high(wo_hi[:, :], wo_raw[:, :])

            head(0, True, False)
            with act.Fori(1, HEADS - 1) as h:
                head(h, False, False)
            head(HEADS - 1, False, True)
            softmax_part(U - 1, False)

            def ct_high(e):
                act.wait_ge(S[f"ct_loaded{e % 2}"], 16 * (e // 2) + 16)
                if e == 0:
                    act.wait_ge(S["vT_ready"], U)
                nc.scalar.activation(ct_hi[:, e], raw[:, (e % 2) * KC * D:(e % 2 + 1) * KC * D].rearrange("p (k n) -> p k n", k=KC), ACT.Copy).then_inc(S["ct_hi_done"], 1)

            ct_high(0)
            o_part(U - 1, 1, False)
            for e in range(1, TOKEN_EXPERTS):
                ct_high(e)

            def xT_high(ph, g):
                act.wait_ge(S[f"{ph}_xT_ready"], g + 1)
                nc.scalar.activation(xT_hi[:, :, :], bank[XT][:, :].rearrange("p (k n) -> p k n", k=KC), ACT.Copy).then_inc(S[f"{ph}_xT_hi"], 1)

            def y_copy(ph, i, j, wait=True):
                act.wait_ge(S[f"{ph}_y"], 2 * i + j + 1)
                if wait:
                    act.wait_ge(S[f"{ph}_y_stored{j}"], 16 * i)
                nc.scalar.activation(rows[:, 2 + j, :], bank[YB][:, :], ACT.Copy).then_inc(S[f"{ph}_y_out"], 1)

            def aT_high(ph, g):
                act.wait_ge(S[f"{ph}_aT_ready"], g + 1)
                for c0, c1 in aT_parts(ph):
                    w = chunk(ph, c0)[1]
                    nc.scalar.activation(aT_hi[0:w, c0:c1, :], aT_bank(ph, c0, c1, w), ACT.Copy).then_inc(S[f"{ph}_aT_hi"], 1)

            def step(ph, i, j, first=False, last=False, wait=True):
                g = 2 * i + j
                W, H = WIDTH[ph], HALVES[ph]
                act.wait_ge(S[f"{ph}_up"], g + 1)
                if not first:
                    act.wait_ge(S[f"{ph}_aT_ready"], g)
                for half in range(H):
                    nc.scalar.activation(act_sb[:, half * W:half * W + W], bank[2 * half][:, 0:W], ACT.Silu).then_inc(S[f"{ph}_silu"], 1)
                if not last:
                    xT_high(ph, g + 1)
                if not first and ph != "s":
                    y_copy(ph, i - 1 + j, 1 - j, wait)
                if ph == "s" and not first:
                    act.wait_ge(S["s_y"], g)
                aT_high(ph, g)

            def feed_forward(ph):
                tiles = NSTEPS[ph]
                xT_high(ph, 0)
                step(ph, 0, 0, first=True)
                step(ph, 0, 1, wait=False)
                step(ph, 1, 0, wait=False)
                with act.Fori(1, tiles // 2 - 1) as i:
                    step(ph, i, 1)
                    step(ph, i + 1, 0)
                step(ph, tiles // 2 - 1, 1)
                step(ph, tiles // 2, 0, last=True)
                y_copy(ph, tiles // 2, 0)

            feed_forward("x")

            for t in range(TILES):
                act.wait_ge(S["x3_T"], t + 1)
                if t >= 2:
                    act.wait_ge(S["logits_ready"], t - 1)
                nc.scalar.activation(x3T[:, t % 2, :], bank[XT + t % 2][:, :], ACT.Copy).then_inc(S["x3_copied"], 1)

            xT_high("s", 0)
            step("s", 0, 0, first=True)
            act.wait_ge(S["minus_max"], 1)
            nc.scalar.activation(logits[:, :], logits[:, :], ACT.Exp).then_inc(S["exp_router"], 1)
            step("s", 0, 1)
            with act.Fori(1, TILES // 2 - 1) as i:
                step("s", i, 0)
                step("s", i, 1)
            step("s", TILES // 2 - 1, 0)
            step("s", TILES // 2 - 1, 1, last=True)
            act.wait_ge(S["s_y"], TILES)
            feed_forward("e")

        @block.vector
        def _(dve):
            def layernorm(n, b, target, free):
                for i in range(TB):
                    nc.vector.bn_stats(stats[:, i, :], resid[:, TB * b + i, :]).then_inc(S["ln_stats"], 1)
                for i in range(TB):
                    dve.wait_ge(S["ln_stats"], TB * n + i + 1)
                    nc.vector.bn_aggr(meanvar[:, i, :], stats[:, i, :]).then_inc(S["ln_aggr"], 1)
                dve.wait_ge(S["ln_aggr"], TB * n + TB)
                nc.vector.tensor_scalar(vareps[:, :], meanvar[:, :, 1], EPS, None, ALU.add).then_inc(S["ln_eps"], 1)
                dve.wait_ge(S["ln_rstd"], n + 1)
                for i in range(TB):
                    free(i)
                    nc.vector.tensor_scalar(target(i), resid[:, TB * b + i, :], meanvar[:, i, 0:1], rstd[:, i:i + 1],
                                            ALU.subtract, ALU.mult).then_inc(S["xn_ready"], 1)

            steps = [0]

            def link(instruction):
                steps[0] += 1
                instruction.then_inc(S["step"], 1)
                dve.wait_ge(S["step"], steps[0])

            def route(experts, tiles, choices, prefix, prefix_done, tile_expert):
                n = experts * TILES
                by = lambda a: a[:, 0:n].rearrange("p (e t) -> p e t", e=experts)
                link(nc.vector.memset(restart[:, 0:n], 1.0))
                link(nc.vector.memset(by(restart)[:, :, 0], 0.0))
                link(nc.vector.tensor_tensor_scan(running[:, 0:n], restart[:, 0:n], prefix[:, n:2 * n], 0.0, ALU.mult, ALU.add))
                link(nc.vector.tensor_tensor(ahead[:, 0:n], running[:, 0:n], prefix[:, n:2 * n], ALU.subtract))
                nc.vector.tensor_tensor(ahead[:, 0:n], ahead[:, 0:n], prefix[:, 0:n], ALU.add).then_inc(prefix_done, 1)
                link(nc.vector.tensor_scalar(places[:, 0:TILES], iota[:, 0:TILES], float(P), None, ALU.mult))
                link(nc.vector.tensor_tensor(by(above), by(running)[:, :, TILES - 1].unsqueeze(2).to_broadcast([P, experts, TILES]),
                                             places[:, 0:TILES].unsqueeze(1).to_broadcast([P, experts, TILES]), ALU.is_gt))
                link(nc.vector.tensor_reduce(full[:, 0:experts], by(above), mybir.AxisListType.X, ALU.add))
                link(nc.vector.tensor_tensor_scan(upto[:, 0:experts], ones[:, 0:experts], full[:, 0:experts], 0.0, ALU.mult, ALU.add))
                link(nc.vector.tensor_tensor(base[:, 0:experts], upto[:, 0:experts], full[:, 0:experts], ALU.subtract))
                link(nc.vector.tensor_scalar(base[:, 0:experts], base[:, 0:experts], float(P), None, ALU.mult))
                dve.wait_ge(prefix_done, 1)
                link(nc.vector.tensor_tensor(by(places), by(ahead), base[:, 0:experts].unsqueeze(2).to_broadcast([P, experts, TILES]), ALU.add))
                for one, slot in choices:
                    link(nc.vector.tensor_tensor(above[:, 0:n], places[:, 0:n], one[:, 0:n], ALU.mult))
                    link(nc.vector.tensor_reduce(slot_f[:, :], above[:, 0:n].rearrange("p (e t) -> p t e", e=experts), mybir.AxisListType.X, ALU.add))
                    link(nc.vector.tensor_copy(slot[:, :], slot_f[:, :]))
                owners = tile_of[:, 0:tiles, 0:experts - 1]
                link(nc.vector.tensor_tensor(owners, iota[:, 0:tiles].unsqueeze(2).to_broadcast([P, tiles, experts - 1]),
                                             upto[:, 0:experts - 1].unsqueeze(1).to_broadcast([P, tiles, experts - 1]), ALU.is_ge))
                link(nc.vector.tensor_reduce(tile_f[:, 0:tiles], owners, mybir.AxisListType.X, ALU.add))
                return nc.vector.tensor_copy(tile_expert[:, :], tile_f[:, 0:tiles])

            def free_xn(b):
                return lambda i: dve.wait_ge(S["xnT_ready"], TB * (b - 1) + i + 1) if b else None

            for b in range(BATCH):
                dve.wait_ge(x_loaded[b], 16)
                layernorm(b, b, lambda i: xn[:, i, :], free_xn(b))
                for i in range(TB):
                    t = TB * b + i
                    cols = slice(t * P, t * P + P)
                    dve.wait_ge(S["xnT_hi_done"], t + 1)
                    nc.vector.tensor_tensor(xnT_lo[:, :, cols], bank[t % 2][:, :].rearrange("p (k n) -> p k n", k=KC),
                                            xnT_hi[:, :, cols].bitcast(F32), ALU.subtract).then_inc(S["xnT_lo_done"], 1)
            dve.wait_ge(S["gate_exp"], BATCH)
            nc.vector.tensor_scalar(gate_den[:, :, :], gate_den[:, :, :], 1.0, None, ALU.add).then_inc(S["gate_done"], 1)
            dve.wait_ge(S["gate_done"], 1)

            dve.wait_ge(S["ids_loaded"], 16)
            dve.wait_ge(S["const_ready"], 7)
            link(nc.vector.memset(ids_ge[:, 0, :], 1.0))
            link(nc.vector.memset(ids_ge[:, TOKEN_EXPERTS, :], 0.0))
            for e in range(1, TOKEN_EXPERTS):
                link(nc.vector.tensor_scalar(ids_ge[:, e, :], ids[:, :], float(e * IDS_PER_EXPERT), None, ALU.is_ge))
            nx = TOKEN_EXPERTS * TILES
            nc.vector.tensor_tensor(chosen[:, 0:nx].rearrange("p (e t) -> p e t", t=TILES), ids_ge[:, 0:TOKEN_EXPERTS, :], ids_ge[:, 1:, :], ALU.subtract).then_inc(S["chosen_ready"], 1)
            dve.wait_ge(S["prefix_ready"], 1)
            route(TOKEN_EXPERTS, XTILES, [(chosen, slot_x)], bank[4], S["prefix_read"], expert_x).then_inc(S["route_x_done"], 1)

            def lo_part(lo, ps, hi, hi_done, done, u):
                dve.wait_ge(S[hi_done], u + 1)
                nc.vector.tensor_tensor(lo, ps, hi.bitcast(F32), ALU.subtract).then_inc(S[done], 1)

            def y_add(u, b, i):
                dve.wait_ge(S["y_ready"], TB * u + i + 1)
                row = resid[:, TB * b + i, :]
                nc.vector.scalar_tensor_tensor(out=row, in0=bank[7][:, :], scalar=factor[:, b % 2, i:i + 1], in1=row,
                                               op0=ALU.mult, op1=ALU.add).then_inc(S["y_added"], 1)

            def p_part(u, first):
                if not first:
                    dve.wait_ge(S["pv_ready"], u)
                dve.wait_ge(S["masked"], 2 * u + 2)
                nc.vector.tensor_copy(p_hi[:, :], probs[:, :]).then_inc(S["p_hi_done"], 1)
                dve.wait_ge(S["p_hi_done"], u + 1)
                nc.vector.tensor_tensor(p_lo[:, :], probs[:, :], p_hi[:, :].bitcast(F32), ALU.subtract).then_inc(S["p_lo_done"], 1)

            def o_part(u, h, b):
                lo_part(o_lo[:, b % 2, :], bank[5][:, :], o_hi[:, b % 2, :], "o_hi_done", "o_lo_done", u)
                dve.wait_ge(S["sum_ready"], u + 1)
                nc.vector.tensor_tensor(denom[:, :], bank[6][:, 0:2 * TB].rearrange("p (t c) -> p t c", c=2)[:, :, 0],
                                        gate_den[:, TB * b:TB * b + TB, bass.ds(h, 1)].rearrange("p t a -> p (t a)"), ALU.mult).then_inc(S["den_done"], 1)
                dve.wait_ge(S["den_done"], u + 1)
                nc.vector.reciprocal(factor[:, b % 2, :], denom[:, :]).then_inc(S["factor_done"], 1)

            def head(h, first):
                for b in range(BATCH):
                    u = BATCH * h + b
                    start = first and b == 0
                    adds = not (first and b < 2)
                    b2 = (b + 2) % BATCH
                    if adds:
                        dve.wait_ge(S["factor_done"], u - 1)
                        y_add(u - 2, b2, 0)
                    lo_part(q_lo[:, :], bank[0][:, :], q_hi[:, :], "q_hi_done", "q_lo_done", u)
                    if not start:
                        p_part(u - 1, first and b == 1)
                    if adds:
                        y_add(u - 2, b2, 1)
                    lo_part(k_lo[:, :], bank[1][:, :], k_hi[:, :], "k_hi_done", "k_lo_done", u)
                    if adds:
                        y_add(u - 2, b2, 2)
                    if not start:
                        o_part(u - 1, h if b else h - 1, (b - 1) % BATCH)
                    if adds:
                        y_add(u - 2, b2, 3)
                    lo_part(v_lo[:, :], bank[1][:, :], v_hi[:, :], "v_hi_done", "v_lo_done", u)

            head(0, True)
            with dve.Fori(1, HEADS) as h:
                head(h, False)

            def layernorm_x(b):
                def free(i):
                    if b:
                        dve.wait_ge(scat[i], 16 * b)
                    else:
                        dve.wait_ge(S["xnT_ready"], TILES)
                dve.wait_ge(S["y_added"], TB * (U - BATCH + b + 1))
                layernorm(BATCH + b, b, lambda i: rows[:, i, :], free)

            layernorm_x(0)
            dve.wait_ge(S["factor_done"], U - 1)
            for i in range(TB):
                y_add(U - 2, BATCH - 2, i)
            p_part(U - 1, False)
            layernorm_x(1)
            o_part(U - 1, HEADS - 1, BATCH - 1)
            dve.wait_ge(S["factor_done"], U)
            for i in range(TB):
                y_add(U - 1, BATCH - 1, i)
            layernorm_x(2)
            layernorm_x(3)
            for e in range(1, TOKEN_EXPERTS):
                dve.wait_ge(S["ct_hi_done"], e + 1)
                nc.vector.tensor_tensor(ct_lo[:, e], raw[:, (e % 2) * KC * D:(e % 2 + 1) * KC * D].rearrange("p (k n) -> p k n", k=KC),
                                        ct_hi[:, e].bitcast(F32), ALU.subtract).then_inc(S["ct_lo_dve"], 1)

            def xT_low(ph, g):
                dve.wait_ge(S[f"{ph}_xT_hi"], g + 1)
                nc.vector.tensor_tensor(xT_lo[:, :, :], bank[XT][:, :].rearrange("p (k n) -> p k n", k=KC), xT_hi[:, :, :].bitcast(F32), ALU.subtract).then_inc(S[f"{ph}_xT_lo"], 1)

            def copy_row(t, j):
                nc.vector.tensor_copy(rows[:, j, :], x3[:, bass.ds(t, 1), :].rearrange("p a d -> p (a d)")).then_inc(S["s_row"], 1)

            def shared_add(t):
                dve.wait_ge(S["s_y"], t + 1)
                row = resid[:, bass.ds(t, 1), :].rearrange("p a d -> p (a d)")
                nc.vector.tensor_tensor(row, bank[YB][:, :], row, ALU.add).then_inc(S["s_y_out"], 1)

            def step(ph, g, j=0, first=False, last=False, rows_left=True):
                W, H = WIDTH[ph], HALVES[ph]
                for i in range(H):
                    dve.wait_ge(S[f"{ph}_silu"], H * g + i + 1)
                    part = act_sb[:, i * W:i * W + W]
                    nc.vector.tensor_tensor(part, part, bank[2 * i + (ph != "x")][:, 0:W], ALU.mult).then_inc(S[f"{ph}_act"], 1)
                if not last:
                    xT_low(ph, g + 1)
                    if ph == "s" and rows_left:
                        copy_row(g + 2, j)
                if ph == "s" and not first:
                    shared_add(g - 1)
                parts = aT_parts(ph)
                for c0, c1 in parts:
                    w = chunk(ph, c0)[1]
                    read = sum(p[0] // KC <= c0 // KC for p in parts)
                    dve.wait_ge(S[f"{ph}_aT_hi"], len(parts) * g + read)
                    nc.vector.tensor_tensor(aT_lo[0:w, c0:c1, :], aT_bank(ph, c0, c1, w), aT_hi[0:w, c0:c1, :].bitcast(F32), ALU.subtract).then_inc(S[f"{ph}_aT_lo"], 1)

            def feed_forward(ph):
                xT_low(ph, 0)
                step(ph, 0, first=True)
                with dve.Fori(1, NSTEPS[ph] - 1) as g:
                    step(ph, g)
                step(ph, NSTEPS[ph] - 1, last=True)

            feed_forward("x")

            for b in range(BATCH):
                for i in range(TB):
                    dve.wait_ge(gath[i], 16 * b + 16)
                    row = resid[:, TB * b + i, :]
                    nc.vector.tensor_tensor(row, row, rows[:, i, :], ALU.add).then_inc(S["x_added"], 1)
                dve.wait_ge(S["x_added"], TB * b + TB)
                layernorm(2 * BATCH + b, b, lambda i: x3[:, TB * b + i, :], lambda i: None)
            dve.wait_ge(S["xn_ready"], 3 * TILES)
            copy_row(0, 0)
            dve.wait_ge(S["logits_ready"], TILES)
            nc.vector.tensor_copy(logits[:, :], bank[YB][:, 0:NE]).then_inc(S["logits_read"], 1)
            xT_low("s", 0)
            copy_row(1, 1)

            dve.wait_ge(S["logits_read"], 1)
            by_expert = logits[:, :].rearrange("p (t e) -> p t e", e=EXPERTS)
            over = lambda a: a.unsqueeze(2).to_broadcast([P, TILES, EXPERTS])
            link(nc.vector.tensor_reduce(row_max[:, :], by_expert, mybir.AxisListType.X, ALU.max))
            nc.vector.tensor_tensor(by_expert, by_expert, over(row_max[:, :]), ALU.subtract).then_inc(S["minus_max"], 1)
            step("s", 0, first=True)
            dve.wait_ge(S["exp_router"], 1)
            link(nc.vector.tensor_reduce(row_sum[:, :], by_expert, mybir.AxisListType.X, ALU.add))
            link(nc.vector.reciprocal(row_sum[:, :], row_sum[:, :]))
            link(nc.vector.tensor_tensor(by_expert, by_expert, over(row_sum[:, :]), ALU.mult))
            for t in range(TILES):
                top = nc.vector.max(best[:, t, :], by_expert[:, t, :])
            link(top)
            for t in range(TILES):
                top = nc.vector.max_index(best_at[:, t, :], best[:, t, :], by_expert[:, t, :])
            link(top)
            link(nc.vector.tensor_copy(best_f[:, :, :], best_at[:, :, 0:TOPK]))
            link(nc.vector.tensor_tensor(row_sum[:, :], best[:, :, 0], best[:, :, 1], ALU.add))
            link(nc.vector.tensor_scalar(row_sum[:, :], row_sum[:, :], 1e-20, None, ALU.add))
            link(nc.vector.reciprocal(row_sum[:, :], row_sum[:, :]))
            for c in range(TOPK):
                link(nc.vector.tensor_tensor(weight_e[c][:, :], best[:, :, c], row_sum[:, :], ALU.mult))
                link(nc.vector.tensor_tensor(choice[c][:, :].rearrange("p (e t) -> p e t", e=EXPERTS),
                                             iota[:, 0:EXPERTS].unsqueeze(2).to_broadcast([P, EXPERTS, TILES]),
                                             best_f[:, :, c].unsqueeze(1).to_broadcast([P, EXPERTS, TILES]), ALU.is_equal))
            nc.vector.tensor_tensor(chosen[:, :], choice[0][:, :], choice[1][:, :], ALU.add).then_inc(S["chosen_ready"], 1)
            for g in range(1, ROUTE_STEP):
                step("s", g, g % 2)
            dve.wait_ge(S["prefix_ready"], 2)
            dve.wait_ge(S["prefix_read"], 1)
            link(route(EXPERTS, ETILES, list(zip(choice, slot_e)), bank[YB], S["prefix_e_read"], expert_e))
            link(nc.vector.tensor_copy(expert_end[:, :], upto[:, :]))
            owners = tile_of[:, :, :]
            link(nc.vector.tensor_reduce(tile_f[:, :], owners[:, :, 0::2], mybir.AxisListType.X, ALU.add))
            link(nc.vector.tensor_reduce(odd_f[:, :], owners[:, :, 1::2], mybir.AxisListType.X, ALU.add))
            nc.vector.tensor_tensor(place_e[:, :], tile_f[:, :], odd_f[:, :], ALU.subtract).then_inc(S["route_e_done"], 1)
            with dve.Fori(ROUTE_STEP // 2, TILES // 2 - 1) as it:
                for j in range(2):
                    step("s", 2 * it + j, j)
            step("s", TILES - 2, rows_left=False)
            step("s", TILES - 1, last=True)
            shared_add(TILES - 1)
            feed_forward("e")

            for t in range(TILES):
                row = resid[:, t, :]
                for c in range(TOPK):
                    n = TOPK * t + c
                    dve.wait_ge(gath[n % TB], 16 * BATCH + 16 * (n // TB) + 16)
                    if c:
                        dve.wait_ge(S["combined"], n)
                    nc.vector.scalar_tensor_tensor(out=row, in0=rows[:, n % TB, :], scalar=weight_e[c][:, t:t + 1], in1=row,
                                                   op0=ALU.mult, op1=ALU.add).then_inc(S["combined"], 1)

        @block.tensor
        def _(pe):
            pe.wait_ge(S["const_ready"], 6)
            for t in range(TILES):
                if t >= 2:
                    pe.wait_ge(S["xnT_lo_done"], t - 1)
                pe.wait_ge(S["xn_ready"], t + 1)
                for k in range(KC):
                    last = nc.tensor.transpose(bank[t % 2][:, k * P:k * P + P], xn[:, t % TB, k * P:k * P + P], ident[:, :])
                last.then_inc(S["xnT_ready"], 1)
            pe.wait_ge(S["wg_split"], 1)
            pe.wait_ge(S["xnT_lo_done"], TILES)
            for b in range(BATCH):
                cols = slice(b * SEQ, b * SEQ + SEQ)
                for k in range(KC):
                    last = triple(bank[2][:, :], wg_hi[:, k, :], wg_lo[:, k, :], xnT_hi[:, k, cols], xnT_lo[:, k, cols], k == 0, k == KC - 1)
                last.then_inc(S["gateT_ready"], 1)
                pe.wait_ge(S["gateT_copied"], b + 1)
                if b:
                    pe.wait_ge(S["gate_exp"], b)
                for i in range(TB):
                    last = nc.tensor.transpose(bank[3][:, i * P:i * P + P], gateT[:, i * P:i * P + P], ident[:, :])
                last.then_inc(S["gate_ready"], 1)

            def count_ahead(experts, to, n):
                pe.wait_ge(S["chosen_ready"], n)
                n = experts * TILES
                nc.tensor.matmul(to[:, 0:n], earlier[:, :], chosen[:, 0:n], start=True, stop=True)
                nc.tensor.matmul(to[:, n:2 * n], ones[:, :], chosen[:, 0:n], start=True, stop=True).then_inc(S["prefix_ready"], 1)

            count_ahead(TOKEN_EXPERTS, bank[4], 1)

            def project(c, b, to, ready):
                cols = slice(b * SEQ, b * SEQ + SEQ)
                for k in range(KC):
                    last = triple(to[:, :], wqkv_hi[:, c, k, :], wqkv_lo[:, c, k, :], xnT_hi[:, k, cols], xnT_lo[:, k, cols], k == 0, k == KC - 1)
                last.then_inc(S[ready], 1)

            def scores(u, first):
                pe.wait_ge(S["q_lo_done"], u + 1)
                pe.wait_ge(S["k_lo_done"], u + 1)
                if first:
                    pe.wait_ge(S["gate_exp"], BATCH)
                    pe.wait_ge(S["prefix_read"], 1)
                else:
                    pe.wait_ge(S["exp_done"], u)
                for j in (0, 1, 3, 2):
                    to = bank[2 + POFF[j] // SEQ][:, POFF[j] % SEQ:POFF[j] % SEQ + SEQ - P * j]
                    last = triple(to, k_hi[:, j * P:j * P + P], k_lo[:, j * P:j * P + P], q_hi[:, j * P:], q_lo[:, j * P:], True, True)
                last.then_inc(S["s_ready"], 1)

            def values(u, first):
                pe.wait_ge(S["p_lo_done"], u + 1)
                if not first:
                    pe.wait_ge(S["o_lo_done"], u)
                for j in range(TB):
                    n = SEQ - P * j
                    last = triple(bank[5][:, P * j:], v_hi[:, j * P:j * P + P], v_lo[:, j * P:j * P + P],
                                  p_hi[:, POFF[j]:POFF[j] + n], p_lo[:, POFF[j]:POFF[j] + n], j == 0, j == TB - 1)
                last.then_inc(S["pv_ready"], 1)
                pe.wait_ge(S["ssum_done"], u + 1)
                if not first:
                    pe.wait_ge(S["factor_done"], u)
                for i in range(TB):
                    src = probs if i == 0 else psum_keys
                    last = nc.tensor.matmul(bank[6][:, 2 * i:2 * i + 2], src[:, i * P:i * P + P], ones[:, 0:2], start=True, stop=True)
                last.then_inc(S["sum_ready"], 1)

            def output(u, b, i, h, very_first):
                pe.wait_ge(S["o_lo_done"], u + 1)
                if i == 0 and b == 0:
                    pe.wait_ge(S["wo_split"], h + 1)
                if not very_first:
                    pe.wait_ge(S["y_added"], TB * u + i)
                triple(bank[7][:, :], o_hi[:, b % 2, i * P:i * P + P], o_lo[:, b % 2, i * P:i * P + P], wo_hi[:, :], wo_lo[:, :], True, True).then_inc(S["y_ready"], 1)

            def head(h, first):
                for b in range(BATCH):
                    u = BATCH * h + b
                    start = first and b == 0
                    outputs = not (first and b < 2)
                    b2, h2 = (b + 2) % BATCH, h if b >= 2 else h - 1
                    if b == 0:
                        for n in ("wq_split", "wk_split", "wv_split"):
                            pe.wait_ge(S[n], h + 1)
                    if not start:
                        pe.wait_ge(S["vT_done"], u)
                    project(0, b, bank[0], "q_ready")
                    if outputs:
                        output(u - 2, b2, 0, h2, first and b == 2)
                    if not start:
                        pe.wait_ge(S["v_lo_done"], u)
                    project(1, b, bank[1], "k_ready")
                    if outputs:
                        output(u - 2, b2, 1, h2, False)
                    pe.wait_ge(S["q_lo_done"], u + 1)
                    project(2, b, bank[0], "vT_ready")
                    if outputs:
                        output(u - 2, b2, 2, h2, False)
                    if not start:
                        values(u - 1, first and b == 1)
                    if outputs:
                        output(u - 2, b2, 3, h2, False)
                    scores(u, start)
                    pe.wait_ge(S["vT_done"], u + 1)
                    for i in range(TB):
                        last = nc.tensor.transpose(bank[1][:, i * P:i * P + P], vT[:, i * P:i * P + P], ident[:, :])
                    last.then_inc(S["v_ready"], 1)

            head(0, True)
            with pe.Fori(1, HEADS) as h:
                head(h, False)
            for i in range(TB):
                output(U - 2, BATCH - 2, i, HEADS - 1, False)
            pe.wait_ge(S["v_lo_done"], U)
            values(U - 1, False)
            for i in range(TB):
                output(U - 1, BATCH - 1, i, HEADS - 1, False)

            def transpose_rows(ph, i, j):
                if ph == "s":
                    pe.wait_ge(S["s_row"], 2 * i + j + 1)
                else:
                    pe.wait_ge(S[f"{ph}_row{j}"], 16 * i + 16)
                for k in range(KC):
                    last = nc.tensor.transpose(bank[XT][:, k * P:k * P + P], rows[:, j, k * P:k * P + P], ident[:, :])
                last.then_inc(S[f"{ph}_xT_ready"], 1)

            def up(ph, g, products, first):
                pe.wait_ge(S[f"{ph}_xT_lo"], g + 1)
                if not first:
                    pe.wait_ge(S[f"{ph}_act"], HALVES[ph] * g)
                for j, (hi, lo) in enumerate(products):
                    for k in range(KC):
                        last = triple(bank[j][:, 0:WIDTH[ph]], xT_hi[:, k, :], xT_lo[:, k, :], hi(k), lo(k), k == 0, k == KC - 1)
                last.then_inc(S[f"{ph}_up"], 1)

            def down(ph, g, hi, lo, second):
                pe.wait_ge(S[f"{ph}_aT_lo"], len(aT_parts(ph)) * (g + 1))
                if second:
                    pe.wait_ge(S[f"{ph}_y_out"], g)
                for c in range(NCH[ph]):
                    w = chunk(ph, c)[1]
                    last = triple(bank[YB][:, :], aT_hi[0:w, c, :], aT_lo[0:w, c, :], hi(c, w), lo(c, w), c == 0, c == NCH[ph] - 1)
                last.then_inc(S[f"{ph}_y"], 1)

            def transpose_act(ph, g):
                pe.wait_ge(S[f"{ph}_act"], HALVES[ph] * (g + 1))
                for c in range(NCH[ph]):
                    c0, w = chunk(ph, c)
                    last = nc.tensor.transpose(bank[AT + c // KC][0:w, c % KC * P:c % KC * P + P], act_sb[:, c0:c0 + w], ident[:, :])
                last.then_inc(S[f"{ph}_aT_ready"], 1)

            def matrix(g):
                e = pe.value_load(expert_x[0:1, bass.ds(g, 1)], min_val=0, max_val=TOKEN_EXPERTS - 1)
                return [lambda k, w=P, m=m: m[0:w, bass.ds(e, 1), k, :].rearrange("p a n -> p (a n)") for m in (ct_hi, ct_lo)]

            def x_step(i, j, first=False, last=False, second=True):
                g = 2 * i + j
                up("x", g, [matrix(g)], first)
                if not last:
                    transpose_rows("x", i + j, 1 - j)
                if not first:
                    down("x", g - 1, *matrix(g - 1), second)
                transpose_act("x", g)

            def feed_forward(step, tiles):
                step(0, 0, first=True)
                step(0, 1, second=False)
                with pe.Fori(1, tiles // 2) as i:
                    step(i, 0)
                    step(i, 1)
                step(tiles // 2, 0, last=True)

            transpose_rows("x", 0, 0)
            pe.wait_ge(S["ct_lo_pool"], 1)
            pe.wait_ge(S["ct_lo_dve"], TOKEN_EXPERTS - 1)
            feed_forward(x_step, XTILES)
            down("x", XTILES - 1, *matrix(XTILES - 1), True)

            def transpose_x3(t):
                pe.wait_ge(S["xn_ready"], 2 * TILES + t + 1)
                if t >= 2:
                    pe.wait_ge(S["x3_copied"], t - 1)
                for k in range(KC):
                    last = nc.tensor.transpose(bank[XT + t % 2][:, k * P:k * P + P], x3[:, t, k * P:k * P + P], ident[:, :])
                last.then_inc(S["x3_T"], 1)

            pe.wait_ge(S["router_loaded"], 16)
            pe.wait_ge(S["x_y_out"], XTILES)
            transpose_x3(0)
            for t in range(TILES):
                if t + 1 < TILES:
                    transpose_x3(t + 1)
                pe.wait_ge(S["x3_copied"], t + 1)
                for k in range(KC):
                    last = nc.tensor.matmul(bank[YB][:, t * EXPERTS:(t + 1) * EXPERTS], x3T[:, t % 2, k * P:k * P + P], router_w[:, k, :], start=(k == 0), stop=(k == KC - 1))
                last.then_inc(S["logits_ready"], 1)

            pe.wait_ge(S["sh_split"], 3)
            shared = [[lambda k, m=m, j=j: m[:, k, j * INNER:(j + 1) * INNER] for m in (sh_up_hi, sh_up_lo)] for j in range(4)]
            shared_down = [lambda c, w, m=m: m[0:w, c, :] for m in (sh_down_hi, sh_down_lo)]

            def s_step(i, j, first=False, last=False, second=True):
                g = 2 * i + j
                up("s", g, shared, first)
                if not last:
                    transpose_rows("s", i + j, 1 - j)
                if not first:
                    down("s", g - 1, *shared_down, second)
                transpose_act("s", g)

            transpose_rows("s", 0, 0)
            s_step(0, 0, first=True)
            pe.wait_ge(S["logits_read"], 1)
            for g in range(1, ROUTE_STEP):
                s_step(g // 2, g % 2, second=g > 1)
            pe.wait_ge(S["s_y_out"], ROUTE_STEP - 1)
            count_ahead(EXPERTS, bank[YB], 2)
            pe.wait_ge(S["prefix_e_read"], 1)
            with pe.Fori(ROUTE_STEP // 2, TILES // 2 - 1) as i:
                s_step(i, 0)
                s_step(i, 1)
            s_step(TILES // 2 - 1, 0)
            s_step(TILES // 2 - 1, 1, last=True)
            down("s", TILES - 1, *shared_down, True)

            def place(g):
                return pe.value_load(place_e[0:1, bass.ds(g, 1)], min_val=0, max_val=1)

            def wait_weights(g, split):
                e = pe.value_load(expert_e[0:1, bass.ds(g, 1)], min_val=0, max_val=EXPERTS - 1)
                pe.wait_ge(S[split], e + 1)

            def e_up(g, first):
                p = place(g)
                wait_weights(g, "up_lo")
                products = [[lambda k, at=part + c * INNER: expert_w[:, bass.ds(p, 1), at + 2 * INNER * k:at + 2 * INNER * k + INNER].rearrange("p a n -> p (a n)")
                             for part in (0, UP)] for c in range(2)]
                up("e", g, products, first)

            def e_down(g, second):
                p = place(g)
                wait_weights(g, "down_lo")
                down("e", g, *[lambda c, w, at=part: expert_w[0:w, bass.ds(p, 1), at + c * D:at + c * D + D].rearrange("p a n -> p (a n)")
                               for part in (2 * UP, 2 * UP + DOWN)], second)

            def e_step(i, j, first=False, last=False, second=True):
                g = 2 * i + j
                e_up(g, first)
                if not last:
                    transpose_rows("e", i + j, 1 - j)
                if not first:
                    e_down(g - 1, second)
                transpose_act("e", g)

            pe.wait_ge(S["s_y_out"], TILES)
            pe.wait_ge(S["route_e_done"], 1)
            transpose_rows("e", 0, 0)
            feed_forward(e_step, ETILES)
            e_down(ETILES - 1, True)


def kernel(x, itok_BxS_13_99985, ctx_2048, L0_attn_w_qkv, L0_attn_w_gates, L0_attn_w_out, L0_ffn_gate_w, L0_ffn_expert_gate, L0_ffn_expert_up, L0_ffn_expert_down, L0_ffn_shared_gate, L0_ffn_shared_up, L0_ffn_shared_down):
    import numpy as np
    import concourse.bacc as bacc
    from concourse.bass_utils import run_bass_kernel_spmd

    c = np.ascontiguousarray
    f = lambda a: np.asarray(a)
    wg = np.zeros((D, P), np.float32)
    wg[:, :HEADS] = f(L0_attn_w_gates)
    chunks = lambda a: a.reshape(-1, P, a.shape[-1]).transpose(1, 0, 2)
    up = np.concatenate([f(L0_ffn_expert_gate), f(L0_ffn_expert_up)], 1).transpose(0, 2, 1)
    down = np.zeros((EXPERTS, IC * P, D), np.float32)
    down[:, :INNER] = f(L0_ffn_expert_down).transpose(0, 2, 1)
    halves = [m[j * INNER:(j + 1) * INNER] for j in range(2) for m in (f(L0_ffn_shared_gate), f(L0_ffn_shared_up))]
    sh_down = np.zeros((SC * P, D), np.float32)
    sh_down[:SHARED] = f(L0_ffn_shared_down).T
    arrays = {
        "x": c(f(x).reshape(T, D)),
        "token_ids": c(f(itok_BxS_13_99985).reshape(TILES, P).T),
        "wqkv": c(f(L0_attn_w_qkv).reshape(KC, P, 3, HEADS, DH).transpose(3, 1, 2, 0, 4)),
        "wgates": c(wg.reshape(KC, P, P).transpose(1, 0, 2)),
        "wo": c(f(L0_attn_w_out).reshape(HEADS, DH, D)),
        "ctxT": c(np.stack([chunks(m.T) for m in f(ctx_2048)])),
        "router": c(chunks(f(L0_ffn_gate_w).T)),
        "exp_up": c(np.stack([chunks(m) for m in up])),
        "exp_down": c(np.stack([chunks(m) for m in down])),
        "sh_up": c(chunks(np.concatenate(halves, 0).T)),
        "sh_down": c(chunks(sh_down)),
    }
    nc = bacc.Bacc("TRN2", target_bir_lowering=False, num_devices=1)
    args = [nc.dram_tensor(n, a.shape, mybir.dt.from_np(a.dtype), kind="ExternalInput").ap() for n, a in arrays.items()]
    args.append(nc.dram_tensor("out", (T, D), F32, kind="ExternalOutput").ap())
    build(nc, *args)
    r = run_bass_kernel_spmd(nc, [arrays], core_ids=[0])
    return r.results[0]["out"].reshape(BATCH, SEQ, D)
```

```python
from contextlib import ExitStack

import concourse.bass as bass
from concourse import mybir

F32 = mybir.dt.float32
F32R = mybir.dt.float32r
ALU = mybir.AluOpType
ACT = mybir.ActivationFunctionType

P = 128
BATCH, SEQ, D = 4, 512, 512
T = BATCH * SEQ
KC = D // P
TILES = T // P
TB = SEQ // P
HEADS, DH = 16, 128
SOFTCAP = 50.0
SCALE = DH ** -0.5
EPS = 1e-5
PCOLS = sum(SEQ - P * j for j in range(TB))
POFF = {0: 0, 1: SEQ, 3: 2 * SEQ - P, 2: 2 * SEQ}

VOCAB, TOKEN_EXPERTS = 25000, 4
IDS_PER_EXPERT = VOCAB // TOKEN_EXPERTS
PARTS = 2
PT = TILES // PARTS
XPART = PT + TOKEN_EXPERTS - 1
XTILES = PARTS * XPART
EXPERTS, TOPK, INNER = 8, 2, 352
SHARED = 2 * INNER
ETILES = TOPK * T // P + EXPERTS - 1
IC = -(-INNER // P)
SC = -(-SHARED // P)


def build(nc, x, token_ids, wqkv, wgates, wo, ctxT, router, exp_up, exp_down, sh_up, sh_down, out):
    with ExitStack() as ctx:
        I32, U32 = mybir.dt.int32, mybir.dt.uint32
        SBUF0, ALIGN = 16512, 32

        class Region:

            def __init__(self, start):
                self.at = start

            def __call__(self, name, shape, dt=F32):
                size = 4
                for n in shape[1:]:
                    size *= n
                t = nc.alloc_sbuf_tensor_at(name, shape, dt, offset=self.at)
                self.at += -(-size // ALIGN) * ALIGN
                return t

        def sem(name):
            return ctx.enter_context(nc.semaphore(name))

        bank = [ctx.enter_context(nc.psum_tensor(f"bank{i}", [P, 512], F32)) for i in range(8)]

        sb = Region(SBUF0)
        resid = sb("resid", [P, TILES, D])
        ident = sb("ident", [P, P])
        earlier = sb("earlier", [P, P])
        ones = sb("ones", [P, P])
        ones_r = sb("ones_r", [P, P], F32R)
        neghalf = sb("neghalf", [P, TB])
        iota = sb("iota", [P, ETILES])
        stats = sb("stats", [P, TB, 6])
        meanvar = sb("meanvar", [P, TB, 2])
        vareps = sb("vareps", [P, TB])
        rstd = sb("rstd", [P, TB])
        ids = sb("ids", [P, TILES], I32)
        slot_x = sb("slot_x", [P, TILES], U32)
        slot_part = sb("slot_part", [P, TILES], U32)
        slot_e = [sb(f"slot_e{c}", [P, TILES], U32) for c in range(TOPK)]
        weight_e = [sb(f"weight_e{c}", [P, TILES]) for c in range(TOPK)]
        expert_x = sb("expert_x", [P, XTILES], I32)
        expert_e = sb("expert_e", [P, ETILES], I32)
        place_e = sb("place_e", [P, ETILES], I32)
        expert_end = sb("expert_end", [P, EXPERTS], I32)
        low_stored = sb("low_stored", [P, 2], I32)
        router_w = sb("router_w", [P, KC, EXPERTS])

        rows = sb("rows", [P, TB, D])

        first_region = sb.at
        xnT_hi = sb("xnT_hi", [P, KC, T], F32R)
        xnT_lo = sb("xnT_lo", [P, KC, T], F32R)
        ct_hi = xnT_hi[:, :, :].rearrange("p e (k f) -> p e k f", k=KC)
        ct_lo = xnT_lo[:, :, :].rearrange("p e (k f) -> p e k f", k=KC)
        UP, DOWN = KC * 2 * INNER, IC * D
        sb = Region(first_region)
        x3_late = sb("x3_late", [P, PT, D])
        routing_at = sb.at
        weights_at = first_region + 4 * TILES * D
        sb = Region(weights_at)
        expert_w = sb("expert_w", [P, 2, 2 * (UP + DOWN)], F32R)
        over_shared = Region(sb.at)
        second_region = weights_at + 4 * 2 * (UP + DOWN)

        sb = Region(second_region)
        sh_up_hi = sb("sh_up_hi", [P, KC, 2 * SHARED], F32R)
        sh_up_lo = sb("sh_up_lo", [P, KC, 2 * SHARED], F32R)
        sh_down_hi = sb("sh_down_hi", [P, SC, D], F32R)
        sh_down_lo = sb("sh_down_lo", [P, SC, D], F32R)
        raw_odd = over_shared("raw_odd", [P, UP + DOWN])
        assert over_shared.at <= sb.at
        xT_hi = sb("xT_hi", [P, KC, P], F32R)
        xT_lo = sb("xT_lo", [P, KC, P], F32R)
        act_sb = sb("act_sb", [P, SHARED])
        aT_hi = sb("aT_hi", [P, SC, P], F32R)
        aT_lo = sb("aT_lo", [P, SC, P], F32R)
        raw_at = sb.at
        raw = sb("raw", [P, UP + DOWN])
        assert sb.at <= nc.sbuf_usable_end

        def up_of(weights):
            return weights.rearrange("p (k n) -> p k n", k=KC)

        def down_of(weights):
            return weights.rearrange("p (c n) -> p c n", c=IC)

        NE = EXPERTS * TILES

        class Routing:

            def __init__(self, name, at):
                self.region = sb = Region(at)
                self.chosen, self.running, self.ahead, self.places, self.above, self.restart = (
                    sb(f"{name}_{n}", [P, NE]) for n in ("chosen", "running", "ahead", "places", "above", "restart"))
                self.tile_of = sb(f"{name}_tile_of", [P, ETILES, EXPERTS - 1])
                self.tile_f = sb(f"{name}_tile_f", [P, ETILES])
                self.slot_f = sb(f"{name}_slot_f", [P, TILES])
                self.full, self.upto, self.base = (sb(f"{name}_{n}", [P, EXPERTS]) for n in ("full", "upto", "base"))

        by_id = Routing("by_id", raw_at)
        sb = by_id.region
        zeros = sb("zeros", [P, D])
        ids_ge = sb("ids_ge", [P, TOKEN_EXPERTS + 1, TILES])
        assert sb.at <= nc.sbuf_usable_end
        x3_early = Region(raw_at)("x3_early", [P, PT, D])
        by_router = Routing("by_router", routing_at)
        sb = by_router.region
        x3T = sb("x3T", [P, 2, D])
        logits = sb("logits", [P, NE])
        choice = [sb(f"choice{c}", [P, NE]) for c in range(TOPK)]
        best = sb("best", [P, TILES, 8])
        best_at = sb("best_at", [P, TILES, 8], U32)
        best_f = sb("best_f", [P, TILES, TOPK])
        odd_f = sb("odd_f", [P, ETILES])
        is_low = sb("is_low", [P, (ETILES + 1) // 2])
        low_f = sb("low_f", [P, 2])
        first_lower, second_lower = (sb(n, [P, TILES]) for n in ("first_lower", "second_lower"))
        share = [sb(f"share{c}", [P, TILES]) for c in range(TOPK)]
        share_part = [sb(f"share_part{c}", [P, TILES]) for c in range(TOPK)]
        row_max = sb("row_max", [P, TILES])
        row_sum = sb("row_sum", [P, TILES])
        assert sb.at <= weights_at

        low_rows = Region(first_region)("low_rows", [P, TILES, D])
        high_rows = x3_early

        def x3(t):
            return x3_early[:, t, :] if t < PT else x3_late[:, t - PT, :]

        sb = Region(second_region)
        xn = rows
        causal = sb("causal", [P, 2, P])
        ct_more = Region(sb.at)("ct_more", [P, 2 * KC * D])
        wqkv_raw = sb("wqkv_raw", [P, 3, KC, DH])
        wqkv_hi = sb("wqkv_hi", [P, 3, KC, DH], F32R)
        wqkv_lo = sb("wqkv_lo", [P, 3, KC, DH], F32R)
        wo_raw = sb("wo_raw", [P, D])
        wo_hi = sb("wo_hi", [P, D], F32R)
        wo_lo = sb("wo_lo", [P, D], F32R)
        gate_den = sb("gate_den", [P, TILES, HEADS])
        vT = sb("vT", [P, SEQ])
        key_sums = sb("key_sums", [P, SEQ])
        key_sums_hi = sb("key_sums_hi", [P, SEQ], F32R)
        key_sums_lo = sb("key_sums_lo", [P, SEQ], F32R)
        sums_T = sb("sums_T", [P, SEQ])
        denom = sb("denom", [P, TB])
        o_hi = sb("o_hi", [P, 2, SEQ], F32R)
        o_lo = sb("o_lo", [P, 2, SEQ], F32R)
        probs = sb("probs", [P, PCOLS])
        xrows = Region(sb.at)("xrows", [P, TB, D])
        wg_raw = sb("wg_raw", [P, KC, P])
        wg_hi = sb("wg_hi", [P, KC, P], F32R)
        wg_lo = sb("wg_lo", [P, KC, P], F32R)
        gateT = sb("gateT", [P, SEQ])
        p_hi = sb("p_hi", [P, PCOLS], F32R)
        p_lo = sb("p_lo", [P, PCOLS], F32R)
        q_hi, q_lo, k_hi, k_lo, v_hi, v_lo = (sb(n, [P, SEQ], F32R) for n in ("q_hi", "q_lo", "k_hi", "k_lo", "v_hi", "v_lo"))
        factor = sb("factor", [P, 2, TB])
        assert sb.at <= raw_at

        xs = [nc.dram_tensor(f"xs{part}", (XPART * P, D), F32, kind="Internal").ap() for part in range(PARTS)]
        xs_out = nc.dram_tensor("xs_out", (XTILES * P, D), F32, kind="Internal").ap()
        es = nc.dram_tensor("es", (ETILES * P, D), F32, kind="Internal").ap()
        es_out = nc.dram_tensor("es_out", (ETILES * P, D), F32, kind="Internal").ap()

        names = """x_loaded0 x_loaded1 x_loaded2 x_loaded3 const_ready ones_ready ones_r_ready ln_stats ln_aggr ln_eps ln_rstd xn_ready xnT_ready xnT_hi_done xnT_lo_done
        wg_loaded  wg_split gateT_ready gateT_copied gate_ready gate_exp gate_done
        wqkv_loaded wo_loaded w_hi wq_split wk_split wv_split wo_split
        q_ready k_ready vT_ready v_ready s_ready pv_ready sum_ready y_ready
        q_hi_done k_hi_done vT_done v_hi_done o_hi_done tanh_done exp_done
        q_lo_done k_lo_done v_lo_done p_hi_done p_lo_done o_lo_done den_done sums_T_done factor_done y_added masked sums_step sums_done sums_hi_done sums_lo_done stored
        ids_loaded router_loaded zeros_ready zero_filled0 zero_filled1 zero_filled2 zero_filled3 step prefix_ready prefix_read prefix_e_read chosen_ready route_x_done route_e_done
        ct_loaded0 ct_loaded1 ct_loaded2 ct_loaded3 ct_hi_done ct_lo_pool ct_lo_dve sh_loaded sh_hi sh_split
        scat0 scat1 scat2 scat3 gath0 gath1 gath2 gath3 gath4 gath5 gath6 gath7 x_added scat_e
        x3_T x3_copied logits_ready logits_read minus_max exp_router
        low_found up_loaded0 up_loaded1 down_loaded0 down_loaded1 up_hi up_lo down_hi down_lo combined
        """ + " ".join(f"{ph}_{n}" for ph in "xse" for n in ("xT_ready", "xT_hi", "xT_lo", "up", "silu", "act", "aT_ready", "aT_hi", "aT_lo", "y", "y_out"))
        names += " s_row " + " ".join(f"{ph}_{n}{j}" for ph in "xe" for n in ("row", "y_stored") for j in range(2))
        S = {n: sem(n) for n in names.split()}
        x_loaded = [S[f"x_loaded{b}"] for b in range(BATCH)]

        scat = [S[f"scat{i}"] for i in range(TB)]
        gath = [S[f"gath{i}"] for i in range(PT)]
        U = HEADS * BATCH
        XT, AT, YB = 4, 5, 7
        LOGITS_STEP, ROUTE_STEP = 4, 6
        BLOCK = 32
        NCH = {"x": KC, "s": SC, "e": IC}
        HALVES = {"x": 1, "s": 2, "e": 1}
        WIDTH = {"x": D, "s": INNER, "e": INNER}
        NSTEPS = {"x": XTILES, "s": TILES, "e": ETILES}

        def chunk(ph, c):
            total = HALVES[ph] * WIDTH[ph]
            return c * P, min(P, total - c * P)

        def by_twos(engine, step, start, stop):
            if start % 2:
                step(start // 2, 1)
                start += 1
            with engine.Fori(start // 2, stop // 2) as i:
                step(i, 0)
                step(i, 1)
            if stop % 2:
                step(stop // 2, 0)

        XN_BANKS = (2, 3, 4, 2)
        TAIL_BANKS = ((7, 0, 1, 4), (2, 3, 7, 0))

        block = ctx.enter_context(nc.Block())
        xv = x.rearrange("(t p) d -> p t d", p=P)
        ov = out.rearrange("(t p) d -> p t d", p=P)

        def ct_raw(e):
            of, at = (raw, e) if e < 2 else (ct_more, e - 2)
            return of[:, at * KC * D:(at + 1) * KC * D].rearrange("p (k n) -> p k n", k=KC)

        def triple(out_ap, a_hi, a_lo, b_hi, b_lo, first, last):
            nc.tensor.matmul(out_ap, a_hi, b_hi, start=first, stop=False)
            nc.tensor.matmul(out_ap, a_hi, b_lo, start=False, stop=False)
            return nc.tensor.matmul(out_ap, a_lo, b_hi, start=False, stop=last)

        def aT_parts(ph):
            return {"x": [(0, KC)], "s": [(0, KC), (KC, SC - 1), (SC - 1, SC)], "e": [(0, IC - 1), (IC - 1, IC)]}[ph]

        def aT_bank(ph, c0, c1, w):
            return bank[AT + c0 // KC][0:w, c0 % KC * P:(c0 % KC + c1 - c0) * P].rearrange("p (c n) -> p c n", n=P)

        @block.sync
        def _(sp):
            sp.dma_start(ids[:, :], token_ids).then_inc(S["ids_loaded"], 16)
            for b in range(BATCH):
                sp.dma_start(resid[:, TB * b:TB * b + TB, :], xv[:, TB * b:TB * b + TB, :]).then_inc(x_loaded[b], 16)
                if b == 0:
                    sp.dma_start(wg_raw[:, :, :], wgates).then_inc(S["wg_loaded"], 16)
                    sp.dma_start(wqkv_raw[:, :, :, :], wqkv[0]).then_inc(S["wqkv_loaded"], 16)
                    sp.dma_start(wo_raw[:, :], wo[0]).then_inc(S["wo_loaded"], 16)
            sp.dma_start(router_w[:, :, :], router).then_inc(S["router_loaded"], 16)
            sp.wait_ge(S["zeros_ready"], 1)
            for n, (rows_of, tiles) in enumerate(((xs[0], XPART), (xs[1], XPART), (es, ETILES))):
                sp.dma_start(rows_of.rearrange("(t p) d -> p t d", p=P), zeros[:, :].unsqueeze(1).to_broadcast([P, tiles, D])).then_inc(S[f"zero_filled{n}"], 16)
            with sp.Fori(1, HEADS) as h:
                sp.wait_ge(S["wv_split"], h)
                sp.dma_start(wqkv_raw[:, :, :, :], wqkv[bass.ds(h, 1)].rearrange("a p c k d -> p (a c) k d")).then_inc(S["wqkv_loaded"], 16)
                sp.wait_ge(S["wo_split"], h)
                sp.dma_start(wo_raw[:, :], wo[bass.ds(h, 1)].rearrange("a p d -> p (a d)")).then_inc(S["wo_loaded"], 16)
            sp.dma_start(es_out.rearrange("(t p) d -> p t d", p=P), zeros[:, :].unsqueeze(1).to_broadcast([P, ETILES, D])).then_inc(S["zero_filled3"], 16)
            sp.wait_ge(S["zero_filled0"], 16)
            sp.wait_ge(S["zero_filled1"], 16)
            sp.wait_ge(S["zero_filled2"], 16)
            sp.wait_ge(S["zero_filled3"], 16)
            sp.wait_ge(S["route_x_done"], 1)
            for e in range(TOKEN_EXPERTS):
                if e == 2:
                    sp.wait_ge(S["vT_ready"], U)
                sp.dma_start(ct_raw(e), ctxT[e]).then_inc(S[f"ct_loaded{e}"], 16)

            def load_row(ph, source, g, j):
                sp.dma_start(rows[:, j, :], source[bass.ds(g * P, P)]).then_inc(S[f"{ph}_row{j}"], 16)

            def store_y(ph, target, g, j):
                sp.wait_ge(S[f"{ph}_y_out"], g + 1)
                sp.dma_start(target[bass.ds(g * P, P)], rows[:, 2 + j, :]).then_inc(S[f"{ph}_y_stored{j}"], 16)

            def step(ph, source, target, i, j, first=False, load=True, source_at=0):
                g = 2 * i + j
                if load:
                    sp.wait_ge(S[f"{ph}_xT_ready"], g + 1)
                    load_row(ph, source, g + 2 - source_at, j)
                if not first:
                    store_y(ph, target, g - 1, 1 - j)

            def last_steps(ph, source, target):
                n = NSTEPS[ph]
                for g in (n - 2, n - 1):
                    step(ph, source, target, g // 2, g % 2, load=False)
                store_y(ph, target, n - 1, (n - 1) % 2)

            for i in range(TB):
                sp.wait_ge(scat[i], 16 * BATCH // PARTS)
            load_row("x", xs[0], 0, 0)
            load_row("x", xs[0], 1, 1)
            step("x", xs[0], xs_out, 0, 0, True)
            by_twos(sp, lambda i, j: step("x", xs[0], xs_out, i, j), 1, XPART - 2)
            for i in range(TB):
                sp.wait_ge(scat[i], 16 * BATCH)
            by_twos(sp, lambda i, j: step("x", xs[1], xs_out, i, j, source_at=XPART), XPART - 2, XTILES - 2)
            last_steps("x", xs[1], xs_out)

            sp.wait_ge(S["scat_e"], 16 * TOPK * TILES)
            sp.wait_ge(S["s_xT_ready"], TILES)
            load_row("e", es, 0, 0)
            load_row("e", es, 1, 1)
            e_step = lambda i, j, first=False: step("e", es, es_out, i, j, first)
            e_step(0, 0, True)
            by_twos(sp, e_step, 1, ETILES - 2)
            last_steps("e", es, es_out)
            for t in range(TILES):
                sp.wait_ge(S["combined"], TILES + t + 1)
                sp.dma_start(ov[:, t, :], resid[:, t, :]).then_inc(S["stored"], 16)
            sp.wait_ge(S["stored"], 16 * TILES)

        @block.gpsimd
        def _(pool):
            nc.gpsimd.memset(zeros[:, :], 0.0).then_inc(S["zeros_ready"], 1)
            nc.gpsimd.memset(ones[:, :], 1.0).then_inc(S["ones_ready"], 1)
            nc.gpsimd.memset(neghalf[:, :], -0.5)
            nc.gpsimd.memset(ident[:, :], 0.0).then_inc(S["const_ready"], 1)
            pool.wait_ge(S["const_ready"], 1)
            nc.gpsimd.affine_select(out=ident[:, :], in_=ident[:, :], compare_op=ALU.not_equal, fill=1.0, base=0,
                                    pattern=[[-1, P]], channel_multiplier=1).then_inc(S["const_ready"], 1)
            pool.wait_ge(S["ones_ready"], 1)
            nc.gpsimd.tensor_tensor(ones_r[:, :], ones[:, :], ones[:, :], ALU.mult).then_inc(S["ones_r_ready"], 1)
            nc.gpsimd.memset(causal[:, :, :], 1.0).then_inc(S["const_ready"], 1)
            pool.wait_ge(S["const_ready"], 3)
            nc.gpsimd.affine_select(out=causal[:, :, :], in_=causal[:, :, :], compare_op=ALU.is_ge, fill=0.0, base=0,
                                    pattern=[[0, 2], [1, P]], channel_multiplier=-1).then_inc(S["const_ready"], 1)

            nc.gpsimd.memset(earlier[:, :], 1.0).then_inc(S["const_ready"], 1)
            pool.wait_ge(S["const_ready"], 5)
            nc.gpsimd.affine_select(out=earlier[:, :], in_=earlier[:, :], compare_op=ALU.is_gt, fill=0.0, base=0,
                                    pattern=[[1, P]], channel_multiplier=-1).then_inc(S["const_ready"], 1)
            nc.gpsimd.iota(iota[:, :], [[1, ETILES]], base=0, channel_multiplier=0, allow_small_or_imprecise_dtypes=True).then_inc(S["const_ready"], 1)

            def low(raw, hi, lo, done, n):
                pool.wait_ge(S["w_hi"], n)
                nc.gpsimd.tensor_tensor(lo, raw, hi.bitcast(F32), ALU.subtract).then_inc(done, 1)

            def low_qkv(h, c, done):
                low(wqkv_raw[:, c, :, :], wqkv_hi[:, c, :, :], wqkv_lo[:, c, :, :], done, 4 * h + c + 2)

            def low_wo(h):
                low(wo_raw[:, :], wo_hi[:, :], wo_lo[:, :], S["wo_split"], 4 * h + 5)

            low(wg_raw[:, :, :], wg_hi[:, :, :], wg_lo[:, :, :], S["wg_split"], 1)
            def rsqrt(n):
                pool.wait_ge(S["ln_eps"], n + 1)
                nc.gpsimd.tensor_tensor(rstd[:, :], vareps[:, :], neghalf[:, :], ALU.pow).then_inc(S["ln_rstd"], 1)

            rsqrt(0)
            low_qkv(0, 0, S["wq_split"])
            low_qkv(0, 1, S["wk_split"])
            low_qkv(0, 2, S["wv_split"])
            low_wo(0)

            def mask(u):
                pool.wait_ge(S["exp_done"], u + 1)
                for diagonal in (probs[:, 0:2 * SEQ].rearrange("p (a c) -> p a c", a=2)[:, :, 0:P],
                                 probs[:, POFF[3]:POFF[3] + 2 * P].rearrange("p (a c) -> p a c", a=2)):
                    nc.gpsimd.tensor_tensor(diagonal, diagonal, causal[:, :, :], ALU.mult).then_inc(S["masked"], 1)

            def sum_keys(u):
                pool.wait_ge(S["masked"], 2 * u + 2)
                nc.gpsimd.tensor_tensor(key_sums[:, P:], probs[:, P:SEQ], probs[:, POFF[1]:POFF[1] + SEQ - P], ALU.add).then_inc(S["sums_step"], 1)
                pool.wait_ge(S["sums_step"], 2 * u + 1)
                nc.gpsimd.tensor_tensor(key_sums[:, 2 * P:], key_sums[:, 2 * P:], probs[:, POFF[2]:POFF[2] + 2 * P], ALU.add).then_inc(S["sums_step"], 1)
                pool.wait_ge(S["sums_step"], 2 * u + 2)
                nc.gpsimd.tensor_tensor(key_sums[:, 3 * P:], key_sums[:, 3 * P:], probs[:, POFF[3]:POFF[3] + P], ALU.add).then_inc(S["sums_done"], 1)
                pool.wait_ge(S["sums_done"], u + 1)
                for source, to in ((probs, slice(0, P)), (key_sums, slice(P, SEQ))):
                    nc.gpsimd.tensor_tensor(key_sums_hi[:, to], source[:, to], ones[:, 0:1].to_broadcast([P, to.stop - to.start]), ALU.mult).then_inc(S["sums_hi_done"], 1)
                pool.wait_ge(S["sums_hi_done"], 2 * u + 2)
                for source, to in ((probs, slice(0, P)), (key_sums, slice(P, SEQ))):
                    nc.gpsimd.tensor_tensor(key_sums_lo[:, to], source[:, to], key_sums_hi[:, to].bitcast(F32), ALU.subtract).then_inc(S["sums_lo_done"], 1)

            def head(h, first, last):
                for b in range(BATCH):
                    u = BATCH * h + b
                    if first and b + 1 < BATCH:
                        rsqrt(b + 1)
                    if not (first and b == 0):
                        if not (first and b == 1):
                            pool.wait_ge(S["sum_ready"], u - 1)
                        mask(u - 1)
                        sum_keys(u - 1)
                    if b == 1 and not first:
                        low_wo(h)
                    if b == BATCH - 1 and not last:
                        for c, done in enumerate(("wq_split", "wk_split", "wv_split")):
                            low_qkv(h + 1, c, S[done])

            def scatter_x(b):
                for i in range(TB):
                    pool.wait_ge(S["xn_ready"], TILES + TB * b + i + 1)
                    nc.gpsimd.indirect_dma_start(xs[b * PARTS // BATCH], bass.IndirectOffsetOnAxis(slot_part[:, TB * b + i:TB * b + i + 1], 0), xrows[:, i, :], None).then_inc(scat[i], 16)

            pool.wait_ge(S["const_ready"], 4)
            head(0, True, False)
            with pool.Fori(1, HEADS - 1) as h:
                head(h, False, False)
            head(HEADS - 1, False, True)

            for part in range(PARTS):
                pool.wait_ge(S[f"zero_filled{part}"], 16)
            pool.wait_ge(S["route_x_done"], 1)
            rsqrt(BATCH)
            scatter_x(0)
            mask(U - 1)
            rsqrt(BATCH + 1)
            pool.wait_ge(S["sum_ready"], U - 1)
            sum_keys(U - 1)
            scatter_x(1)
            pool.wait_ge(S["ct_hi_done"], 1)
            nc.gpsimd.tensor_tensor(ct_lo[:, 0], ct_raw(0), ct_hi[:, 0].bitcast(F32), ALU.subtract).then_inc(S["ct_lo_pool"], 1)
            for b in range(2, BATCH):
                rsqrt(BATCH + b)
                scatter_x(b)

            def split(raw, hi, lo, hi_done, n, done):
                nc.gpsimd.tensor_tensor(hi, raw, ones[:, 0:1].to_broadcast([P, raw.shape[1]]), ALU.mult).then_inc(hi_done, 1)
                pool.wait_ge(hi_done, n)
                nc.gpsimd.tensor_tensor(lo, raw, hi.bitcast(F32), ALU.subtract).then_inc(done, 1)

            pool.wait_ge(S["ct_lo_pool"], 1)
            pool.wait_ge(S["ct_lo_dve"], TOKEN_EXPERTS - 1)
            pool.wait_ge(S["y_added"], U * TB)
            for i in range(TB):
                pool.wait_ge(scat[i], 16 * BATCH)
            for c, (source, hi, lo) in enumerate(((sh_up[:, 0:2, :], sh_up_hi[:, 0:2], sh_up_lo[:, 0:2]), (sh_up[:, 2:4, :], sh_up_hi[:, 2:4], sh_up_lo[:, 2:4]), (sh_down, sh_down_hi[:, :], sh_down_lo[:, :]))):
                piece = raw[:, 0:hi.shape[1] * hi.shape[2]]
                if c:
                    pool.wait_ge(S["sh_split"], c)
                nc.gpsimd.dma_start(piece.rearrange("p (k n) -> p k n", k=hi.shape[1]), source).then_inc(S["sh_loaded"], 16)
                pool.wait_ge(S["sh_loaded"], 16 * c + 16)
                hi, lo = (a.rearrange("p k n -> p (k n)") for a in (hi, lo))
                split(piece, hi, lo, S["sh_hi"], c + 1, S["sh_split"])

            pool.wait_ge(S["sh_split"], 3)
            for part in range(PARTS):
                tiles = XPART * (part + 1)
                for j in range(2):
                    pool.wait_ge(S[f"x_y_stored{j}"], 16 * ((tiles + 1 - j) // 2))
                for i in range(PT):
                    t = PT * part + i
                    nc.gpsimd.indirect_dma_start(x3(t), None, xs_out[0:tiles * P, :], bass.IndirectOffsetOnAxis(slot_x[:, t:t + 1], 0)).then_inc(gath[i], 16)
                for b in range(BATCH // PARTS):
                    rsqrt(2 * BATCH + BATCH // PARTS * part + b)

            def load_weights(e, p):
                to = (raw, raw_odd)[p]
                nc.gpsimd.dma_start(up_of(to[:, 0:UP]), exp_up[bass.ds(e, 1)].rearrange("e p k n -> p (e k) n")).then_inc(S[f"up_loaded{p}"], 16)
                nc.gpsimd.dma_start(down_of(to[:, UP:]), exp_down[bass.ds(e, 1)].rearrange("e p k n -> p (e k) n")).then_inc(S[f"down_loaded{p}"], 16)

            def split_weights(i, p, wait=True):
                e = 2 * i + p
                if wait:
                    tiles_before = pool.value_load(expert_end[0:1, bass.ds(e - 2, 1)], min_val=0, max_val=ETILES)
                source = (raw, raw_odd)[p]
                for part, used, lo, hi in (("up", "e_xT_ready", 0, UP), ("down", "e_aT_ready", UP, UP + DOWN)):
                    pool.wait_ge(S[f"{part}_loaded{p}"], 16 * i + 16)
                    if wait:
                        pool.wait_ge(S[used], tiles_before + 1)
                    split(source[:, lo:hi], expert_w[:, p, 2 * lo:lo + hi], expert_w[:, p, lo + hi:2 * hi], S[f"{part}_hi"], e + 1, S[f"{part}_lo"])

            def next_weights(e, p):
                pool.wait_ge(S["down_lo"], e + 1)
                load_weights(e + 2, p)

            pool.wait_ge(S["zero_filled2"], 16)
            pool.wait_ge(S["route_e_done"], 1)
            for t in range(TILES):
                for c in range(TOPK):
                    nc.gpsimd.indirect_dma_start(es, bass.IndirectOffsetOnAxis(slot_e[c][:, t:t + 1], 0), x3(t), None).then_inc(S["scat_e"], 16)
            pool.wait_ge(S["scat_e"], 16 * TOPK * TILES)
            pool.wait_ge(S["s_row"], PT)
            load_weights(0, 0)
            split_weights(0, 0, False)
            pool.wait_ge(S["s_y"], TILES)
            load_weights(1, 1)
            next_weights(0, 0)
            split_weights(0, 1, False)
            next_weights(1, 1)
            with pool.Fori(1, EXPERTS // 2 - 1) as i:
                for p in range(2):
                    split_weights(i, p)
                    next_weights(2 * i + p, p)
            for p in range(2):
                split_weights(EXPERTS // 2 - 1, p)

            stored = [pool.value_load(low_stored[0:1, j:j + 1], min_val=16, max_val=16 * len(range(j, ETILES, 2))) for j in range(2)]
            for j in range(2):
                pool.wait_ge(S["zero_filled3"], 16)
                pool.wait_ge(S[f"e_y_stored{j}"], stored[j])
            for t in range(TILES):
                nc.gpsimd.indirect_dma_start(low_rows[:, t, :], None, es_out, bass.IndirectOffsetOnAxis(slot_e[0][:, t:t + 1], 0)).then_inc(S["low_found"], 16)
            for j in range(2):
                pool.wait_ge(S[f"e_y_stored{j}"], 16 * ((ETILES + 1 - j) // 2))
            for t in range(TILES):
                if t >= PT:
                    pool.wait_ge(S["combined"], TILES + t - PT + 1)
                nc.gpsimd.indirect_dma_start(high_rows[:, t % PT, :], None, es_out, bass.IndirectOffsetOnAxis(slot_e[1][:, t:t + 1], 0)).then_inc(gath[t % PT], 16)

        @block.scalar
        def _(act):
            def high(hi, raw):
                nc.scalar.activation(hi, raw, ACT.Copy).then_inc(S["w_hi"], 1)

            act.wait_ge(S["wg_loaded"], 16)
            high(wg_hi[:, :, :], wg_raw[:, :, :])
            act.wait_ge(S["wqkv_loaded"], 16)
            for c in range(3):
                high(wqkv_hi[:, c, :, :], wqkv_raw[:, c, :, :])
            act.wait_ge(S["wo_loaded"], 16)
            high(wo_hi[:, :], wo_raw[:, :])
            def xnT_high(t):
                act.wait_ge(S["xnT_ready"], t + 1)
                nc.scalar.activation(xnT_hi[:, :, t * P:t * P + P], bank[XN_BANKS[t % TB]][:, :].rearrange("p (k n) -> p k n", k=KC), ACT.Copy).then_inc(S["xnT_hi_done"], 1)

            for t in range(TB):
                xnT_high(t)

            def gate_copy(b):
                act.wait_ge(S["gateT_ready"], b + 1)
                if b:
                    act.wait_ge(S["gate_ready"], b)
                nc.scalar.activation(gateT[:, :], bank[5][:, :], ACT.Copy).then_inc(S["gateT_copied"], 1)

            def gate_exp(b):
                act.wait_ge(S["gate_ready"], b + 1)
                nc.scalar.activation(gate_den[:, TB * b:TB * b + TB, :],
                                     bank[6][:, :].rearrange("p (t h) -> p t h", t=TB)[:, :, 0:HEADS], ACT.Exp, scale=-1.0).then_inc(S["gate_exp"], 1)

            def softmax_part(u, first):
                if not first:
                    act.wait_ge(S["p_lo_done"], u)
                    act.wait_ge(S["sums_lo_done"], 2 * u)
                act.wait_ge(S["s_ready"], u + 1)
                for i, (lo, n) in enumerate(((0, SEQ), (SEQ, SEQ), (2 * SEQ, 2 * P))):
                    nc.scalar.activation(probs[:, lo:lo + n], bank[2 + i][:, 0:n], ACT.Tanh, scale=SCALE / SOFTCAP).then_inc(S["tanh_done"], 1)
                act.wait_ge(S["tanh_done"], 3 * u + 3)
                nc.scalar.activation(probs[:, :], probs[:, :], ACT.Exp, scale=SOFTCAP).then_inc(S["exp_done"], 1)

            def o_part(u, b, early):
                act.wait_ge(S["pv_ready"], u + 1)
                if not early:
                    act.wait_ge(S["y_ready"], TB * (u - 1))
                nc.scalar.activation(o_hi[:, b % 2, :], bank[5][:, :], ACT.Copy).then_inc(S["o_hi_done"], 1)

            def high_qkv(h, c, u, ready):
                act.wait_ge(S["wqkv_loaded"], 16 * h + 32)
                act.wait_ge(S[ready], u + 1)
                high(wqkv_hi[:, c, :, :], wqkv_raw[:, c, :, :])

            def ct_high(e):
                act.wait_ge(S[f"ct_loaded{e}"], 16)
                if e == 0:
                    act.wait_ge(S["vT_ready"], U)
                nc.scalar.activation(ct_hi[:, e], ct_raw(e), ACT.Copy).then_inc(S["ct_hi_done"], 1)

            def head(h, first, last):
                for b in range(BATCH):
                    u = BATCH * h + b
                    start = first and b == 0
                    refresh = b == BATCH - 1 and not last
                    if not start:
                        softmax_part(u - 1, first and b == 1)
                    act.wait_ge(S["q_ready"], u + 1)
                    if not start:
                        act.wait_ge(S["s_ready"], u)
                    nc.scalar.activation(q_hi[:, :], bank[0][:, :], ACT.Copy).then_inc(S["q_hi_done"], 1)
                    if first:
                        gate_copy(b)
                    act.wait_ge(S["k_ready"], u + 1)
                    nc.scalar.activation(k_hi[:, :], bank[1][:, :], ACT.Copy).then_inc(S["k_hi_done"], 1)
                    if first and b + 1 < BATCH:
                        xnT_high(TB * b + TB)
                        xnT_high(TB * b + TB + 1)
                    if first:
                        gate_exp(b)
                    if refresh:
                        high_qkv(h, 0, u, "q_ready")
                    act.wait_ge(S["vT_ready"], u + 1)
                    if not start:
                        act.wait_ge(S["v_ready"], u)
                    nc.scalar.activation(vT[:, :], bank[0][:, :], ACT.Copy).then_inc(S["vT_done"], 1)
                    if first and b + 1 < BATCH:
                        xnT_high(TB * b + TB + 2)
                        xnT_high(TB * b + TB + 3)
                    if refresh:
                        high_qkv(h, 1, u, "k_ready")
                    if not start:
                        o_part(u - 1, b + 1, first and b < 3)
                    if refresh:
                        high_qkv(h, 2, u, "vT_ready")
                    if last and b == BATCH - 1:
                        ct_high(0)
                        ct_high(1)
                    act.wait_ge(S["v_ready"], u + 1)
                    if not start:
                        act.wait_ge(S["pv_ready"], u)
                    nc.scalar.activation(v_hi[:, :], bank[1][:, :], ACT.Copy).then_inc(S["v_hi_done"], 1)
                    if b == 1 and not first:
                        act.wait_ge(S["wo_loaded"], 16 * h + 16)
                        act.wait_ge(S["y_ready"], TB * BATCH * h)
                        high(wo_hi[:, :], wo_raw[:, :])

            head(0, True, False)
            with act.Fori(1, HEADS - 1) as h:
                head(h, False, False)
            head(HEADS - 1, False, True)
            softmax_part(U - 1, False)
            ct_high(2)
            ct_high(3)
            o_part(U - 1, 1, False)

            def xT_high(ph, g):
                act.wait_ge(S[f"{ph}_xT_ready"], g + 1)
                nc.scalar.activation(xT_hi[:, :, :], bank[XT][:, :].rearrange("p (k n) -> p k n", k=KC), ACT.Copy).then_inc(S[f"{ph}_xT_hi"], 1)

            def y_copy(ph, i, j, wait=True):
                act.wait_ge(S[f"{ph}_y"], 2 * i + j + 1)
                if wait:
                    act.wait_ge(S[f"{ph}_y_stored{j}"], 16 * i)
                nc.scalar.activation(rows[:, 2 + j, :], bank[YB][:, :], ACT.Copy).then_inc(S[f"{ph}_y_out"], 1)

            def aT_high(ph, g):
                act.wait_ge(S[f"{ph}_aT_ready"], g + 1)
                for c0, c1 in aT_parts(ph):
                    w = chunk(ph, c0)[1]
                    nc.scalar.activation(aT_hi[0:w, c0:c1, :], aT_bank(ph, c0, c1, w), ACT.Copy).then_inc(S[f"{ph}_aT_hi"], 1)

            def step(ph, i, j, first=False, last=False, wait=True):
                g = 2 * i + j
                W, H = WIDTH[ph], HALVES[ph]
                act.wait_ge(S[f"{ph}_up"], g + 1)
                if not first:
                    act.wait_ge(S[f"{ph}_aT_ready"], g)
                for half in range(H):
                    nc.scalar.activation(act_sb[:, half * W:half * W + W], bank[2 * half][:, 0:W], ACT.Silu).then_inc(S[f"{ph}_silu"], 1)
                if not last:
                    xT_high(ph, g + 1)
                if not first and ph != "s":
                    y_copy(ph, i - 1 + j, 1 - j, wait)
                if ph == "s" and not first:
                    act.wait_ge(S["s_y"], g)
                aT_high(ph, g)

            def feed_forward(ph):
                n = NSTEPS[ph]
                xT_high(ph, 0)
                step(ph, 0, 0, first=True)
                step(ph, 0, 1, wait=False)
                step(ph, 1, 0, wait=False)
                by_twos(act, lambda i, j: step(ph, i, j), 3, n - 1)
                step(ph, (n - 1) // 2, (n - 1) % 2, last=True)
                y_copy(ph, (n - 1) // 2, (n - 1) % 2)

            feed_forward("x")

            def copy_x3T(part):
                for t in range(PT * part, PT * part + PT):
                    act.wait_ge(S["x3_T"], t + 1)
                    if t >= 2:
                        act.wait_ge(S["logits_ready"], t - 1)
                    nc.scalar.activation(x3T[:, t % 2, :], bank[t % 2][:, :], ACT.Copy).then_inc(S["x3_copied"], 1)

            copy_x3T(0)
            xT_high("s", 0)
            step("s", 0, 0, first=True)
            by_twos(act, lambda i, j: step("s", i, j), 1, LOGITS_STEP)
            copy_x3T(1)
            step("s", LOGITS_STEP // 2, 0)
            act.wait_ge(S["minus_max"], 1)
            nc.scalar.activation(logits[:, :], logits[:, :], ACT.Exp).then_inc(S["exp_router"], 1)
            by_twos(act, lambda i, j: step("s", i, j), LOGITS_STEP + 1, TILES - 1)
            step("s", TILES // 2 - 1, 1, last=True)
            act.wait_ge(S["s_y"], TILES)
            feed_forward("e")

        @block.vector
        def _(dve):
            def ln_stats(n, b, i):
                nc.vector.bn_stats(stats[:, i, :], resid[:, TB * b + i, :]).then_inc(S["ln_stats"], 1)

            def ln_eps(n):
                for i in range(TB):
                    dve.wait_ge(S["ln_stats"], TB * n + i + 1)
                    nc.vector.bn_aggr(meanvar[:, i, :], stats[:, i, :]).then_inc(S["ln_aggr"], 1)
                dve.wait_ge(S["ln_aggr"], TB * n + TB)
                nc.vector.tensor_scalar(vareps[:, :], meanvar[:, :, 1], EPS, None, ALU.add).then_inc(S["ln_eps"], 1)

            def ln_apply(n, b, target, free):
                dve.wait_ge(S["ln_rstd"], n + 1)
                for i in range(TB):
                    free(i)
                    nc.vector.tensor_scalar(target(i), resid[:, TB * b + i, :], meanvar[:, i, 0:1], rstd[:, i:i + 1],
                                            ALU.subtract, ALU.mult).then_inc(S["xn_ready"], 1)

            steps = [0]

            def link(instruction):
                steps[0] += 1
                instruction.then_inc(S["step"], 1)
                dve.wait_ge(S["step"], steps[0])

            def count(w, prefix, prefix_done):
                n = NE
                running, ahead, restart = w.running, w.ahead, w.restart
                by = lambda a: a[:, 0:n].rearrange("p (e t) -> p e t", e=EXPERTS)
                link(nc.vector.memset(restart[:, 0:n], 1.0))
                link(nc.vector.memset(by(restart)[:, :, 0], 0.0))
                link(nc.vector.tensor_tensor_scan(running[:, 0:n], restart[:, 0:n], prefix[:, n:2 * n], 0.0, ALU.mult, ALU.add))
                link(nc.vector.tensor_tensor(ahead[:, 0:n], running[:, 0:n], prefix[:, n:2 * n], ALU.subtract))
                nc.vector.tensor_tensor(ahead[:, 0:n], ahead[:, 0:n], prefix[:, 0:n], ALU.add).then_inc(prefix_done, 1)

            def route(w, tiles, choices, prefix_done, tile_expert, part_end=None):
                experts, n = EXPERTS, NE
                running, ahead, places, above = w.running, w.ahead, w.places, w.above
                tile_of, tile_f, slot_f, full, upto, base = w.tile_of, w.tile_f, w.slot_f, w.full, w.upto, w.base
                by = lambda a: a[:, 0:n].rearrange("p (e t) -> p e t", e=experts)
                link(nc.vector.tensor_scalar(places[:, 0:TILES], iota[:, 0:TILES], float(P), None, ALU.mult))
                link(nc.vector.tensor_tensor(by(above), by(running)[:, :, TILES - 1].unsqueeze(2).to_broadcast([P, experts, TILES]),
                                             places[:, 0:TILES].unsqueeze(1).to_broadcast([P, experts, TILES]), ALU.is_gt))
                link(nc.vector.tensor_reduce(full[:, 0:experts], by(above), mybir.AxisListType.X, ALU.add))
                if not part_end:
                    link(nc.vector.tensor_scalar(full[:, :], full[:, :], 1.0, None, ALU.max))
                link(nc.vector.tensor_tensor_scan(upto[:, 0:experts], ones[:, 0:experts], full[:, 0:experts], 0.0, ALU.mult, ALU.add))
                if part_end:
                    last = slice(experts // 2 - 1, experts // 2)
                    link(nc.vector.tensor_scalar(base[:, last], upto[:, last], -1.0, float(part_end), ALU.mult, ALU.add))
                    link(nc.vector.tensor_tensor(full[:, last], full[:, last], base[:, last], ALU.add))
                    link(nc.vector.tensor_tensor_scan(upto[:, 0:experts], ones[:, 0:experts], full[:, 0:experts], 0.0, ALU.mult, ALU.add))
                link(nc.vector.tensor_tensor(base[:, 0:experts], upto[:, 0:experts], full[:, 0:experts], ALU.subtract))
                link(nc.vector.tensor_scalar(base[:, 0:experts], base[:, 0:experts], float(P), None, ALU.mult))
                dve.wait_ge(prefix_done, 1)
                link(nc.vector.tensor_tensor(by(places), by(ahead), base[:, 0:experts].unsqueeze(2).to_broadcast([P, experts, TILES]), ALU.add))
                for one, slot in choices:
                    link(nc.vector.tensor_tensor(above[:, 0:n], places[:, 0:n], one[:, 0:n], ALU.mult))
                    link(nc.vector.tensor_reduce(slot_f[:, :], above[:, 0:n].rearrange("p (e t) -> p t e", e=experts), mybir.AxisListType.X, ALU.add))
                    link(nc.vector.tensor_copy(slot[:, :], slot_f[:, :]))
                owners = tile_of[:, 0:tiles, 0:experts - 1]
                link(nc.vector.tensor_tensor(owners, iota[:, 0:tiles].unsqueeze(2).to_broadcast([P, tiles, experts - 1]),
                                             upto[:, 0:experts - 1].unsqueeze(1).to_broadcast([P, tiles, experts - 1]), ALU.is_ge))
                link(nc.vector.tensor_reduce(tile_f[:, 0:tiles], owners, mybir.AxisListType.X, ALU.add))
                return nc.vector.tensor_copy(tile_expert[:, :], tile_f[:, 0:tiles])

            def free_xn(b):
                return lambda i: dve.wait_ge(S["xnT_ready"], TB * (b - 1) + i + 1) if b else None

            dve.wait_ge(S["ids_loaded"], 16)
            dve.wait_ge(S["const_ready"], 7)
            link(nc.vector.memset(ids_ge[:, 0, :], 1.0))
            link(nc.vector.memset(ids_ge[:, TOKEN_EXPERTS, :], 0.0))
            for e in range(1, TOKEN_EXPERTS):
                link(nc.vector.tensor_scalar(ids_ge[:, e, :], ids[:, :], float(e * IDS_PER_EXPERT), None, ALU.is_ge))
            link(nc.vector.memset(by_id.chosen[:, :], 0.0))
            for part in range(PARTS):
                of = slice(PT * part, PT * part + PT)
                chosen = by_id.chosen[:, :].rearrange("p (e t) -> p e t", t=TILES)[:, TOKEN_EXPERTS * part:TOKEN_EXPERTS * (part + 1), of]
                done = nc.vector.tensor_tensor(chosen, ids_ge[:, 0:TOKEN_EXPERTS, of], ids_ge[:, 1:, of], ALU.subtract)
            done.then_inc(S["chosen_ready"], 1)
            dve.wait_ge(S["prefix_ready"], 1)
            count(by_id, bank[7], S["prefix_read"])

            def route_x():
                link(route(by_id, XTILES, [(by_id.chosen, slot_x)], S["prefix_read"], expert_x, part_end=XPART))
                link(nc.vector.tensor_copy(slot_part[:, 0:PT], by_id.slot_f[:, 0:PT]))
                link(nc.vector.tensor_scalar(slot_part[:, PT:], by_id.slot_f[:, PT:], float(-XPART * P), None, ALU.add))
                nc.vector.tensor_scalar(expert_x[:, XPART:], by_id.tile_f[:, XPART:XTILES], float(-TOKEN_EXPERTS), None, ALU.add).then_inc(S["route_x_done"], 1)

            def ln_stats_in(b):
                dve.wait_ge(x_loaded[b], 16)
                for i in range(TB):
                    ln_stats(b, b, i)
                ln_eps(b)

            def ln_apply_in(b):
                ln_apply(b, b, lambda i: xn[:, i, :], free_xn(b))

            def xnT_low(t):
                cols = slice(t * P, t * P + P)
                dve.wait_ge(S["xnT_hi_done"], t + 1)
                nc.vector.tensor_tensor(xnT_lo[:, :, cols], bank[XN_BANKS[t % TB]][:, :].rearrange("p (k n) -> p k n", k=KC),
                                        xnT_hi[:, :, cols].bitcast(F32), ALU.subtract).then_inc(S["xnT_lo_done"], 1)

            ln_stats_in(0)
            ln_apply_in(0)
            for t in range(TB):
                xnT_low(t)

            def lo_part(lo, ps, hi, hi_done, done, u):
                dve.wait_ge(S[hi_done], u + 1)
                nc.vector.tensor_tensor(lo, ps, hi.bitcast(F32), ALU.subtract).then_inc(S[done], 1)

            def y_add(u, b, i, of=7):
                dve.wait_ge(S["y_ready"], TB * u + i + 1)
                row = resid[:, TB * b + i, :]
                nc.vector.scalar_tensor_tensor(out=row, in0=bank[of][:, :], scalar=factor[:, b % 2, i:i + 1], in1=row,
                                               op0=ALU.mult, op1=ALU.add).then_inc(S["y_added"], 1)

            def p_part(u, first):
                if not first:
                    dve.wait_ge(S["pv_ready"], u)
                dve.wait_ge(S["masked"], 2 * u + 2)
                nc.vector.tensor_copy(p_hi[:, :], probs[:, :]).then_inc(S["p_hi_done"], 1)
                dve.wait_ge(S["p_hi_done"], u + 1)
                nc.vector.tensor_tensor(p_lo[:, :], probs[:, :], p_hi[:, :].bitcast(F32), ALU.subtract).then_inc(S["p_lo_done"], 1)

            def o_low(u, b):
                lo_part(o_lo[:, b % 2, :], bank[5][:, :], o_hi[:, b % 2, :], "o_hi_done", "o_lo_done", u)

            def y_factors(u, h, b):
                dve.wait_ge(S["sum_ready"], u + 1)
                nc.vector.transpose(sums_T[:, :], bank[6][:, :]).then_inc(S["sums_T_done"], 1)
                dve.wait_ge(S["sums_T_done"], u + 1)
                for q in range(P // BLOCK):
                    of = slice(q * BLOCK, q * BLOCK + BLOCK)
                    nc.vector.tensor_tensor(denom[of, :], sums_T[of, :].rearrange("p (t q c) -> p t q c", t=TB, c=BLOCK)[:, :, q, 0],
                                            gate_den[of, TB * b:TB * b + TB, bass.ds(h, 1)].rearrange("p t a -> p (t a)"), ALU.mult).then_inc(S["den_done"], 1)
                dve.wait_ge(S["den_done"], P // BLOCK * (u + 1))
                nc.vector.reciprocal(factor[:, b % 2, :], denom[:, :]).then_inc(S["factor_done"], 1)

            def ln_apply_x(b):
                def free(i):
                    if b:
                        dve.wait_ge(scat[i], 16 * b)
                ln_apply(BATCH + b, b, lambda i: xrows[:, i, :], free)

            def head(h, first, last=False):
                for b in range(BATCH):
                    u = BATCH * h + b
                    norm = last and b == BATCH - 1
                    start = first and b == 0
                    adds = not (first and b < 2)
                    b2 = (b + 2) % BATCH
                    ahead = first and b + 1 < BATCH
                    if ahead:
                        ln_stats_in(b + 1)
                    if adds:
                        dve.wait_ge(S["factor_done"], u - 1)
                        y_add(u - 2, b2, 0)
                    if norm:
                        dve.wait_ge(S["y_added"], TB * (U - BATCH + 1))
                        ln_stats(BATCH, 0, 0)
                    lo_part(q_lo[:, :], bank[0][:, :], q_hi[:, :], "q_hi_done", "q_lo_done", u)
                    if ahead:
                        ln_apply_in(b + 1)
                    if not start:
                        p_part(u - 1, first and b == 1)
                    if adds:
                        y_add(u - 2, b2, 1)
                    if norm:
                        ln_stats(BATCH, 0, 1)
                    if first and b == BATCH - 1:
                        route_x()
                    lo_part(k_lo[:, :], bank[1][:, :], k_hi[:, :], "k_hi_done", "k_lo_done", u)
                    if ahead:
                        xnT_low(TB * b + TB)
                        xnT_low(TB * b + TB + 1)
                    if adds:
                        y_add(u - 2, b2, 2)
                    if first:
                        dve.wait_ge(S["gate_exp"], b + 1)
                        of = gate_den[:, TB * b:TB * b + TB, :]
                        nc.vector.tensor_scalar(of, of, 1.0, None, ALU.add).then_inc(S["gate_done"], 1)
                        dve.wait_ge(S["gate_done"], b + 1)
                    if ahead:
                        xnT_low(TB * b + TB + 2)
                        xnT_low(TB * b + TB + 3)
                    if norm:
                        ln_stats(BATCH, 0, 2)
                        ln_stats(BATCH, 0, 3)
                        ln_eps(BATCH)
                    if not start:
                        o_low(u - 1, (b - 1) % BATCH)
                        y_factors(u - 1, h if b else h - 1, (b - 1) % BATCH)
                    if adds:
                        y_add(u - 2, b2, 3)
                    if norm:
                        ln_apply_x(0)
                    lo_part(v_lo[:, :], bank[1][:, :], v_hi[:, :], "v_hi_done", "v_lo_done", u)

            head(0, True)
            with dve.Fori(1, HEADS - 1) as h:
                head(h, False)
            head(HEADS - 1, False, True)

            def ln_stats_x(b):
                dve.wait_ge(S["y_added"], TB * (U - BATCH + b + 1))
                for i in range(TB):
                    ln_stats(BATCH + b, b, i)
                ln_eps(BATCH + b)

            def ct_low(e):
                dve.wait_ge(S["ct_hi_done"], e + 1)
                nc.vector.tensor_tensor(ct_lo[:, e], ct_raw(e), ct_hi[:, e].bitcast(F32), ALU.subtract).then_inc(S["ct_lo_dve"], 1)

            ln_stats_x(1)
            p_part(U - 1, False)
            ct_low(1)
            ln_apply_x(1)
            dve.wait_ge(S["factor_done"], U - 1)
            for i in range(2):
                y_add(U - 2, BATCH - 2, i, TAIL_BANKS[0][i])
            o_low(U - 1, BATCH - 1)
            for i in range(2, TB):
                y_add(U - 2, BATCH - 2, i, TAIL_BANKS[0][i])
            ct_low(2)
            y_factors(U - 1, HEADS - 1, BATCH - 1)
            dve.wait_ge(S["factor_done"], U)
            for i in range(TB):
                y_add(U - 1, BATCH - 1, i, TAIL_BANKS[1][i])
            ct_low(3)

            def weights_split(split, g):
                e = dve.value_load(expert_e[0:1, bass.ds(g, 1)], min_val=0, max_val=EXPERTS - 1)
                dve.wait_ge(S[split], e + 1)

            def xT_low(ph, g):
                if ph == "e":
                    weights_split("up_lo", g)
                dve.wait_ge(S[f"{ph}_xT_hi"], g + 1)
                nc.vector.tensor_tensor(xT_lo[:, :, :], bank[XT][:, :].rearrange("p (k n) -> p k n", k=KC), xT_hi[:, :, :].bitcast(F32), ALU.subtract).then_inc(S[f"{ph}_xT_lo"], 1)

            def copy_row(t, j):
                source = x3(t) if isinstance(t, int) else x3_late[:, bass.ds(t - PT, 1), :].rearrange("p a d -> p (a d)")
                nc.vector.tensor_copy(rows[:, j, :], source).then_inc(S["s_row"], 1)

            def shared_add(t):
                dve.wait_ge(S["s_y"], t + 1)
                row = resid[:, bass.ds(t, 1), :].rearrange("p a d -> p (a d)")
                nc.vector.tensor_tensor(row, bank[YB][:, :], row, ALU.add).then_inc(S["s_y_out"], 1)

            def step(ph, g, j=0, first=False, last=False, rows_left=True):
                W, H = WIDTH[ph], HALVES[ph]
                for i in range(H):
                    dve.wait_ge(S[f"{ph}_silu"], H * g + i + 1)
                    part = act_sb[:, i * W:i * W + W]
                    nc.vector.tensor_tensor(part, part, bank[2 * i + (ph != "x")][:, 0:W], ALU.mult).then_inc(S[f"{ph}_act"], 1)
                if not last:
                    xT_low(ph, g + 1)
                    if ph == "s" and rows_left:
                        copy_row(g + 2, j)
                if ph == "s" and not first:
                    shared_add(g - 1)
                if ph == "e":
                    weights_split("down_lo", g)
                parts = aT_parts(ph)
                for c0, c1 in parts:
                    w = chunk(ph, c0)[1]
                    read = sum(p[0] // KC <= c0 // KC for p in parts)
                    dve.wait_ge(S[f"{ph}_aT_hi"], len(parts) * g + read)
                    nc.vector.tensor_tensor(aT_lo[0:w, c0:c1, :], aT_bank(ph, c0, c1, w), aT_hi[0:w, c0:c1, :].bitcast(F32), ALU.subtract).then_inc(S[f"{ph}_aT_lo"], 1)

            def add_x(t):
                dve.wait_ge(gath[t % PT], 16 * (t // PT) + 16)
                row = resid[:, t, :]
                nc.vector.tensor_tensor(row, row, x3(t), ALU.add).then_inc(S["x_added"], 1)

            def stats_3(t):
                dve.wait_ge(S["x_added"], t + 1)
                ln_stats(2 * BATCH + t // TB, t // TB, t % TB)
                if t % TB == TB - 1:
                    ln_eps(2 * BATCH + t // TB)

            def apply_3(b):
                ln_apply(2 * BATCH + b, b, lambda i: x3(TB * b + i), lambda i: None)

            xT_low("x", 0)
            step("x", 0, first=True)
            ln_stats_x(2)
            step("x", 1)
            ln_apply_x(2)
            step("x", 2)
            ln_stats_x(3)
            step("x", 3)
            ln_apply_x(3)
            with dve.Fori(4, XPART + 3) as g:
                step("x", g)
            for g in range(XPART + 3, XTILES):
                step("x", g, last=g == XTILES - 1)
                k, part = divmod(g - XPART - 3, 3)
                if k < BATCH // PARTS:
                    if part < 2:
                        for t in (TB * k + 2 * part, TB * k + 2 * part + 1):
                            add_x(t)
                            stats_3(t)
                    else:
                        apply_3(k)

            def copy_logits(part):
                n = PT * EXPERTS
                dve.wait_ge(S["logits_ready"], PT * (part + 1))
                nc.vector.tensor_copy(logits[:, n * part:n * part + n], bank[2][:, 0:n]).then_inc(S["logits_read"], 1)

            copy_row(0, 0)
            copy_row(1, 1)
            copy_logits(0)
            xT_low("s", 0)
            step("s", 0, first=True)
            for b in range(BATCH // PARTS, BATCH):
                for t in range(TB * b, TB * b + TB):
                    add_x(t)
                    stats_3(t)
                g = b - BATCH // PARTS + 1
                step("s", g, g % 2)
                apply_3(b)
            for g in range(BATCH // PARTS + 1, LOGITS_STEP):
                step("s", g, g % 2)
            copy_logits(1)

            dve.wait_ge(S["logits_read"], PARTS)
            by_expert = logits[:, :].rearrange("p (t e) -> p t e", e=EXPERTS)
            over = lambda a: a.unsqueeze(2).to_broadcast([P, TILES, EXPERTS])
            link(nc.vector.tensor_reduce(row_max[:, :], by_expert, mybir.AxisListType.X, ALU.max))
            nc.vector.tensor_tensor(by_expert, by_expert, over(row_max[:, :]), ALU.subtract).then_inc(S["minus_max"], 1)
            step("s", LOGITS_STEP, LOGITS_STEP % 2)
            dve.wait_ge(S["exp_router"], 1)
            link(nc.vector.tensor_reduce(row_sum[:, :], by_expert, mybir.AxisListType.X, ALU.add))
            link(nc.vector.reciprocal(row_sum[:, :], row_sum[:, :]))
            link(nc.vector.tensor_tensor(by_expert, by_expert, over(row_sum[:, :]), ALU.mult))
            for t in range(TILES):
                top = nc.vector.max(best[:, t, :], by_expert[:, t, :])
            link(top)
            for t in range(TILES):
                top = nc.vector.max_index(best_at[:, t, :], best[:, t, :], by_expert[:, t, :])
            link(top)
            link(nc.vector.tensor_copy(best_f[:, :, :], best_at[:, :, 0:TOPK]))
            link(nc.vector.tensor_tensor(row_sum[:, :], best[:, :, 0], best[:, :, 1], ALU.add))
            link(nc.vector.tensor_scalar(row_sum[:, :], row_sum[:, :], 1e-20, None, ALU.add))
            link(nc.vector.reciprocal(row_sum[:, :], row_sum[:, :]))
            for c in range(TOPK):
                link(nc.vector.tensor_tensor(share[c][:, :], best[:, :, c], row_sum[:, :], ALU.mult))
            link(nc.vector.tensor_tensor(first_lower[:, :], best_f[:, :, 1], best_f[:, :, 0], ALU.is_gt))
            link(nc.vector.tensor_scalar(second_lower[:, :], first_lower[:, :], -1.0, 1.0, ALU.mult, ALU.add))
            for c, (of, lower) in enumerate(((ALU.min, (first_lower, second_lower)), (ALU.max, (second_lower, first_lower)))):
                for i in range(TOPK):
                    link(nc.vector.tensor_tensor(share_part[i][:, :], share[i][:, :], lower[i][:, :], ALU.mult))
                link(nc.vector.tensor_tensor(weight_e[c][:, :], share_part[0][:, :], share_part[1][:, :], ALU.add))
                link(nc.vector.tensor_tensor(row_max[:, :], best_f[:, :, 0], best_f[:, :, 1], of))
                link(nc.vector.tensor_tensor(choice[c][:, :].rearrange("p (e t) -> p e t", e=EXPERTS),
                                             iota[:, 0:EXPERTS].unsqueeze(2).to_broadcast([P, EXPERTS, TILES]),
                                             row_max[:, :].unsqueeze(1).to_broadcast([P, EXPERTS, TILES]), ALU.is_equal))
            nc.vector.tensor_tensor(by_router.chosen[:, :], choice[0][:, :], choice[1][:, :], ALU.add).then_inc(S["chosen_ready"], 1)
            for g in range(LOGITS_STEP + 1, ROUTE_STEP):
                step("s", g, g % 2)
            dve.wait_ge(S["prefix_ready"], 2)
            dve.wait_ge(S["prefix_read"], 1)
            count(by_router, bank[YB], S["prefix_e_read"])
            link(route(by_router, ETILES, list(zip(choice, slot_e)), S["prefix_e_read"], expert_e))
            link(nc.vector.tensor_copy(expert_end[:, :], by_router.upto[:, :]))
            for j in range(2):
                tiles = len(range(j, ETILES, 2))
                link(nc.vector.tensor_tensor(is_low[:, 0:tiles], by_router.upto[:, EXPERTS - 2:EXPERTS - 1].to_broadcast([P, tiles]), iota[:, j::2], ALU.is_gt))
                link(nc.vector.tensor_reduce(low_f[:, j:j + 1], is_low[:, 0:tiles], mybir.AxisListType.X, ALU.add))
            link(nc.vector.tensor_scalar(low_stored[:, :], low_f[:, :], 16.0, None, ALU.mult))
            owners, tile_f = by_router.tile_of[:, :, :], by_router.tile_f
            link(nc.vector.tensor_reduce(tile_f[:, :], owners[:, :, 0::2], mybir.AxisListType.X, ALU.add))
            link(nc.vector.tensor_reduce(odd_f[:, :], owners[:, :, 1::2], mybir.AxisListType.X, ALU.add))
            nc.vector.tensor_tensor(place_e[:, :], tile_f[:, :], odd_f[:, :], ALU.subtract).then_inc(S["route_e_done"], 1)
            with dve.Fori(ROUTE_STEP // 2, TILES // 2 - 1) as i:
                for j in range(2):
                    step("s", 2 * i + j, j)
            step("s", TILES - 2, rows_left=False)
            step("s", TILES - 1, last=True)
            shared_add(TILES - 1)

            xT_low("e", 0)
            step("e", 0, first=True)
            with dve.Fori(1, ETILES - 1) as g:
                step("e", g)
            step("e", ETILES - 1, last=True)

            def combine(t, c, found):
                row = resid[:, t, :]
                nc.vector.scalar_tensor_tensor(out=row, in0=found, scalar=weight_e[c][:, t:t + 1], in1=row, op0=ALU.mult, op1=ALU.add).then_inc(S["combined"], 1)

            dve.wait_ge(S["low_found"], 16 * TILES)
            for t in range(TILES):
                combine(t, 0, low_rows[:, t, :])
            for t in range(TILES):
                dve.wait_ge(S["combined"], t + 1)
                dve.wait_ge(gath[t % PT], 16 * PARTS + 16 * (t // PT) + 16)
                combine(t, 1, high_rows[:, t % PT, :])

        @block.tensor
        def _(pe):
            pe.wait_ge(S["const_ready"], 6)
            def count_ahead(chosen, to, n):
                pe.wait_ge(S["chosen_ready"], n)
                nc.tensor.matmul(to[:, 0:NE], earlier[:, :], chosen[:, :], start=True, stop=True)
                nc.tensor.matmul(to[:, NE:2 * NE], ones[:, :], chosen[:, :], start=True, stop=True).then_inc(S["prefix_ready"], 1)

            count_ahead(by_id.chosen, bank[7], 1)

            def transpose_xn(t):
                if t % TB == TB - 1:
                    pe.wait_ge(S["xnT_lo_done"], t - TB + 2)
                pe.wait_ge(S["xn_ready"], t + 1)
                for k in range(KC):
                    last = nc.tensor.transpose(bank[XN_BANKS[t % TB]][:, k * P:k * P + P], xn[:, t % TB, k * P:k * P + P], ident[:, :])
                last.then_inc(S["xnT_ready"], 1)

            def gates(b):
                if b >= 2:
                    pe.wait_ge(S["o_lo_done"], b - 1)
                cols = slice(b * SEQ, b * SEQ + SEQ)
                for k in range(KC):
                    last = triple(bank[5][:, :], wg_hi[:, k, :], wg_lo[:, k, :], xnT_hi[:, k, cols], xnT_lo[:, k, cols], k == 0, k == KC - 1)
                last.then_inc(S["gateT_ready"], 1)

            def transpose_gates(b):
                pe.wait_ge(S["gateT_copied"], b + 1)
                if b >= 2:
                    pe.wait_ge(S["sums_T_done"], b - 1)
                for i in range(TB):
                    last = nc.tensor.transpose(bank[6][:, i * P:i * P + P], gateT[:, i * P:i * P + P], ident[:, :])
                last.then_inc(S["gate_ready"], 1)

            for t in range(TB):
                transpose_xn(t)
            pe.wait_ge(S["wg_split"], 1)
            pe.wait_ge(S["ones_r_ready"], 1)

            def project(c, b, to, ready):
                cols = slice(b * SEQ, b * SEQ + SEQ)
                for k in range(KC):
                    last = triple(to[:, :], wqkv_hi[:, c, k, :], wqkv_lo[:, c, k, :], xnT_hi[:, k, cols], xnT_lo[:, k, cols], k == 0, k == KC - 1)
                last.then_inc(S[ready], 1)

            def scores(u, first):
                pe.wait_ge(S["q_lo_done"], u + 1)
                pe.wait_ge(S["k_lo_done"], u + 1)
                if not first:
                    pe.wait_ge(S["exp_done"], u)
                for j in (0, 1, 3, 2):
                    to = bank[2 + POFF[j] // SEQ][:, POFF[j] % SEQ:POFF[j] % SEQ + SEQ - P * j]
                    last = triple(to, k_hi[:, j * P:j * P + P], k_lo[:, j * P:j * P + P], q_hi[:, j * P:], q_lo[:, j * P:], True, True)
                last.then_inc(S["s_ready"], 1)

            def values(u, first, sums=True):
                pe.wait_ge(S["p_lo_done"], u + 1)
                if not first:
                    pe.wait_ge(S["o_lo_done"], u)
                for j in range(TB):
                    n = SEQ - P * j
                    last = triple(bank[5][:, P * j:], v_hi[:, j * P:j * P + P], v_lo[:, j * P:j * P + P],
                                  p_hi[:, POFF[j]:POFF[j] + n], p_lo[:, POFF[j]:POFF[j] + n], j == 0, j == TB - 1)
                last.then_inc(S["pv_ready"], 1)
                if sums:
                    sum_probs(u, first)

            def sum_probs(u, first):
                pe.wait_ge(S["sums_lo_done"], 2 * u + 2)
                if not first:
                    pe.wait_ge(S["sums_T_done"], u)
                nc.tensor.matmul(bank[6][:, :], ones_r[:, :], key_sums_hi[:, :], start=True, stop=False)
                nc.tensor.matmul(bank[6][:, :], ones_r[:, :], key_sums_lo[:, :], start=False, stop=True).then_inc(S["sum_ready"], 1)

            def output(u, b, i, h, empty, to=7):
                pe.wait_ge(S["o_lo_done"], u + 1)
                if i == 0 and b == 0:
                    pe.wait_ge(S["wo_split"], h + 1)
                if not empty:
                    pe.wait_ge(S["y_added"], TB * u + i)
                triple(bank[to][:, :], o_hi[:, b % 2, i * P:i * P + P], o_lo[:, b % 2, i * P:i * P + P], wo_hi[:, :], wo_lo[:, :], True, True).then_inc(S["y_ready"], 1)

            def head(h, first):
                for b in range(BATCH):
                    u = BATCH * h + b
                    start = first and b == 0
                    outputs = not (first and b < 2)
                    b2, h2 = (b + 2) % BATCH, h if b >= 2 else h - 1
                    if b == 0:
                        for n in ("wq_split", "wk_split", "wv_split"):
                            pe.wait_ge(S[n], h + 1)
                    if not start:
                        pe.wait_ge(S["vT_done"], u)
                    ahead = first and b + 1 < BATCH
                    if first:
                        pe.wait_ge(S["xnT_lo_done"], TB * b + TB)
                    project(0, b, bank[0], "q_ready")
                    if first:
                        gates(b)
                    if first and b == 2:
                        pe.wait_ge(S["prefix_read"], 1)
                    if outputs:
                        output(u - 2, b2, 0, h2, first and b == 2)
                    if not start:
                        pe.wait_ge(S["v_lo_done"], u)
                    project(1, b, bank[1], "k_ready")
                    if outputs:
                        output(u - 2, b2, 1, h2, False)
                    if ahead:
                        if not start:
                            pe.wait_ge(S["exp_done"], u)
                        transpose_xn(TB * b + TB)
                        transpose_xn(TB * b + TB + 1)
                    if first:
                        transpose_gates(b)
                    pe.wait_ge(S["q_lo_done"], u + 1)
                    project(2, b, bank[0], "vT_ready")
                    if outputs:
                        output(u - 2, b2, 2, h2, False)
                    if ahead:
                        transpose_xn(TB * b + TB + 2)
                        transpose_xn(TB * b + TB + 3)
                    if first:
                        pe.wait_ge(S["gate_exp"], b + 1)
                    if not start:
                        values(u - 1, first and b == 1)
                    if outputs:
                        output(u - 2, b2, 3, h2, False)
                    if ahead:
                        pe.wait_ge(S["xnT_lo_done"], TB * b + 2 * TB)
                    scores(u, start)
                    pe.wait_ge(S["vT_done"], u + 1)
                    for i in range(TB):
                        last = nc.tensor.transpose(bank[1][:, i * P:i * P + P], vT[:, i * P:i * P + P], ident[:, :])
                    last.then_inc(S["v_ready"], 1)

            head(0, True)
            with pe.Fori(1, HEADS) as h:
                head(h, False)
            def last_outputs(u, tiles):
                for i in tiles:
                    output(u, u % BATCH, i, HEADS - 1, True, TAIL_BANKS[u - (U - 2)][i])

            pe.wait_ge(S["y_added"], TB * (U - 2))
            last_outputs(U - 2, (0, 1))
            pe.wait_ge(S["v_lo_done"], U)
            last_outputs(U - 2, (2,))
            pe.wait_ge(S["exp_done"], U)
            last_outputs(U - 2, (3,))
            values(U - 1, False, False)
            last_outputs(U - 1, (0, 1))
            sum_probs(U - 1, False)
            pe.wait_ge(S["y_added"], TB * (U - 2) + 2)
            last_outputs(U - 1, (2, 3))
            pe.wait_ge(S["y_added"], TB * (U - 1))

            def transpose_rows(ph, i, j):
                if ph == "s":
                    pe.wait_ge(S["s_row"], 2 * i + j + 1)
                else:
                    pe.wait_ge(S[f"{ph}_row{j}"], 16 * i + 16)
                for k in range(KC):
                    last = nc.tensor.transpose(bank[XT][:, k * P:k * P + P], rows[:, j, k * P:k * P + P], ident[:, :])
                last.then_inc(S[f"{ph}_xT_ready"], 1)

            def up(ph, g, products, first):
                pe.wait_ge(S[f"{ph}_xT_lo"], g + 1)
                if not first:
                    pe.wait_ge(S[f"{ph}_act"], HALVES[ph] * g)
                for j, (hi, lo) in enumerate(products):
                    for k in range(KC):
                        last = triple(bank[j][:, 0:WIDTH[ph]], xT_hi[:, k, :], xT_lo[:, k, :], hi(k), lo(k), k == 0, k == KC - 1)
                last.then_inc(S[f"{ph}_up"], 1)

            def down(ph, g, hi, lo, second, between=None):
                pe.wait_ge(S[f"{ph}_aT_lo"], len(aT_parts(ph)) * (g + 1))
                if second:
                    pe.wait_ge(S[f"{ph}_y_out"], g)
                for c in range(NCH[ph]):
                    w = chunk(ph, c)[1]
                    if c == NCH[ph] - 1 and between:
                        between()
                    last = triple(bank[YB][:, :], aT_hi[0:w, c, :], aT_lo[0:w, c, :], hi(c, w), lo(c, w), c == 0, c == NCH[ph] - 1)
                last.then_inc(S[f"{ph}_y"], 1)

            def transpose_act(ph, g):
                pe.wait_ge(S[f"{ph}_act"], HALVES[ph] * (g + 1))
                for c in range(NCH[ph]):
                    c0, w = chunk(ph, c)
                    last = nc.tensor.transpose(bank[AT + c // KC][0:w, c % KC * P:c % KC * P + P], act_sb[:, c0:c0 + w], ident[:, :])
                last.then_inc(S[f"{ph}_aT_ready"], 1)

            def matrix(g):
                e = pe.value_load(expert_x[0:1, bass.ds(g, 1)], min_val=0, max_val=TOKEN_EXPERTS - 1)
                return [lambda k, w=P, m=m: m[0:w, bass.ds(e, 1), k, :].rearrange("p a n -> p (a n)") for m in (ct_hi, ct_lo)]

            def x_step(i, j, first=False, last=False, second=True):
                g = 2 * i + j
                up("x", g, [matrix(g)], first)
                if not last:
                    transpose_rows("x", i + j, 1 - j)
                if not first:
                    down("x", g - 1, *matrix(g - 1), second)
                transpose_act("x", g)

            def feed_forward(step, n):
                step(0, 0, first=True)
                step(0, 1, second=False)
                by_twos(pe, step, 2, n - 1)
                step((n - 1) // 2, (n - 1) % 2, last=True)

            transpose_rows("x", 0, 0)
            pe.wait_ge(S["ct_lo_pool"], 1)
            pe.wait_ge(S["ct_lo_dve"], TOKEN_EXPERTS - 1)
            pe.wait_ge(S["y_added"], U * TB)
            feed_forward(x_step, XTILES)
            down("x", XTILES - 1, *matrix(XTILES - 1), True)

            def transpose_x3(t):
                pe.wait_ge(S["xn_ready"], 2 * TILES + t + 1)
                if t >= 2:
                    pe.wait_ge(S["x3_copied"], t - 1)
                for k in range(KC):
                    last = nc.tensor.transpose(bank[t % 2][:, k * P:k * P + P], x3(t)[:, k * P:k * P + P], ident[:, :])
                last.then_inc(S["x3_T"], 1)

            def route_logits(part):
                start, stop = PT * part, PT * part + PT
                transpose_x3(start)
                for t in range(start, stop):
                    if t + 1 < stop:
                        transpose_x3(t + 1)
                    pe.wait_ge(S["x3_copied"], t + 1)
                    for k in range(KC):
                        last = nc.tensor.matmul(bank[2][:, (t - start) * EXPERTS:(t - start + 1) * EXPERTS], x3T[:, t % 2, k * P:k * P + P], router_w[:, k, :],
                                                start=(k == 0), stop=(k == KC - 1))
                    last.then_inc(S["logits_ready"], 1)

            pe.wait_ge(S["router_loaded"], 16)
            route_logits(0)

            pe.wait_ge(S["sh_split"], 3)
            shared = [[lambda k, m=m, j=j: m[:, k, j * INNER:(j + 1) * INNER] for m in (sh_up_hi, sh_up_lo)] for j in range(4)]
            shared_down = [lambda c, w, m=m: m[0:w, c, :] for m in (sh_down_hi, sh_down_lo)]

            def s_step(i, j, first=False, last=False, second=True):
                g = 2 * i + j
                up("s", g, shared, first)
                if not last:
                    transpose_rows("s", i + j, 1 - j)
                if not first:
                    down("s", g - 1, *shared_down, second)
                transpose_act("s", g)

            transpose_rows("s", 0, 0)
            pe.wait_ge(S["logits_read"], 1)
            s_step(0, 0, first=True)
            for g in range(1, LOGITS_STEP):
                s_step(g // 2, g % 2, second=g > 1)
            route_logits(1)
            pe.wait_ge(S["logits_read"], PARTS)
            for g in range(LOGITS_STEP, ROUTE_STEP):
                s_step(g // 2, g % 2)
            pe.wait_ge(S["s_y_out"], ROUTE_STEP - 1)
            count_ahead(by_router.chosen, bank[YB], 2)
            pe.wait_ge(S["prefix_e_read"], 1)
            by_twos(pe, s_step, ROUTE_STEP, TILES - 1)
            s_step(TILES // 2 - 1, 1, last=True)
            down("s", TILES - 1, *shared_down, True)

            def place(g):
                return pe.value_load(place_e[0:1, bass.ds(g, 1)], min_val=0, max_val=1)

            def e_up(g, p, first=False):
                products = [[lambda k, at=part + c * INNER: expert_w[:, bass.ds(p, 1), at + 2 * INNER * k:at + 2 * INNER * k + INNER].rearrange("p a n -> p (a n)")
                             for part in (0, UP)] for c in range(2)]
                up("e", g, products, first)

            def e_down(g, p, second, between=None):
                down("e", g, *[lambda c, w, at=part: expert_w[0:w, bass.ds(p, 1), at + c * D:at + c * D + D].rearrange("p a n -> p (a n)")
                               for part in (2 * UP, 2 * UP + DOWN)], second, between)

            def e_step(i, j, first=False, last=False, second=True):
                g = 2 * i + j
                following = []
                if not first:
                    p = place(g - 1)
                if not last:
                    transpose_rows("e", i + j, 1 - j)
                if first:
                    following.append(place(g + 1))
                else:
                    e_down(g - 1, p, second, None if last else lambda: following.append(place(g + 1)))
                transpose_act("e", g)
                if not last:
                    e_up(g + 1, following[0])

            pe.wait_ge(S["s_y_out"], TILES)
            pe.wait_ge(S["route_e_done"], 1)
            transpose_rows("e", 0, 0)
            e_up(0, place(0), first=True)
            feed_forward(e_step, ETILES)
            e_down(ETILES - 1, place(ETILES - 1), True)


def kernel(x, itok_BxS_13_99985, ctx_2048, L0_attn_w_qkv, L0_attn_w_gates, L0_attn_w_out, L0_ffn_gate_w, L0_ffn_expert_gate, L0_ffn_expert_up, L0_ffn_expert_down, L0_ffn_shared_gate, L0_ffn_shared_up, L0_ffn_shared_down):
    import numpy as np
    import concourse.bacc as bacc
    from concourse.bass_utils import run_bass_kernel_spmd

    c = np.ascontiguousarray
    f = lambda a: np.asarray(a)
    wg = np.zeros((D, P), np.float32)
    wg[:, :HEADS] = f(L0_attn_w_gates)
    chunks = lambda a: a.reshape(-1, P, a.shape[-1]).transpose(1, 0, 2)
    up = np.concatenate([f(L0_ffn_expert_gate), f(L0_ffn_expert_up)], 1).transpose(0, 2, 1)
    down = np.zeros((EXPERTS, IC * P, D), np.float32)
    down[:, :INNER] = f(L0_ffn_expert_down).transpose(0, 2, 1)
    halves = [m[j * INNER:(j + 1) * INNER] for j in range(2) for m in (f(L0_ffn_shared_gate), f(L0_ffn_shared_up))]
    sh_down = np.zeros((SC * P, D), np.float32)
    sh_down[:SHARED] = f(L0_ffn_shared_down).T
    arrays = {
        "x": c(f(x).reshape(T, D)),
        "token_ids": c(f(itok_BxS_13_99985).reshape(TILES, P).T),
        "wqkv": c(f(L0_attn_w_qkv).reshape(KC, P, 3, HEADS, DH).transpose(3, 1, 2, 0, 4)),
        "wgates": c(wg.reshape(KC, P, P).transpose(1, 0, 2)),
        "wo": c(f(L0_attn_w_out).reshape(HEADS, DH, D)),
        "ctxT": c(np.stack([chunks(m.T) for m in f(ctx_2048)])),
        "router": c(chunks(f(L0_ffn_gate_w).T)),
        "exp_up": c(np.stack([chunks(m) for m in up])),
        "exp_down": c(np.stack([chunks(m) for m in down])),
        "sh_up": c(chunks(np.concatenate(halves, 0).T)),
        "sh_down": c(chunks(sh_down)),
    }
    nc = bacc.Bacc("TRN2", target_bir_lowering=False, num_devices=1)
    args = [nc.dram_tensor(n, a.shape, mybir.dt.from_np(a.dtype), kind="ExternalInput").ap() for n, a in arrays.items()]
    args.append(nc.dram_tensor("out", (T, D), F32, kind="ExternalOutput").ap())
    build(nc, *args)
    r = run_bass_kernel_spmd(nc, [arrays], core_ids=[0])
    return r.results[0]["out"].reshape(BATCH, SEQ, D)
```
